# Optimizing a Trainium2 kernel written in Bass

```python
import numpy as np
import jax
import jax.numpy as jnp

def _softmax(x, axis=-1):
    return jax.nn.softmax(x, axis=axis)

def _gelu(x):
    return jax.nn.gelu(x, approximate=True)

def _silu(x):
    return jax.nn.silu(x)

def _sigmoid(x):
    return jax.nn.sigmoid(x)

def _layernorm(x, axis=-1, eps=1e-05):
    m = jnp.mean(x, axis=axis, keepdims=True)
    v = jnp.var(x, axis=axis, keepdims=True)
    return (x - m) / jnp.sqrt(v + eps)

def _scatter_add(tgt, idx, src, axis=0):
    return tgt.at[idx].add(src)

def _segment_sum(src, seg, n):
    return jax.ops.segment_sum(src, seg, n)
kernel_name = 'mk_decoder_preln_d1_seqx_r8_6e1b73'

def setup_inputs(seed: int=0):
    np.random.seed(seed)
    _w = jnp.asarray

    def _rec_inputs():
        import jax
        import jax.numpy as jnp
        _rk = jax.random.key(seed)
        x = -0.0003929 + 0.9999 * jax.random.normal(jax.random.fold_in(_rk, 1), (8, 128, 512), jnp.float32)
        _lenS = 128 - jax.random.randint(jax.random.fold_in(_rk, 7), (8,), 0, max(1, 128 // 4) + 1, jnp.int32)
        _lenS2 = 128 - jax.random.randint(jax.random.fold_in(_rk, 8), (8,), 0, max(1, 128 // 4) + 1, jnp.int32)
        _ctx_4096P = jax.random.normal(jax.random.fold_in(_rk, 11), (8, 16, 512), jnp.float32)
        _ctx_4096c = jax.random.dirichlet(jax.random.fold_in(_rk, 511), 0.3 * jnp.ones((16,), jnp.float32), (8, 128))
        _ctx_4096t = jnp.einsum('bsk,bkd->bsd', _ctx_4096c, _ctx_4096P)
        _ctx_4096t = _ctx_4096t * jax.lax.rsqrt(jnp.mean(jnp.square(_ctx_4096t)) + 1e-12) * 0.953939
        ctx_4096 = 2.81802e-05 + 1.00001 * (_ctx_4096t + 0.3 * jax.random.normal(jax.random.fold_in(_rk, 611), (8, 128, 512), jnp.float32))
        itok_BxS2_0_2047 = jax.random.randint(jax.random.fold_in(_rk, 12), (8, 128), 0, 256, jnp.int32)
        return (x, ctx_4096, itok_BxS2_0_2047)
    x, ctx_4096, itok_BxS2_0_2047 = _rec_inputs()

    def _L0_attn_setup():
        import jax, jax.numpy as jnp
        import numpy as np
        D_MODEL, N_HEADS, LATENT, ROPE = (512, 128, 64, 64)
        HEAD_DIM = D_MODEL // N_HEADS
        B, S = (2, 128)
        key = jax.random.key(seed)
        ks = jax.random.split(key, 9)

        def w(k, i, o):
            return jax.random.normal(k, (i, o), dtype=jnp.float32) * (1.0 / np.sqrt(i))
        return {'x': jax.random.normal(ks[0], (B, S, D_MODEL), dtype=jnp.float32), 'Wq_down': w(ks[1], D_MODEL, LATENT), 'Wq_up': w(ks[2], LATENT, N_HEADS * HEAD_DIM), 'Wq_rope': w(ks[3], D_MODEL, N_HEADS * ROPE), 'Wkv_down': w(ks[4], D_MODEL, LATENT), 'Wk_up': w(ks[5], LATENT, N_HEADS * HEAD_DIM), 'Wv_up': w(ks[6], LATENT, N_HEADS * HEAD_DIM), 'Wk_rope': w(ks[7], D_MODEL, ROPE), 'Wo': w(ks[8], N_HEADS * HEAD_DIM, D_MODEL)}
    _L0_attn_all = _L0_attn_setup()
    _L0_attn_in = {k: v for k, v in _L0_attn_all.items() if k in ('Wq_down', 'Wq_up', 'Wq_rope', 'Wkv_down', 'Wk_up', 'Wv_up', 'Wk_rope', 'Wo')}
    del _L0_attn_all

    def _L0_xattn_setup():
        import jax, jax.numpy as jnp
        import numpy as np
        HIDDEN = 512
        N_HEADS = 32
        N_KV_HEADS = 8
        HEAD_DIM = HIDDEN // N_HEADS
        N_REP = N_HEADS // N_KV_HEADS
        ROPE_THETA = 10000.0
        B, S = (2, 256)

        def _rotate_half(x):
            x1, x2 = jnp.split(x, 2, axis=-1)
            return jnp.concatenate((-x2, x1), axis=-1)

        def _rope_cos_sin(position_ids):
            inv_freq = 1.0 / ROPE_THETA ** (jnp.arange(0, HEAD_DIM, 2, dtype=jnp.float32) / HEAD_DIM)
            freqs = position_ids[..., None].astype(jnp.float32) * inv_freq
            emb = jnp.concatenate((freqs, freqs), axis=-1)
            return (jnp.cos(emb)[:, None, :, :], jnp.sin(emb)[:, None, :, :])
        key = jax.random.key(seed)
        ks = jax.random.split(key, 9)
        sc = 1.0 / np.sqrt(HIDDEN)
        query = jax.random.normal(ks[0], (B, S, HIDDEN), jnp.float32)
        key_t = jax.random.normal(ks[1], (B, S, HIDDEN), jnp.float32)
        value = jax.random.normal(ks[2], (B, S, HIDDEN), jnp.float32)
        position_ids = jnp.sort(jax.random.randint(ks[3], (B, S), 0, S), axis=-1)
        Wq = jax.random.normal(ks[4], (HIDDEN, N_HEADS * HEAD_DIM), jnp.float32) * sc
        Wk = jax.random.normal(ks[5], (HIDDEN, N_KV_HEADS * HEAD_DIM), jnp.float32) * sc
        Wv = jax.random.normal(ks[6], (HIDDEN, N_KV_HEADS * HEAD_DIM), jnp.float32) * sc
        Wo = jax.random.normal(ks[7], (N_HEADS * HEAD_DIM, HIDDEN), jnp.float32) * sc
        return {'query': query, 'key': key_t, 'value': value, 'position_ids': position_ids, 'Wq': Wq, 'Wk': Wk, 'Wv': Wv, 'Wo': Wo}
    _L0_xattn_all = _L0_xattn_setup()
    _L0_xattn_in = {k: v for k, v in _L0_xattn_all.items() if k in ('Wq', 'Wk', 'Wv', 'Wo')}
    del _L0_xattn_all

    def _L0_ffn_setup():
        import jax, jax.numpy as jnp
        import numpy as np
        B, S, D_IN, D_OUT = (2, 256, 512, 512)
        E, K, R = (8, 2, 16)
        SCALING = 32.0 / 16.0
        key = jax.random.key(seed)
        ks = jax.random.split(key, 6)
        x = jax.random.normal(ks[0], (B, S, D_IN), dtype=jnp.float32)
        gate_w = jax.random.normal(ks[1], (E, D_IN), dtype=jnp.float32) * 0.02
        base_w = jax.random.normal(ks[2], (D_OUT, D_IN), dtype=jnp.float32) * 0.02
        base_b = jax.random.normal(ks[3], (D_OUT,), dtype=jnp.float32) * 0.02
        lora_A = jax.random.normal(ks[4], (E, R, D_IN), dtype=jnp.float32) * 0.02
        lora_B = jax.random.normal(ks[5], (E, D_OUT, R), dtype=jnp.float32) * 0.02
        return {'x': x, 'gate_w': gate_w, 'base_w': base_w, 'base_b': base_b, 'lora_A': lora_A, 'lora_B': lora_B}
    _L0_ffn_all = _L0_ffn_setup()
    _L0_ffn_in = {k: v for k, v in _L0_ffn_all.items() if k in ('gate_w', 'base_w', 'base_b', 'lora_A', 'lora_B')}
    del _L0_ffn_all
    return {'x': x, 'ctx_4096': ctx_4096, 'itok_BxS2_0_2047': itok_BxS2_0_2047, 'L0_attn_Wq_down': _L0_attn_in['Wq_down'], 'L0_attn_Wq_up': _L0_attn_in['Wq_up'], 'L0_attn_Wq_rope': _L0_attn_in['Wq_rope'], 'L0_attn_Wkv_down': _L0_attn_in['Wkv_down'], 'L0_attn_Wk_up': _L0_attn_in['Wk_up'], 'L0_attn_Wv_up': _L0_attn_in['Wv_up'], 'L0_attn_Wk_rope': _L0_attn_in['Wk_rope'], 'L0_attn_Wo': _L0_attn_in['Wo'], 'L0_xattn_Wq': _L0_xattn_in['Wq'], 'L0_xattn_Wk': _L0_xattn_in['Wk'], 'L0_xattn_Wv': _L0_xattn_in['Wv'], 'L0_xattn_Wo': _L0_xattn_in['Wo'], 'L0_ffn_gate_w': _L0_ffn_in['gate_w'], 'L0_ffn_base_w': _L0_ffn_in['base_w'], 'L0_ffn_base_b': _L0_ffn_in['base_b'], 'L0_ffn_lora_A': _L0_ffn_in['lora_A'], 'L0_ffn_lora_B': _L0_ffn_in['lora_B']}

def reference(x, ctx_4096, itok_BxS2_0_2047, L0_attn_Wq_down, L0_attn_Wq_up, L0_attn_Wq_rope, L0_attn_Wkv_down, L0_attn_Wk_up, L0_attn_Wv_up, L0_attn_Wk_rope, L0_attn_Wo, L0_xattn_Wq, L0_xattn_Wk, L0_xattn_Wv, L0_xattn_Wo, L0_ffn_gate_w, L0_ffn_base_w, L0_ffn_base_b, L0_ffn_lora_A, L0_ffn_lora_B):
    import jax
    import jax.numpy as jnp

    def _L0_attn_ref(x, Wq_down, Wq_up, Wq_rope, Wkv_down, Wk_up, Wv_up, Wk_rope, Wo):
        import jax, jax.numpy as jnp
        import numpy as np
        D_MODEL, N_HEADS, LATENT, ROPE = (512, 128, 64, 64)
        HEAD_DIM = D_MODEL // N_HEADS
        B, S = (2, 128)
        b, s, _ = x.shape
        c_q = x @ Wq_down
        c_kv = x @ Wkv_down
        q_c = (c_q @ Wq_up).reshape(b, s, N_HEADS, HEAD_DIM)
        q_r = (x @ Wq_rope).reshape(b, s, N_HEADS, ROPE)
        k_c = (c_kv @ Wk_up).reshape(b, s, N_HEADS, HEAD_DIM)
        v_c = (c_kv @ Wv_up).reshape(b, s, N_HEADS, HEAD_DIM)
        k_r = x @ Wk_rope
        scale = jnp.asarray((HEAD_DIM + ROPE) ** 0.5, x.dtype)
        scores = (jnp.einsum('bqhd,bkhd->bhqk', q_c, k_c) + jnp.einsum('bqhd,bkd->bhqk', q_r, k_r)) / scale
        attn = jax.nn.softmax(scores, axis=-1)
        out = jnp.einsum('bhqk,bkhd->bqhd', attn, v_c)
        out = out.reshape(b, s, N_HEADS * HEAD_DIM)
        return out @ Wo

    def _L0_xattn_ref(query, key, value, position_ids, Wq, Wk, Wv, Wo):
        import jax, jax.numpy as jnp
        import numpy as np
        HIDDEN = 512
        N_HEADS = 32
        N_KV_HEADS = 8
        HEAD_DIM = HIDDEN // N_HEADS
        N_REP = N_HEADS // N_KV_HEADS
        ROPE_THETA = 10000.0
        B, S = (2, 256)

        def _rotate_half(x):
            x1, x2 = jnp.split(x, 2, axis=-1)
            return jnp.concatenate((-x2, x1), axis=-1)

        def _rope_cos_sin(position_ids):
            inv_freq = 1.0 / ROPE_THETA ** (jnp.arange(0, HEAD_DIM, 2, dtype=jnp.float32) / HEAD_DIM)
            freqs = position_ids[..., None].astype(jnp.float32) * inv_freq
            emb = jnp.concatenate((freqs, freqs), axis=-1)
            return (jnp.cos(emb)[:, None, :, :], jnp.sin(emb)[:, None, :, :])
        nb, q_len, _ = query.shape
        q = jnp.einsum('bse,ef->bsf', query, Wq).reshape(nb, q_len, N_HEADS, HEAD_DIM).transpose(0, 2, 1, 3)
        k = jnp.einsum('bse,ef->bsf', key, Wk).reshape(nb, q_len, N_KV_HEADS, HEAD_DIM).transpose(0, 2, 1, 3)
        v = jnp.einsum('bse,ef->bsf', value, Wv).reshape(nb, q_len, N_KV_HEADS, HEAD_DIM).transpose(0, 2, 1, 3)
        cos, sin = _rope_cos_sin(position_ids)
        q = q * cos + _rotate_half(q) * sin
        k = k * cos + _rotate_half(k) * sin
        k = jnp.repeat(k, N_REP, axis=1)
        v = jnp.repeat(v, N_REP, axis=1)
        scale = 1.0 / jnp.sqrt(jnp.asarray(HEAD_DIM, q.dtype))
        scores = jnp.einsum('bhqd,bhkd->bhqk', q, k) * scale
        probs = jax.nn.softmax(scores, axis=-1)
        ctx = jnp.einsum('bhqk,bhkd->bhqd', probs, v)
        ctx = ctx.transpose(0, 2, 1, 3).reshape(nb, q_len, N_HEADS * HEAD_DIM)
        return jnp.einsum('bsf,fe->bse', ctx, Wo)

    def _L0_ffn_ref(x, gate_w, base_w, base_b, lora_A, lora_B):
        import jax, jax.numpy as jnp
        import numpy as np
        B, S, D_IN, D_OUT = (2, 256, 512, 512)
        E, K, R = (8, 2, 16)
        SCALING = 32.0 / 16.0
        gate_logits = jnp.einsum('bsd,ed->bse', x, gate_w)
        weights, selected = jax.lax.top_k(gate_logits, K)
        weights = jax.nn.softmax(weights.astype(jnp.float32), axis=2).astype(x.dtype)
        result = jnp.einsum('bsd,od->bso', x, base_w) + base_b
        w_full = jnp.sum(jax.nn.one_hot(selected, E, dtype=x.dtype) * weights[..., None], axis=2)
        low = jnp.einsum('bsd,erd->ebsr', x, lora_A)
        lora_out = jnp.einsum('ebsr,eor,bse->bso', low, lora_B, w_full)
        result = result + SCALING * lora_out
        return result
    x = x + _L0_attn_ref(_layernorm(x, axis=-1), L0_attn_Wq_down, L0_attn_Wq_up, L0_attn_Wq_rope, L0_attn_Wkv_down, L0_attn_Wk_up, L0_attn_Wv_up, L0_attn_Wk_rope, L0_attn_Wo)
    x = x + _L0_xattn_ref(_layernorm(x, axis=-1), ctx_4096, ctx_4096, itok_BxS2_0_2047, L0_xattn_Wq, L0_xattn_Wk, L0_xattn_Wv, L0_xattn_Wo)
    x = x + _L0_ffn_ref(_layernorm(x, axis=-1), L0_ffn_gate_w, L0_ffn_base_w, L0_ffn_base_b, L0_ffn_lora_A, L0_ffn_lora_B)
    return x

_drawn_inputs = setup_inputs


def setup_inputs(seed=0):
    import zlib

    import numpy as np

    out = dict(_drawn_inputs(seed))
    spreads = {}
    factors = {'L0_ffn_base_b': 3.738}
    for name, (base, spread) in spreads.items():
        noise = np.random.default_rng([zlib.crc32(name.encode()), seed]).standard_normal(out[name].shape)
        drawn = base * np.exp(spread * noise) if base else spread * noise
        out[name] = jnp.asarray(drawn.astype(out[name].dtype))
    for name, factor in factors.items():
        out[name] = (out[name] * factor).astype(out[name].dtype)
    return out
```

```python
import math
from contextlib import ExitStack

import concourse.bass as bass
from concourse import mybir

F32 = mybir.dt.float32
F16 = mybir.dt.float16
I32 = mybir.dt.int32
ALU = mybir.AluOpType
ACT = mybir.ActivationFunctionType
AX = mybir.AxisListType

P = 128
B, S, DM = 8, 128, 512
TOK = B * S
KT = DM // P
HALF = TOK // 2
EPS = 1e-5
WS = 256.0

H, HD, RD, LAT = 128, 4, 64, 64
GH = 4
NG = H // GH
HT = H // KT
GW = GH * RD
CR = 3 * HD
CROW = RD
MROW = RD + GH * CR
MS = 16.0
ATT_SCALE = float(HD + RD) ** -0.5
VC = HD + 1

XH, NKV, XD_, THETA = 32, 8, 16, 10000.0
REP = XH // NKV
HF = XD_ // 2
XT_H = P // XD_
XS = float(XD_) ** -0.5
XVC = XD_ + 1
XW = DM + 2 * NKV * XD_
NU = B * KT
TWO_PI = (6.28125, 0.0019340515136718750, 1.2556659146e-06)
MAGIC = 1.5 * 2 ** 23

E, R, SCALING = 8, 16, 2.0
AG = E * R + E


def build(nc, x, ctxT, pos, wdkr, wup, wvup, wqr, wo, xwqkv, xwo, bw, ag, lb, bb, out):
    es = ExitStack()
    with es:
        def sem(name):
            return es.enter_context(nc.semaphore(name))

        top = [(nc.sbuf_base + 63) // 64 * 64]
        size = {F32: 4, F16: 2, I32: 4}

        def sb(name, shape, dt=F32):
            n = size[dt]
            for s in shape[1:]:
                n *= s
            at = top[0]
            top[0] = at + (n + 63) // 64 * 64
            return nc.alloc_sbuf_tensor_at(name, shape, dt, offset=at)

        xs = sb("xs", [P, B, DM])
        ident = sb("ident", [P, P])
        stats = sb("stats", [P, B, 6])
        mv = sb("mv", [P, B, 2])
        rstd = sb("rstd", [P, B])
        wscale = sb("wscale", [P, 1, 1])
        wo_sb = sb("wo_sb", [P, KT, DM])
        wx_raw = sb("wx_raw", [P, KT, XW])
        xwo_sb = sb("xwo_sb", [P, KT, DM])
        bw_raw = sb("bw_raw", [P, KT, DM])
        ag_raw = sb("ag_raw", [P, KT, AG])
        lb_sb = sb("lb_sb", [P, DM])
        bias = sb("bias", [P, DM])
        posi = sb("posi", [P, B], I32)
        posf = sb("posf", [P, B])
        invf = sb("invf", [P, HF])
        ang = sb("ang", [P, B, HF])
        turns = sb("turns", [P, B, HF])
        red = sb("red", [P, 2, B, HF])
        sincos = sb("sincos", [P, 2, B, HF])
        cosq = sb("cosq", [P, B, HF])
        sinq = sb("sinq", [P, B, 2, HF])
        cosk = sb("cosk", [P, B, HF])
        sink = sb("sink", [P, B, 2, HF])
        mask = sb("mask", [P, XT_H])
        before = sb("before", [P, E, E])
        phase = top[0]

        XTh = sb("XTh", [P, KT, TOK], F16)
        XTl = sb("XTl", [P, KT, TOK], F16)
        Wraw = sb("Wraw", [P, 2, KT, GW])
        Wh = sb("Wh", [P, 2, KT, GW], F16)
        Wl = sb("Wl", [P, 2, KT, GW], F16)
        QC = sb("QC", [P, 2, 2, GH, HALF], F16)
        t2_at = top[0]
        QS = sb("QS", [P, 2, 2, GH, HALF], F16)
        KC = sb("KC", [P, 2, TOK], F16)
        KS = sb("KS", [P, TOK], F16)
        pr_at = top[0]
        PR = sb("PR", [P, B, GH * S])
        V = sb("V", [P, B, H, VC])
        Vg = sb("Vg", [P, 2, B, 32])
        os_at = top[0]
        OS = sb("OS", [P, 2, GH * S])
        mneg = sb("mneg", [P, 2, 2, GH, B // 2])
        mT = sb("mT", [16, 2, S], F16)
        stg = sb("stg", [P, 4, KT, TOK], F16)
        end1 = top[0]
        top[0] = pr_at
        xn = sb("xn", [P, B, DM])
        top[0] = t2_at
        wd_raw = sb("wd_raw", [P, KT, 3 * LAT])
        wd_h = sb("wd_h", [P, KT, 3 * LAT], F16)
        wd_l = sb("wd_l", [P, KT, 3 * LAT], F16)
        up = sb("up", [P, DM])
        vup = sb("vup", [P, DM])
        top[0] = os_at
        cT = sb("cT", [P, TOK])
        assert top[0] <= os_at + 2 * GH * S * 4
        top[0] = end1 - 4 * KT * TOK * 2
        U = sb("U", [P, KT, TOK])
        SU = sb("SU", [P, KT, TOK])
        assert end1 <= nc.sbuf_usable_end
        top[0] = phase
        ctx_raw = sb("ctx_raw", [P, KT, TOK])
        cth_at = top[0]
        CTh = sb("CTh", [P, KT, TOK], F16)
        CTl = sb("CTl", [P, KT, TOK], F16)
        Wxh = sb("Wxh", [P, KT, XW], F16)
        Wxl = sb("Wxl", [P, KT, XW], F16)
        X2h = sb("X2h", [P, KT, TOK], F16)
        X2l = sb("X2l", [P, KT, TOK], F16)
        qr_at = top[0]
        qr = sb("qr", [P, B, DM])
        kr = sb("kr", [P, B, NKV, REP, XD_])
        xv = sb("xv", [P, B, NKV, XVC])
        rt = sb("rt", [P, 2, DM])
        kTs = sb("kTs", [P, 2, P])
        qTs = sb("qTs", [P, 2, P])
        xm = sb("xm", [P, 4, REP])
        XPT = sb("XPT", [P, 2, REP, S])
        rz = sb("rz", [P, XT_H])
        assert top[0] <= end1 - 4 * KT * TOK * 2
        top[0] = phase
        O2 = sb("O2", [P, B, DM])
        top[0] = cth_at
        KD = sb("KD", [P, 2, XT_H, S])
        XP = sb("XP", [P, 4, REP, S])
        assert top[0] <= cth_at + KT * TOK * 4
        top[0] = cth_at
        O2T = sb("O2T", [P, 2, KT, S])
        bwh = sb("bwh", [P, KT, DM], F16)
        bwl = sb("bwl", [P, KT, DM], F16)
        top[0] = qr_at
        agh = sb("agh", [P, KT, AG], F16)
        agl = sb("agl", [P, KT, AG], F16)
        lg = sb("lg", [P, B, E])
        ex = sb("ex", [P, B, E])
        mx = sb("mx", [P, B])
        gt = sb("gt", [P, B, E, E])
        eq = sb("eq", [P, B, E, E])
        rank = sb("rank", [P, B, E])
        low = sb("low", [P, B, E * R])
        lowT = sb("lowT", [P, 2, S])
        assert top[0] <= qr_at + B * DM * 4

        PS = es.enter_context(nc.psum_tensor("PS", [P, 8, 512], F32))

        YD = nc.dram_tensor("q_content_parts", [H, CR, TOK], F16, kind="Internal").ap()
        XD = nc.dram_tensor("k_content_parts", [H, CR, TOK], F16, kind="Internal").ap()
        OD = nc.dram_tensor("head_outputs", [NG, GH * VC, GH, B, S], F32, kind="Internal").ap()

        s_x, s_wd, s_up, s_wo = sem("x_in"), sem("wd_in"), sem("up_in"), sem("wo_in")
        s_zero, s_fill, s_id = sem("zeroed"), sem("filled"), sem("ident_ready")
        s_con = sem("constants")
        s_dch, s_pch = sem("dve_chain"), sem("pool_chain")
        s_var, s_sd, s_xn = sem("var_ready"), sem("sd_ready"), sem("xn_ready")
        s_tp, s_th, s_tl = sem("xT_ready"), sem("xT_high"), sem("xT_low")
        s_wds = sem("wd_split")
        s_c, s_ce, s_kl, s_kc = sem("c_ready"), sem("c_out"), sem("k_low"), sem("k_copied")
        s_u, s_uh, s_ul, s_uv = sem("up_ready"), sem("up_high"), sem("up_low"), sem("v_out")
        s_yx = sem("content_stored")
        s_w = [sem("w_in0"), sem("w_in1")]
        s_ws = sem("w_split")
        s_vg = sem("vg_ready")
        s_q, s_qh, s_ql = sem("q_ready"), sem("q_high"), sem("q_low")
        s_y = [sem("y_in0"), sem("y_in1")]
        s_a, s_m, s_mt, s_me = sem("a_ready"), sem("max_ready"), sem("mT_ready"), sem("mT_out")
        s_md = [sem("m_in0"), sem("m_in1")]
        s_qd = [sem("qs_in0"), sem("qs_in1")]
        s_b, s_e, s_pv, s_oe = sem("b_ready"), sem("exp_ready"), sem("pv_ready"), sem("o_out")
        s_od = [sem("o_stored0"), sem("o_stored1")]
        s_ud, s_un, s_o1, s_x1 = sem("u_in"), sem("u_norm"), sem("o1_ready"), sem("x1_ready")
        s_out = sem("stored")
        s_wx, s_ctx, s_pos, s_ffn = sem("xw_in"), sem("ctx_in"), sem("pos_in"), sem("ffn_in")
        s_red, s_sc, s_tab = sem("angles_ready"), sem("sincos_ready"), sem("rope_tables")
        s_xh, s_xl = sem("x_parts_high"), sem("x_parts_low")
        s_kv, s_kvr, s_kvv = sem("kv_ready"), sem("k_roped"), sem("xv_out")
        s_xq, s_xqr = sem("xq_ready"), sem("xq_roped")
        s_xt, s_kT, s_qT, s_kd = sem("turned"), sem("kT_out"), sem("qT_out"), sem("kd_ready")
        s_s, s_xm, s_ex, s_pt, s_pe = sem("xs_ready"), sem("xmax_ready"), sem("xexp_ready"), sem("pT_ready"), sem("pT_out")
        s_xo, s_xon = sem("xo_ready"), sem("xo_out")
        s_ot, s_oT, s_o2, s_x2 = sem("oT_ready"), sem("oT_out"), sem("o2_ready"), sem("x2_ready")
        s_bh, s_bl, s_xb = sem("ffn_high"), sem("ffn_low"), sem("bias_added")
        s_lg, s_lge, s_ge, s_gx = sem("low_ready"), sem("low_out"), sem("gate_in"), sem("gate_exp")
        s_lw, s_lt, s_lT, s_f, s_x3 = sem("low_weighted"), sem("lowT_ready"), sem("lowT_out"), sem("ffn_ready"), sem("x3_ready")

        bQ, bA, bB, bM, bO = (0, 1), (2, 3), (4, 5), 6, 7
        block = es.enter_context(nc.Block())

        def steps(eng, step, first, last, before, after):
            for g in before:
                step(g, g % 2)
            with eng.Fori(0, (last - first + 1) // 2) as i:
                step(2 * i + first, 1)
                step(2 * i + first + 1, 0)
            for g in after:
                step(g, g % 2)

        @block.sync
        def _(sp):
            for b in range(B):
                sp.dma_start(xs[:, b, :], x[b]).then_inc(s_x, 16)
                if b == 0:
                    sp.wait_ge(s_x, 16)
            sp.dma_start(wd_raw[:], wdkr).then_inc(s_wd, 16)
            sp.dma_start(up[:], wup).then_inc(s_up, 16)
            sp.dma_start(vup[P - LAT:P, :], wvup).then_inc(s_up, 16)
            for g in range(2):
                sp.dma_start(Wraw[:, g], wqr[g]).then_inc(s_w[g], 16)
            sp.dma_start(wo_sb[:], wo).then_inc(s_wo, 16)
            sp.dma_start(posi[:], pos).then_inc(s_pos, 16)
            sp.dma_start(wx_raw[:], xwqkv).then_inc(s_wx, 16)
            for t, d in ((xwo_sb, xwo), (bw_raw, bw), (ag_raw, ag), (lb_sb, lb), (bias, bb.to_broadcast([P, DM]))):
                sp.dma_start(t[:], d).then_inc(s_ffn, 16)
            sp.wait_ge(s_uh, 16)
            sp.wait_ge(s_ul, 16)
            for p, (q, k) in enumerate([(0, 2), (0, 3), (1, 2)]):
                for D, w in ((YD, q), (XD, k)):
                    for T in range(KT):
                        sp.dma_start(D[HT * T:HT * (T + 1), HD * p:HD * (p + 1), :],
                                     stg[:, w, T, :]).then_inc(s_yx, 16)
            sp.wait_ge(s_yx, 16 * 6 * KT)
            sp.wait_ge(s_zero, 4)
            sp.wait_ge(s_kc, 2)

            def contents(g, par):
                for j in range(GH):
                    r = CROW + CR * j
                    sp.dma_start(QC[r:r + CR, par, :, j, :], YD[bass.ds(g * GH + j, 1)].rearrange("h r k -> (h r) k")
                                 ).then_inc(s_y[par], 16)
                sp.dma_start(KC[CROW:MROW, par, :], XD[bass.ds(g * GH, GH)].rearrange("h r k -> (h r) k")
                             ).then_inc(s_y[par], 16)

            def q_again(g, par, t):
                sp.wait_ge(s_qh, 8 * g + 4 * (t + 1))
                sp.dma_start(QS[RD:P, par, t], QC[0:RD, par, t]).then_inc(s_qd[t], 16)

            def maxima(g, par, t):
                sp.wait_ge(s_me, 2 * g + t + 1)
                sp.dma_start(QC[MROW:MROW + 1, par, t], mT[:, t, :]).then_inc(s_md[t], 16)

            def outputs(g, t):
                sp.wait_ge(s_oe, 2 * g + t + 1)
                for b in range(4):
                    sp.dma_start(OD[bass.ds(g, 1), :, :, 4 * t + b, :].rearrange("a r j q -> (a r) j q"),
                                 OS[32 * b:32 * b + GH * VC, t, :]).then_inc(s_od[t], 16)

            def step(g, par):
                cur, nxt = not isinstance(g, int) or g >= 0, not isinstance(g, int) or g + 1 < NG
                if cur:
                    q_again(g, par, 1)
                if nxt:
                    if not isinstance(g, int) or g >= 1:
                        sp.wait_ge(s_b, 8 * g)
                    contents(g + 1, 1 - par)
                if not isinstance(g, int) or g >= 1:
                    outputs(g - 1, 1)
                if not isinstance(g, int) or g + 3 < NG:
                    sp.wait_ge(s_ws, g + 2)
                    sp.dma_start(Wraw[:, 1 - par], wqr[bass.ds(g + 3, 1)].rearrange("a p k n -> (a p) k n")
                                 ).then_inc(s_w[1 - par], 16)
                if cur:
                    maxima(g, par, 1)
                if nxt:
                    q_again(g + 1, 1 - par, 0)
                if cur:
                    outputs(g, 0)
                if nxt:
                    maxima(g + 1, 1 - par, 0)

            steps(sp, step, 1, 28, [-1, 0], [29, 30, 31])
            outputs(NG - 1, 1)
            sp.wait_ge(s_od[0], 64 * NG)
            sp.wait_ge(s_od[1], 64 * NG)
            sp.wait_ge(s_b, 8 * NG)
            for T in range(KT):
                src = OD[T * NG // KT:(T + 1) * NG // KT].rearrange("g r j b q -> g r j (b q)")
                for j in range(GH):
                    rows = slice(j * P // GH, (j + 1) * P // GH)
                    sums = src[:, VC * j + HD:VC * (j + 1), j, :].to_broadcast([NG // KT, HD, TOK])
                    sp.dma_start(U[rows, T, :], src[:, VC * j:VC * j + HD, j, :]).then_inc(s_ud, 16)
                    sp.dma_start(SU[rows, T, :], sums).then_inc(s_ud, 16)
            sp.wait_ge(s_oe, 2 * NG)
            sp.dma_start(ctx_raw[:], ctxT).then_inc(s_ctx, 16)
            for b in range(B):
                sp.wait_ge(s_x3, b + 1)
                sp.dma_start(out[b], xs[:, b, :]).then_inc(s_out, 16)
            sp.wait_ge(s_out, 16 * B)

        @block.gpsimd
        def _(pool):
            nc.gpsimd.memset(ident[:], 0.0).then_inc(s_pch, 1)
            pool.wait_ge(s_pch, 1)
            nc.gpsimd.affine_select(out=ident[:], in_=ident[:], compare_op=ALU.not_equal, fill=1.0,
                                    base=0, pattern=[[-1, P]], channel_multiplier=1).then_inc(s_id, 1)
            pool.wait_ge(s_id, 1)
            nc.gpsimd.memset(QC[RD:P], 0.0).then_inc(s_zero, 1)
            pool.wait_ge(s_zero, 1)
            nc.gpsimd.memset(KC[96:P], MS).then_inc(s_zero, 1)
            pool.wait_ge(s_zero, 2)
            nc.gpsimd.memset(Vg[:], 0.0).then_inc(s_zero, 1)
            nc.gpsimd.memset(V[:, :, :, HD], 1.0).then_inc(s_zero, 1)
            nc.gpsimd.memset(wscale[:], WS).then_inc(s_zero, 1)

            def split(g, par):
                if not isinstance(g, int) or g >= 2:
                    pool.wait_ge(s_q, 4 * (g - 1))
                pool.wait_ge(s_w[par], 8 * (g - par) + 16)
                scale = wscale[:].to_broadcast([P, KT, GW])
                nc.gpsimd.tensor_tensor(Wh[:, par], Wraw[:, par], scale, ALU.mult).then_inc(s_pch, 1)
                pool.wait_ge(s_pch, 2 * g + 2)
                nc.gpsimd.tensor_tensor(Wraw[:, par], Wraw[:, par], scale, ALU.mult).then_inc(s_pch, 1)
                pool.wait_ge(s_pch, 2 * g + 3)
                nc.gpsimd.tensor_tensor(Wl[:, par], Wraw[:, par], Wh[:, par], ALU.subtract).then_inc(s_ws, 1)

            def values(g, par):
                if not isinstance(g, int) or g >= 2:
                    pool.wait_ge(s_pv, 2 * (g - 1))
                nc.gpsimd.tensor_copy(
                    Vg[:, par, :, 0:GH * VC],
                    V[:].rearrange("p b h c -> p b (h c)")[:, :, bass.ds(g * (GH * VC), GH * VC)]).then_inc(s_vg, 1)

            pool.wait_ge(s_zero, 5)
            split(0, 0)
            split(1, 1)
            pool.wait_ge(s_ce, 4)
            for i in range(2):
                nc.gpsimd.tensor_copy(KC[0:RD, i, :], KS[0:RD, :]).then_inc(s_kc, 1)
            pool.wait_ge(s_uv, B)
            values(0, 0)

            def step(g, par):
                if not isinstance(g, int) or g + 2 < NG:
                    split(g + 2, par)
                if not isinstance(g, int) or g + 1 < NG:
                    values(g + 1, 1 - par)

            steps(pool, step, 1, 28, [0], [29, 30])

            for i in range(HF):
                nc.gpsimd.memset(invf[:, i:i + 1], 1.0 / THETA ** (2 * i / XD_))
            nc.gpsimd.memset(before[:], 1.0)
            nc.gpsimd.memset(mask[:], 1.0).then_inc(s_con, 1)
            pool.wait_ge(s_con, 1)
            nc.gpsimd.affine_select(out=mask[:], in_=mask[:], compare_op=ALU.is_ge, fill=0.0, base=0,
                                    pattern=[[-XD_, XT_H]], channel_multiplier=1).then_inc(s_con, 1)
            nc.gpsimd.affine_select(out=before[:], in_=before[:], compare_op=ALU.is_gt, fill=0.0, base=0,
                                    pattern=[[1, E], [-1, E]], channel_multiplier=0).then_inc(s_con, 1)
            pool.wait_ge(s_con, 2)
            nc.gpsimd.affine_select(out=mask[:], in_=mask[:], compare_op=ALU.is_ge, fill=0.0, base=XD_ - 1,
                                    pattern=[[XD_, XT_H]], channel_multiplier=-1).then_inc(s_con, 1)
            pool.wait_ge(s_pv, 2 * NG)
            pool.wait_ge(s_b, 8 * NG)
            nc.gpsimd.memset(xv[:, :, :, XD_], 1.0).then_inc(s_con, 1)
            pool.wait_ge(s_con, 5)
            for u in range(NU):
                pool.wait_ge(s_kT, u + 1)
                if u >= 2:
                    pool.wait_ge(s_s, 2 * (u - 1))
                nc.gpsimd.tensor_tensor(KD[:, u % 2], kTs[:, u % 2, None, :].to_broadcast([P, XT_H, S]),
                                        mask[:, :, None].to_broadcast([P, XT_H, S]), ALU.mult).then_inc(s_kd, 1)
            pool.wait_ge(s_ffn, 80)
            for b in range(B):
                pool.wait_ge(s_xn, 2 * B + b + 1)
                nc.gpsimd.tensor_tensor(xs[:, b, :], xs[:, b, :], bias[:], ALU.add).then_inc(s_xb, 1)

        @block.scalar
        def _(act):
            def norm_high(n, dst):
                act.wait_ge(s_var, n + 1)
                nc.scalar.activation(rstd[:], rstd[:], ACT.Sqrt).then_inc(s_sd, 1)
                for b in range(B):
                    act.wait_ge(s_tp, n * B + b + 1)
                    nc.scalar.activation(dst[:, :, b * S:(b + 1) * S],
                                         PS[:, b % 2, :].rearrange("p (k s) -> p k s", k=KT), ACT.Copy).then_inc(s_th, 1)

            norm_high(0, XTh)
            act.wait_ge(s_c, 4)
            for t in range(2):
                sl = slice(t * HALF, (t + 1) * HALF)
                nc.scalar.activation(cT[:, sl], PS[:, 2 + t, :], ACT.Copy, scale=1 / WS).then_inc(s_ce, 1)
                nc.scalar.activation(KS[0:RD, sl], PS[0:RD, 4 + t, :], ACT.Copy, scale=1 / WS).then_inc(s_ce, 1)
            for u in range(16):
                act.wait_ge(s_u, u + 1)
                w, T, t = u // 8, u // 2 % 4, u % 2
                nc.scalar.activation(stg[:, 2 * w, T, t * HALF:(t + 1) * HALF], PS[:, (6, 7, 0, 1)[u % 4], :],
                                     ACT.Copy).then_inc(s_uh, 1)
            act.wait_ge(s_zero, 4)
            for b in range(B):
                act.wait_ge(s_u, 17 + b)
                nc.scalar.activation(V[:, b, :, 0:HD], PS[:, (6, 7, 0, 1)[b % 4], :].rearrange("p (h d) -> p h d", d=HD),
                                     ACT.Copy).then_inc(s_uv, 1)

            def q_high(g, par, c):
                t, p = c // 2, c % 2
                act.wait_ge(s_q, 4 * g + c + 1)
                for h in range(2):
                    nc.scalar.activation(QC[0:RD, par, t, 2 * p + h, :],
                                         PS[RD * h:RD * (h + 1), bQ[c % 2], :], ACT.Copy, scale=1 / WS).then_inc(s_qh, 1)

            def exps(g, b):
                act.wait_ge(s_b, 8 * g + b + 1)
                if not isinstance(g, int) or g >= 1:
                    act.wait_ge(s_pv, 2 * g - 1 + b // 4)
                nc.scalar.activation(PR[:, b, :], PS[:, bB[b % 2], :], ACT.Exp, scale=ATT_SCALE).then_inc(s_e, 1)

            def o_out(g, t):
                act.wait_ge(s_pv, 2 * g + t + 1)
                if not isinstance(g, int) or g >= 1:
                    act.wait_ge(s_od[t], 64 * g)
                nc.scalar.activation(OS[:, t, :], PS[:, bO, :], ACT.Copy).then_inc(s_oe, 1)

            def step(g, par):
                cur, nxt = not isinstance(g, int) or g >= 0, not isinstance(g, int) or g + 1 < NG
                if not isinstance(g, int) or g >= 1:
                    o_out(g - 1, 1)
                if nxt:
                    if not isinstance(g, int) or g >= 1:
                        act.wait_ge(s_b, 8 * g)
                    q_high(g + 1, 1 - par, 0)
                if cur:
                    for b in range(4):
                        exps(g, b)
                if nxt:
                    q_high(g + 1, 1 - par, 1)
                if cur:
                    o_out(g, 0)
                    exps(g, 4)
                    exps(g, 5)
                if nxt:
                    q_high(g + 1, 1 - par, 2)
                if cur:
                    exps(g, 6)
                    exps(g, 7)
                if nxt:
                    q_high(g + 1, 1 - par, 3)

            steps(act, step, 1, 30, [-1, 0], [31])
            o_out(NG - 1, 1)

            act.wait_ge(s_wx, 16)
            act.wait_ge(s_b, 8 * NG)
            nc.scalar.activation(Wxh[:], wx_raw[:], ACT.Copy, scale=WS).then_inc(s_xh, 1)
            act.wait_ge(s_ctx, 16)
            for k in range(KT):
                nc.scalar.activation(CTh[:, k], ctx_raw[:, k], ACT.Copy).then_inc(s_xh, 1)
            act.wait_ge(s_red, 1)
            nc.scalar.activation(sincos[:].rearrange("p a b f -> p (a b f)"), red[:].rearrange("p a b f -> p (a b f)"),
                                 ACT.Sin).then_inc(s_sc, 1)
            act.wait_ge(s_con, 5)
            for b in range(B):
                act.wait_ge(s_kvr, b + 1)
                nc.scalar.activation(xv[:, b, :, 0:XD_], PS[:, 4 + b % 2, NKV * XD_:2 * NKV * XD_].rearrange("p (h d) -> p h d", d=XD_),
                                     ACT.Copy, scale=1 / WS).then_inc(s_kvv, 1)
            norm_high(1, X2h)

            def q_turned(u):
                act.wait_ge(s_xt, u + 1)
                nc.scalar.activation(qTs[:, u % 2], PS[:, 1, 0:P], ACT.Copy).then_inc(s_qT, 1)

            q_turned(0)
            for u in range(NU):
                if u + 1 < NU:
                    q_turned(u + 1)
                for n in (2 * u, 2 * u + 1):
                    act.wait_ge(s_xm, n + 1)
                    if n >= 4:
                        act.wait_ge(s_pt, n - 3)
                    for j in range(REP):
                        last = nc.scalar.activation(XP[:, n % 4, j], PS[:, 2 + n % 4, j * S:(j + 1) * S], ACT.Exp,
                                                    bias=xm[:, n % 4, j:j + 1])
                    last.then_inc(s_ex, 1)
            for b in range(B):
                act.wait_ge(s_ot, b + 1)
                if b >= 2:
                    act.wait_ge(s_o2, b - 1)
                nc.scalar.activation(O2T[:, b % 2], PS[:, b % 2, :].rearrange("p (k s) -> p k s", k=KT), ACT.Copy
                                     ).then_inc(s_oT, 1)

            act.wait_ge(s_ffn, 80)
            act.wait_ge(s_kv, B)
            nc.scalar.activation(bwh[:], bw_raw[:], ACT.Copy, scale=WS).then_inc(s_bh, 1)
            nc.scalar.activation(agh[:], ag_raw[:], ACT.Copy, scale=WS).then_inc(s_bh, 1)
            norm_high(2, X2h)
            for b in range(B):
                act.wait_ge(s_lge, b + 1)
                nc.scalar.activation(low[:, b, :], PS[:, 2 + b % 2, 0:E * R], ACT.Copy, scale=1 / WS).then_inc(s_ge, 1)
            act.wait_ge(s_gx, 1)
            nc.scalar.activation(ex[:], ex[:], ACT.Exp).then_inc(s_gx, 1)
            for b in range(B):
                act.wait_ge(s_lt, b + 1)
                if b >= 2:
                    act.wait_ge(s_f, b - 1)
                nc.scalar.activation(lowT[:, b % 2], PS[:, 4 + b % 2, 0:S], ACT.Copy, scale=WS).then_inc(s_lT, 1)

        @block.vector
        def _(dve):
            chain = [0]

            def link(ins):
                chain[0] += 1
                ins.then_inc(s_dch, 1)
                dve.wait_ge(s_dch, chain[0])

            dve.wait_ge(s_wd, 16)
            link(nc.vector.tensor_scalar(wd_raw[:], wd_raw[:], WS, None, ALU.mult))
            link(nc.vector.tensor_copy(wd_h[:], wd_raw[:]))
            nc.vector.tensor_tensor(wd_l[:], wd_raw[:], wd_h[:], ALU.subtract).then_inc(s_wds, 1)

            def layernorm(n, to, high, lows):
                for b in range(B):
                    last = nc.vector.bn_stats(stats[:, b, :], xs[:, b, :])
                link(last)
                for b in range(B):
                    last = nc.vector.bn_aggr(mv[:, b, :], stats[:, b, :])
                link(last)
                nc.vector.tensor_scalar(rstd[:], mv[:, :, 1], EPS, None, ALU.add).then_inc(s_var, 1)
                dve.wait_ge(s_sd, n + 1)
                link(nc.vector.reciprocal(rstd[:], rstd[:]))
                for b in range(B):
                    nc.vector.tensor_scalar(to[:, b, :], xs[:, b, :], mv[:, b, 0:1], rstd[:, b:b + 1],
                                            ALU.subtract, ALU.mult).then_inc(s_xn, 1)
                for b in range(B):
                    dve.wait_ge(s_th, n * B + b + 1)
                    sl = slice(b * S, (b + 1) * S)
                    nc.vector.tensor_tensor(lows[:, :, sl], PS[:, b % 2, :].rearrange("p (k s) -> p k s", k=KT),
                                            high[:, :, sl], ALU.subtract).then_inc(s_tl, 1)

            dve.wait_ge(s_x, 16 * B)
            layernorm(0, xn, XTh, XTl)
            for t in range(2):
                sl = slice(t * HALF, (t + 1) * HALF)
                dve.wait_ge(s_ce, 2 * t + 2)
                nc.vector.scalar_tensor_tensor(KS[RD:P, sl], PS[0:RD, 4 + t, :], 1 / WS, KS[0:RD, sl],
                                               ALU.mult, ALU.subtract).then_inc(s_kl, 1)
            for u in range(16):
                dve.wait_ge(s_uh, u + 1)
                w, T, t = u // 8, u // 2 % 4, u % 2
                sl = slice(t * HALF, (t + 1) * HALF)
                nc.vector.tensor_tensor(stg[:, 2 * w + 1, T, sl], PS[:, (6, 7, 0, 1)[u % 4], :],
                                        stg[:, 2 * w, T, sl], ALU.subtract).then_inc(s_ul, 1)

            def q_low(g, par, c):
                t, p = c // 2, c % 2
                for h in range(2):
                    dve.wait_ge(s_qh, 8 * g + 2 * c + h + 1)
                    j = 2 * p + h
                    nc.vector.scalar_tensor_tensor(QS[0:RD, par, t, j, :], PS[RD * h:RD * (h + 1), bQ[c % 2], :], 1 / WS,
                                                   QC[0:RD, par, t, j, :], ALU.mult, ALU.subtract).then_inc(s_ql, 1)

            def row_max(g, par, b):
                dve.wait_ge(s_a, 8 * g + b + 1)
                nc.vector.tensor_reduce(mneg[:, par, b // 4, :, b % 4],
                                        PS[:, bA[b % 2], :].rearrange("p (j k) -> p j k", j=GH),
                                        AX.X, ALU.max, negate=True).then_inc(s_m, 1)

            def max_out(g, t):
                dve.wait_ge(s_mt, 2 * g + t + 1)
                if not isinstance(g, int) or g >= 1:
                    dve.wait_ge(s_md[t], 16 * g)
                nc.vector.tensor_scalar(mT[:, t, :], PS[0:16, bM, 0:S], 1 / MS, None, ALU.mult).then_inc(s_me, 1)

            def step(g, par):
                cur, nxt = not isinstance(g, int) or g >= 0, not isinstance(g, int) or g + 1 < NG
                if cur:
                    for b in (4, 5, 6):
                        row_max(g, par, b)
                if nxt:
                    q_low(g + 1, 1 - par, 0)
                if cur:
                    row_max(g, par, 7)
                    max_out(g, 1)
                if nxt:
                    q_low(g + 1, 1 - par, 1)
                    row_max(g + 1, 1 - par, 0)
                    row_max(g + 1, 1 - par, 1)
                    q_low(g + 1, 1 - par, 2)
                    row_max(g + 1, 1 - par, 2)
                    row_max(g + 1, 1 - par, 3)
                    max_out(g + 1, 0)
                    q_low(g + 1, 1 - par, 3)

            steps(dve, step, 1, 30, [-1, 0], [31])
            dve.wait_ge(s_ud, 16 * 2 * GH * KT)
            for T in range(KT):
                link(nc.vector.reciprocal(SU[:, T, :], SU[:, T, :]))
                nc.vector.tensor_tensor(U[:, T, :], U[:, T, :], SU[:, T, :], ALU.mult).then_inc(s_un, 1)
            for b in range(B):
                dve.wait_ge(s_o1, b + 1)
                nc.vector.tensor_tensor(xs[:, b, :], xs[:, b, :], PS[:, b % 4, :], ALU.add).then_inc(s_x1, 1)

            dve.wait_ge(s_pos, 16)
            dve.wait_ge(s_con, 5)
            link(nc.vector.tensor_copy(posf[:], posi[:]))
            link(nc.vector.tensor_tensor(ang[:], posf[:, :, None].to_broadcast([P, B, HF]),
                                         invf[:, None, :].to_broadcast([P, B, HF]), ALU.mult))
            for i, quarter in enumerate((0.0, 0.25)):
                r = red[:, i]
                link(nc.vector.tensor_scalar(turns[:], ang[:], 1 / (2 * math.pi), quarter, ALU.mult, ALU.add))
                link(nc.vector.tensor_scalar(turns[:], turns[:], MAGIC, None, ALU.add))
                link(nc.vector.tensor_scalar(turns[:], turns[:], MAGIC, None, ALU.subtract))
                src = ang[:]
                for part in TWO_PI:
                    link(nc.vector.scalar_tensor_tensor(r, turns[:], -part, src, ALU.mult, ALU.add))
                    src = r
                link(nc.vector.tensor_scalar(r, r, quarter * 2 * math.pi, math.pi, ALU.add, ALU.min))
                last = nc.vector.tensor_scalar(r, r, -math.pi, None, ALU.max)
                if i == 0:
                    link(last)
            last.then_inc(s_red, 1)
            dve.wait_ge(s_xh, 1)
            nc.vector.scalar_tensor_tensor(Wxl[:], wx_raw[:], WS, Wxh[:], ALU.mult, ALU.subtract).then_inc(s_xl, 1)
            for k in range(KT):
                dve.wait_ge(s_xh, k + 2)
                nc.vector.tensor_tensor(CTl[:, k], ctx_raw[:, k], CTh[:, k], ALU.subtract).then_inc(s_xl, 1)
            dve.wait_ge(s_sc, 1)
            for co, si, f in ((cosq, sinq, XS / WS), (cosk, sink, 1 / WS)):
                nc.vector.tensor_scalar(co[:], sincos[:, 1], f, None, ALU.mult)
                nc.vector.tensor_scalar(si[:, :, 0, :], sincos[:, 0], -f, None, ALU.mult)
                last = nc.vector.tensor_scalar(si[:, :, 1, :], sincos[:, 0], f, None, ALU.mult)
            link(last)

            def rope(to, src, nh, b, co, si):
                q = src.rearrange("p (h a f) -> p h a f", a=2, f=HF)
                t = [rt[:, i, 0:nh * XD_].rearrange("p (h a f) -> p h a f", a=2, f=HF) for i in range(2)]
                nc.vector.tensor_tensor(t[0], q, co[:, b, None, None, :].to_broadcast([P, nh, 2, HF]), ALU.mult)
                nc.vector.tensor_tensor(t[1][:, :, 0, :], q[:, :, 1, :], si[:, b, 0, None, :].to_broadcast([P, nh, HF]), ALU.mult)
                link(nc.vector.tensor_tensor(t[1][:, :, 1, :], q[:, :, 0, :], si[:, b, 1, None, :].to_broadcast([P, nh, HF]), ALU.mult))
                if nh == XH:
                    return nc.vector.tensor_tensor(to, rt[:, 0, :], rt[:, 1, :], ALU.add)
                t = [rt[:, i, 0:nh * XD_].rearrange("p (h d) -> p h d", d=XD_)[:, :, None, :].to_broadcast([P, nh, REP, XD_])
                     for i in range(2)]
                return nc.vector.tensor_tensor(to, t[0], t[1], ALU.add)

            for b in range(B):
                dve.wait_ge(s_kv, b + 1)
                rope(kr[:, b], PS[:, 4 + b % 2, 0:NKV * XD_], NKV, b, cosk, sink).then_inc(s_kvr, 1)
                dve.wait_ge(s_kvr, b + 1)
            layernorm(1, O2, X2h, X2l)
            for b in range(B):
                dve.wait_ge(s_xq, b + 1)
                rope(qr[:, b], PS[:, 2 + b % 2, :], XH, b, cosq, sinq).then_inc(s_xqr, 1)
                dve.wait_ge(s_xqr, b + 1)

            def k_turned(u):
                dve.wait_ge(s_xt, u + 1)
                if u >= 2:
                    dve.wait_ge(s_kd, u - 1)
                nc.vector.tensor_copy(kTs[:, u % 2], PS[:, 0, 0:P]).then_inc(s_kT, 1)

            def x_max(n):
                dve.wait_ge(s_s, n + 1)
                if n >= 4:
                    dve.wait_ge(s_ex, n - 3)
                nc.vector.tensor_reduce(xm[:, n % 4], PS[:, 2 + n % 4, :].rearrange("p (j k) -> p j k", j=REP),
                                        AX.X, ALU.max, negate=True).then_inc(s_xm, 1)

            def p_turned(n):
                dve.wait_ge(s_pt, n + 1)
                if n >= 2:
                    dve.wait_ge(s_xo, n - 1)
                nc.vector.tensor_copy(XPT[:, n % 2].rearrange("p j q -> p (j q)"), PS[:, 6 + n % 2, :]).then_inc(s_pe, 1)

            k_turned(0)
            x_max(0)
            x_max(1)
            for u in range(NU):
                if u + 1 < NU:
                    k_turned(u + 1)
                p_turned(2 * u)
                if u + 1 < NU:
                    x_max(2 * u + 2)
                p_turned(2 * u + 1)
                if u + 1 < NU:
                    x_max(2 * u + 3)
                dve.wait_ge(s_xo, 2 * u + 2)
                o = PS[:, 1, 256:256 + XT_H * XVC].rearrange("p (h c) -> p h c", c=XVC)
                link(nc.vector.reciprocal(rz[:], o[:, :, XD_]))
                b, t = u // KT, u % KT
                nc.vector.tensor_tensor(O2[:, b, t * P:(t + 1) * P].rearrange("p (h d) -> p h d", d=XD_), o[:, :, 0:XD_],
                                        rz[:, :, None].to_broadcast([P, XT_H, XD_]), ALU.mult).then_inc(s_xon, 1)
                dve.wait_ge(s_xon, u + 1)
            for b in range(B):
                dve.wait_ge(s_o2, b + 1)
                nc.vector.tensor_tensor(xs[:, b, :], xs[:, b, :], PS[:, 2 + b % 2, :], ALU.add).then_inc(s_x2, 1)

            dve.wait_ge(s_bh, 2)
            nc.vector.scalar_tensor_tensor(bwl[:], bw_raw[:], WS, bwh[:], ALU.mult, ALU.subtract).then_inc(s_bl, 1)
            nc.vector.scalar_tensor_tensor(agl[:], ag_raw[:], WS, agh[:], ALU.mult, ALU.subtract).then_inc(s_bl, 1)
            dve.wait_ge(s_x2, B)
            layernorm(2, O2, X2h, X2l)
            for b in range(B):
                dve.wait_ge(s_lg, b + 1)
                nc.vector.tensor_scalar(lg[:, b, :], PS[:, 2 + b % 2, E * R:AG], 1 / WS, None, ALU.mult).then_inc(s_lge, 1)
            dve.wait_ge(s_lge, B)
            link(nc.vector.tensor_reduce(mx[:], lg[:], AX.X, ALU.max))
            nc.vector.tensor_tensor(ex[:], lg[:], mx[:, :, None].to_broadcast([P, B, E]), ALU.subtract).then_inc(s_gx, 1)
            one = lg[:, :, :, None].to_broadcast([P, B, E, E])
            other = lg[:, :, None, :].to_broadcast([P, B, E, E])
            nc.vector.tensor_tensor(gt[:], other, one, ALU.is_gt)
            link(nc.vector.tensor_tensor(eq[:], other, one, ALU.is_equal))
            link(nc.vector.tensor_tensor(eq[:], eq[:], before[:, None, :, :].to_broadcast([P, B, E, E]), ALU.mult))
            link(nc.vector.tensor_tensor(gt[:], gt[:], eq[:], ALU.add))
            link(nc.vector.tensor_reduce(rank[:], gt[:], AX.X, ALU.add))
            dve.wait_ge(s_gx, 2)
            link(nc.vector.scalar_tensor_tensor(ex[:], rank[:], 1.5, ex[:], ALU.is_lt, ALU.mult))
            link(nc.vector.tensor_reduce(mx[:], ex[:], AX.X, ALU.add))
            link(nc.vector.reciprocal(mx[:], mx[:]))
            link(nc.vector.tensor_scalar(mx[:], mx[:], SCALING, None, ALU.mult))
            link(nc.vector.tensor_tensor(ex[:], ex[:], mx[:, :, None].to_broadcast([P, B, E]), ALU.mult))
            dve.wait_ge(s_ge, B)
            for b in range(B):
                l = low[:, b, :].rearrange("p (e r) -> p e r", r=R)
                nc.vector.tensor_tensor(l, l, ex[:, b, :, None].to_broadcast([P, E, R]), ALU.mult).then_inc(s_lw, 1)
            for b in range(B):
                dve.wait_ge(s_f, b + 1)
                dve.wait_ge(s_xb, b + 1)
                nc.vector.scalar_tensor_tensor(xs[:, b, :], PS[:, 6 + b % 2, :], 1 / WS, xs[:, b, :],
                                               ALU.mult, ALU.add).then_inc(s_x3, 1)

        @block.tensor
        def _(pe):
            mm = nc.tensor.matmul
            def norm_turn(n, src):
                for b in range(B):
                    pe.wait_ge(s_xn, n * B + b + 1)
                    if b >= 2:
                        pe.wait_ge(s_tl, n * B + b - 1)
                    for k in range(KT):
                        last = nc.tensor.transpose(PS[:, b % 2, k * S:(k + 1) * S], src[:, b, k * P:(k + 1) * P], ident[:])
                    last.then_inc(s_tp, 1)

            pe.wait_ge(s_id, 1)
            norm_turn(0, xn)

            pe.wait_ge(s_wds, 1)
            pe.wait_ge(s_tl, B)
            for m, (c0, w) in enumerate([(0, 2 * LAT), (2 * LAT, RD)]):
                for t in range(2):
                    sl = slice(t * HALF, (t + 1) * HALF)
                    for k in range(KT):
                        for n, (wt, xt) in enumerate([(wd_h, XTh), (wd_h, XTl), (wd_l, XTh)]):
                            last = mm(PS[0:w, 2 + 2 * m + t, :], wt[:, k, c0:c0 + w], xt[:, k, sl],
                                      start=(k == 0 and n == 0), stop=(k == KT - 1 and n == 2))
                    last.then_inc(s_c, 1)
            pe.wait_ge(s_up, 32)
            pe.wait_ge(s_ce, 4)
            for u in range(24):
                bank = (6, 7, 0, 1)[u % 4]
                if 4 <= u < 20:
                    pe.wait_ge(s_ul, u - 3)
                if u >= 20:
                    pe.wait_ge(s_uv, u - 19)
                if u < 16:
                    w, T, t = u // 8, u // 2 % 4, u % 2
                    r = LAT * w
                    mm(PS[:, bank, :], up[r:r + LAT, T * P:(T + 1) * P], cT[r:r + LAT, t * HALF:(t + 1) * HALF],
                       start=True, stop=True).then_inc(s_u, 1)
                else:
                    b = u - 16
                    mm(PS[:, bank, :], cT[LAT:P, b * S:(b + 1) * S], vup[LAT:P, :],
                       start=True, stop=True).then_inc(s_u, 1)
            pe.wait_ge(s_kl, 2)
            pe.wait_ge(s_ul, 16)
            pe.wait_ge(s_uv, B)

            def project(g, par, c, k):
                t, p = c // 2, c % 2
                sl = slice(t * HALF, (t + 1) * HALF)
                if k == 0:
                    if c == 0:
                        pe.wait_ge(s_ws, g + 1)
                    if not isinstance(g, int) or g >= 1 or c >= 2:
                        pe.wait_ge(s_ql, 8 * g + 2 * (c - 1))
                for n, (wt, xt) in enumerate([(Wh, XTh), (Wh, XTl), (Wl, XTh)]):
                    last = mm(PS[:, bQ[c % 2], :], wt[:, par, k, p * P:(p + 1) * P], xt[:, k, sl],
                              start=(k == 0 and n == 0), stop=(k == KT - 1 and n == 2))
                if k == KT - 1:
                    last.then_inc(s_q, 1)

            def rough_scores(g, par, b):
                if b == 0:
                    pe.wait_ge(s_y[par], (g - par) * 40 + 80)
                if b % 4 == 0:
                    pe.wait_ge(s_qh, 8 * g + b + 4)
                if not isinstance(g, int) or g >= 1 or b >= 2:
                    pe.wait_ge(s_m, 8 * g + b - 1)
                for j in range(GH):
                    last = mm(PS[:, bA[b % 2], j * S:(j + 1) * S], QC[0:MROW, par, b // 4, j, b % 4 * S:(b % 4 + 1) * S],
                              KC[0:MROW, par, b * S:(b + 1) * S], start=True, stop=True)
                last.then_inc(s_a, 1)

            def max_turn(g, par, t):
                pe.wait_ge(s_m, 8 * g + 4 * t + 4)
                if not isinstance(g, int) or g >= 1 or t >= 1:
                    pe.wait_ge(s_me, 2 * g + t)
                nc.tensor.transpose(PS[0:16, bM, 0:S], mneg[:, par, t].rearrange("p j b -> p (j b)"), ident[:]).then_inc(s_mt, 1)

            def scores(g, par, b):
                t = b // 4
                if b % 4 == 0:
                    pe.wait_ge(s_md[t], 16 * (g + 1))
                    pe.wait_ge(s_qd[t], 16 * (g + 1))
                    pe.wait_ge(s_ql, 8 * g + 4 * t + 4)
                if not isinstance(g, int) or g >= 1 or b >= 2:
                    pe.wait_ge(s_e, 8 * g + b - 1)
                mm(PS[:, bB[b % 2], :].rearrange("p (j q) -> p j q", j=GH), KC[0:MROW + 1, par, b * S:(b + 1) * S],
                   QC[0:MROW + 1, par, t, :, b % 4 * S:(b % 4 + 1) * S], start=True, stop=False)
                mm(PS[:, bB[b % 2], :].rearrange("p (j q) -> p j q", j=GH), KS[:, b * S:(b + 1) * S],
                   QS[:, par, t, :, b % 4 * S:(b % 4 + 1) * S], start=False, stop=True).then_inc(s_b, 1)

            def weigh(g, par, t):
                pe.wait_ge(s_e, 8 * g + 4 * t + 4)
                if t == 0:
                    pe.wait_ge(s_vg, g + 1)
                if not isinstance(g, int) or g >= 1 or t >= 1:
                    pe.wait_ge(s_oe, 2 * g + t)
                for b in range(4):
                    last = mm(PS[32 * b:32 * (b + 1), bO, :], Vg[:, par, 4 * t + b, :], PR[:, 4 * t + b, :],
                              start=True, stop=True)
                last.then_inc(s_pv, 1)

            def step(g, par):
                cur, nxt = not isinstance(g, int) or g >= 0, not isinstance(g, int) or g + 1 < NG
                prev = not isinstance(g, int) or g >= 1
                o = 1 - par
                for c in range(4):
                    for k in range(KT):
                        if nxt:
                            project(g + 1, o, c, k)
                        at = (c, k)
                        if cur and at in ((0, 1), (0, 2), (0, 3), (1, 0)):
                            rough_scores(g, par, 4 * c + k + 3)
                        if prev and at == (0, 2):
                            weigh(g - 1, o, 1)
                        if cur and at == (1, 2):
                            max_turn(g, par, 1)
                        if cur and c == 1:
                            scores(g, par, k)
                        if cur and at == (2, 1):
                            weigh(g, par, 0)
                        if nxt and at in ((2, 2), (2, 3), (3, 0), (3, 1)):
                            rough_scores(g + 1, o, 4 * c + k - 10)
                        if cur and at in ((2, 2), (2, 3), (3, 0), (3, 1)):
                            scores(g, par, 4 * c + k - 6)
                        if nxt and at == (3, 3):
                            max_turn(g + 1, o, 0)

            steps(pe, step, 1, 30, [-1, 0], [31])
            weigh(NG - 1, (NG - 1) % 2, 1)

            pe.wait_ge(s_wo, 16)
            for T in range(KT):
                pe.wait_ge(s_un, T + 1)
            for b in range(B):
                if b >= 4:
                    pe.wait_ge(s_x1, b - 3)
                for T in range(KT):
                    last = mm(PS[:, b % 4, :], U[:, T, b * S:(b + 1) * S], wo_sb[:, T, :], start=(T == 0), stop=(T == KT - 1))
                last.then_inc(s_o1, 1)

            def parts(bank, xh, xl, wh, wl, b, c0, c1, start=True, stop=True):
                sl = slice(b * S, (b + 1) * S)
                for k in range(KT):
                    for n, (xt, wt) in enumerate([(xh, wh), (xh, wl), (xl, wh)]):
                        last = mm(PS[:, bank, 0:c1 - c0], xt[:, k, sl], wt[:, k, c0:c1],
                                  start=(start and k == 0 and n == 0), stop=(stop and k == KT - 1 and n == 2))
                return last

            def x_out(b):
                pe.wait_ge(s_oT, b + 1)
                if b >= 2:
                    pe.wait_ge(s_x2, b - 1)
                for k in range(KT):
                    last = mm(PS[:, 2 + b % 2, :], O2T[:, b % 2, k], xwo_sb[:, k, :], start=(k == 0), stop=(k == KT - 1))
                last.then_inc(s_o2, 1)

            pe.wait_ge(s_xl, 1 + KT)
            for b in range(B):
                if b >= 2:
                    pe.wait_ge(s_kvv, b - 1)
                parts(4 + b % 2, CTh, CTl, Wxh, Wxl, b, DM, XW).then_inc(s_kv, 1)
            pe.wait_ge(s_x1, B)
            norm_turn(1, O2)
            pe.wait_ge(s_tl, 2 * B)
            for b in range(B):
                if b >= 2:
                    pe.wait_ge(s_xqr, b - 1)
                parts(2 + b % 2, X2h, X2l, Wxh, Wxl, b, 0, DM).then_inc(s_xq, 1)
            pe.wait_ge(s_xqr, B)

            def turn(u):
                b, t = u // KT, u % KT
                if u >= 1:
                    pe.wait_ge(s_kT, u)
                    pe.wait_ge(s_qT, u)
                if u >= 2:
                    pe.wait_ge(s_xon, u - 1)
                keys = kr[:, b, 2 * t:2 * t + 2].rearrange("p h r d -> p (h r d)")
                nc.tensor.transpose(PS[:, 0, 0:P], keys, ident[:])
                nc.tensor.transpose(PS[:, 1, 0:P], qr[:, b, t * P:(t + 1) * P], ident[:]).then_inc(s_xt, 1)

            def x_scores(u):
                pe.wait_ge(s_kd, u + 1)
                pe.wait_ge(s_qT, u + 1)
                for n in (2 * u, 2 * u + 1):
                    if n >= 4:
                        pe.wait_ge(s_ex, n - 3)
                    mm(PS[:, 2 + n % 4, :], qTs[:, u % 2], KD[:, u % 2, REP * (n % 2):REP * (n % 2 + 1), :],
                       start=True, stop=True).then_inc(s_s, 1)

            turn(0)
            x_scores(0)
            for u in range(NU):
                b, t = u // KT, u % KT
                if u + 1 < NU:
                    turn(u + 1)
                for n in (2 * u, 2 * u + 1):
                    pe.wait_ge(s_ex, n + 1)
                    if n >= 2:
                        pe.wait_ge(s_pe, n - 1)
                    for j in range(REP):
                        last = nc.tensor.transpose(PS[:, 6 + n % 2, j * S:(j + 1) * S], XP[:, n % 4, j], ident[:])
                    last.then_inc(s_pt, 1)
                    if n % 2 == 0 and u + 1 < NU:
                        x_scores(u + 1)
                for n in (2 * u, 2 * u + 1):
                    pe.wait_ge(s_pe, n + 1)
                    if n % 2 == 0:
                        if u >= 1:
                            pe.wait_ge(s_xon, u)
                        if u + 1 < NU:
                            pe.wait_ge(s_qT, u + 2)
                    for j in range(REP):
                        c = 256 + (n % 2 * REP + j) * XVC
                        last = mm(PS[:, 1, c:c + XVC], XPT[:, n % 2, j], xv[:, b, 2 * t + n % 2, :], start=True, stop=True)
                    last.then_inc(s_xo, 1)
            pe.wait_ge(s_xon, NU)
            pe.wait_ge(s_ffn, 80)
            for b in range(B):
                if b >= 2:
                    pe.wait_ge(s_oT, b - 1)
                for k in range(KT):
                    last = nc.tensor.transpose(PS[:, b % 2, k * S:(k + 1) * S], O2[:, b, k * P:(k + 1) * P], ident[:])
                last.then_inc(s_ot, 1)
                if b >= 1:
                    x_out(b - 1)
            x_out(B - 1)

            pe.wait_ge(s_bl, 2)
            pe.wait_ge(s_x2, B)
            norm_turn(2, O2)
            pe.wait_ge(s_tl, 3 * B)
            for b in range(B):
                if b >= 2:
                    pe.wait_ge(s_ge, b - 1)
                parts(2 + b % 2, X2h, X2l, agh, agl, b, 0, AG).then_inc(s_lg, 1)
            for b in range(B):
                pe.wait_ge(s_lw, b + 1)
                if b >= 2:
                    pe.wait_ge(s_x3, b - 1)
                parts(6 + b % 2, X2h, X2l, bwh, bwl, b, 0, DM, stop=False)
                if b >= 2:
                    pe.wait_ge(s_lT, b - 1)
                nc.tensor.transpose(PS[:, 4 + b % 2, 0:S], low[:, b, :], ident[:]).then_inc(s_lt, 1)
                pe.wait_ge(s_lT, b + 1)
                mm(PS[:, 6 + b % 2, :], lowT[:, b % 2], lb_sb[:], start=False, stop=True).then_inc(s_f, 1)


def kernel(**inputs):
    import numpy as np
    import concourse.bacc as bacc
    from concourse.bass_utils import run_bass_kernel_spmd

    a = {k: np.asarray(v) for k, v in inputs.items()}
    rows = lambda w: np.ascontiguousarray(w.reshape(KT, P, -1).transpose(1, 0, 2))
    arrays = {
        "x": a["x"],
        "ctxT": rows(a["ctx_4096"].reshape(TOK, DM).T),
        "pos": np.ascontiguousarray(a["itok_BxS2_0_2047"].T),
        "wdkr": rows(np.concatenate([a["L0_attn_Wq_down"], a["L0_attn_Wkv_down"], a["L0_attn_Wk_rope"]], 1)),
        "wup": np.concatenate([a["L0_attn_Wq_up"], a["L0_attn_Wk_up"]], 0),
        "wvup": a["L0_attn_Wv_up"],
        "wqr": np.ascontiguousarray(a["L0_attn_Wq_rope"].reshape(KT, P, NG, GW).transpose(2, 1, 0, 3)),
        "wo": rows(a["L0_attn_Wo"].reshape(KT, NG // KT, GH, HD, DM).transpose(0, 2, 1, 3, 4).reshape(DM, DM)),
        "xwqkv": rows(np.concatenate([a["L0_xattn_Wq"], a["L0_xattn_Wk"], a["L0_xattn_Wv"]], 1)),
        "xwo": rows(a["L0_xattn_Wo"]),
        "bw": rows(a["L0_ffn_base_w"].T),
        "ag": rows(np.concatenate([a["L0_ffn_lora_A"].reshape(P, DM).T, a["L0_ffn_gate_w"].T], 1)),
        "lb": np.ascontiguousarray(a["L0_ffn_lora_B"].transpose(0, 2, 1).reshape(P, DM)),
        "bb": a["L0_ffn_base_b"].reshape(1, DM),
    }
    nc = bacc.Bacc("TRN2", target_bir_lowering=False, num_devices=1)
    args = [nc.dram_tensor("in_" + k, v.shape, mybir.dt.from_np(v.dtype), kind="ExternalInput").ap() for k, v in arrays.items()]
    out = nc.dram_tensor("y", (B, S, DM), F32, kind="ExternalOutput").ap()
    build(nc, *args, out)
    r = run_bass_kernel_spmd(nc, [{"in_" + k: np.ascontiguousarray(v) for k, v in arrays.items()}], core_ids=[0])
    return r.results[0]["y"]
```

```python
import math
from contextlib import ExitStack

import concourse.bass as bass
from concourse import mybir

F32 = mybir.dt.float32
F16 = mybir.dt.float16
I32 = mybir.dt.int32
ALU = mybir.AluOpType
ACT = mybir.ActivationFunctionType
AX = mybir.AxisListType

P = 128
B, S, DM = 8, 128, 512
TOK = B * S
KT = DM // P
HALF = TOK // 2
EPS = 1e-5
WS = 256.0

H, HD, RD, LAT = 128, 4, 64, 64
GH = 4
NG = H // GH
HT = H // KT
GW = GH * RD
CR = 3 * HD
CROW = RD
MROW = RD + GH * CR
MS = 16.0
ATT_SCALE = float(HD + RD) ** -0.5
VC = HD + 1

XH, NKV, XD_, THETA = 32, 8, 16, 10000.0
REP = XH // NKV
HF = XD_ // 2
XT_H = P // XD_
XS = float(XD_) ** -0.5
XVC = XD_ + 1
KW = NKV * XD_
NU = B * KT
TWO_PI = (6.28125, 0.0019340515136718750, 1.2556659146e-06)
MAGIC = 1.5 * 2 ** 23

E, R, SCALING = 8, 16, 2.0
AG = E * R + E


def build(nc, x, ctxT, pos, wdkr, wup, wvup, wqr, wo, xwq, xwkv, xwo, bw, ag, lb, bb, out):
    es = ExitStack()
    with es:
        def sem(name):
            return es.enter_context(nc.semaphore(name))

        top = [(nc.sbuf_base + 63) // 64 * 64]
        size = {F32: 4, F16: 2, I32: 4}

        def sb(name, shape, dt=F32):
            n = size[dt]
            for s in shape[1:]:
                n *= s
            at = top[0]
            top[0] = at + (n + 63) // 64 * 64
            return nc.alloc_sbuf_tensor_at(name, shape, dt, offset=at)

        xs = sb("xs", [P, B, DM])
        ident = sb("ident", [P, P])
        stats = sb("stats", [P, B, 6])
        mv = sb("mv", [P, 3, B, 2])
        rstd = sb("rstd", [P, 3, B])
        power = sb("power", [P, 1])
        wscale = sb("wscale", [P, 1, 1])
        wo_sb = sb("wo_sb", [P, KT, DM])
        wx_raw = sb("wx_raw", [P, KT, DM])
        krc = sb("krc", [P, B, NKV, XD_])
        xv = sb("xv", [P, B, NKV, XVC])
        xwo_sb = sb("xwo_sb", [P, KT, DM])
        bw_raw = sb("bw_raw", [P, KT, DM])
        ag_raw = sb("ag_raw", [P, KT, AG])
        posi = sb("posi", [P, B], I32)
        posf = sb("posf", [P, B])
        invf = sb("invf", [P, HF])
        ang = sb("ang", [P, B, HF])
        turns = sb("turns", [P, B, HF])
        red = sb("red", [P, 2, B, HF])
        sincos = sb("sincos", [P, 2, B, HF])
        cosq = sb("cosq", [P, B, HF])
        sinq = sb("sinq", [P, B, 2, HF])
        cosk = sb("cosk", [P, B, HF])
        sink = sb("sink", [P, B, 2, HF])
        mask = sb("mask", [P, XT_H])
        before = sb("before", [P, E, E])
        phase = top[0]

        XTh = sb("XTh", [P, KT, TOK], F16)
        XTl = sb("XTl", [P, KT, TOK], F16)
        Wraw = sb("Wraw", [P, 2, KT, GW])
        Wh = sb("Wh", [P, 2, KT, GW], F16)
        Wl = sb("Wl", [P, 2, KT, GW], F16)
        QC = sb("QC", [P, 2, 2, GH, HALF], F16)
        t2_at = top[0]
        QS = sb("QS", [P, 2, 2, GH, HALF], F16)
        KC = sb("KC", [P, 2, TOK], F16)
        KS = sb("KS", [P, TOK], F16)
        pr_at = top[0]
        PR = sb("PR", [P, B, GH * S])
        v_at = top[0]
        V = sb("V", [P, B, H, VC])
        Vg = sb("Vg", [P, 2, B, 32])
        os_at = top[0]
        OS = sb("OS", [P, 2, GH * S])
        mneg = sb("mneg", [P, 2, 2, GH, B // 2])
        mT = sb("mT", [16, 2, S], F16)
        stg = sb("stg", [P, 4, KT, TOK], F16)
        end1 = top[0]
        top[0] = pr_at
        xn = sb("xn", [P, B, DM])
        top[0] = t2_at
        wd_raw = sb("wd_raw", [P, KT, 3 * LAT])
        wd_h = sb("wd_h", [P, KT, 3 * LAT], F16)
        wd_l = sb("wd_l", [P, KT, 3 * LAT], F16)
        up = sb("up", [P, DM])
        vup = sb("vup", [P, DM])
        top[0] = os_at
        cT = sb("cT", [P, TOK])
        assert top[0] <= os_at + 2 * GH * S * 4
        top[0] = end1 - 4 * KT * TOK * 2
        U = sb("U", [P, KT, TOK])
        SU = sb("SU", [P, KT, TOK])
        assert end1 <= nc.sbuf_usable_end
        top[0] = v_at
        kvw_raw = sb("kvw_raw", [P, KT, 2 * KW])
        kvw_h = sb("kvw_h", [P, KT, 2 * KW], F16)
        kvw_l = sb("kvw_l", [P, KT, 2 * KW], F16)
        krt = sb("krt", [P, 2, KW])
        assert top[0] <= v_at + B * H * VC * 4
        top[0] = end1 - 4 * KT * TOK * 2
        ctx_raw = sb("ctx_raw", [P, KT, TOK])
        CTh = sb("CTh", [P, KT, TOK], F16)
        CTl = sb("CTl", [P, KT, TOK], F16)
        top[0] = phase
        lb_sb = sb("lb_sb", [P, DM])
        bias = sb("bias", [P, DM])
        Wxh = sb("Wxh", [P, KT, DM], F16)
        Wxl = sb("Wxl", [P, KT, DM], F16)
        bwh = sb("bwh", [P, KT, DM], F16)
        bwl = sb("bwl", [P, KT, DM], F16)
        agh = sb("agh", [P, KT, AG], F16)
        agl = sb("agl", [P, KT, AG], F16)
        kr = sb("kr", [P, B, NKV, REP, XD_])
        pn = sb("pn", [P, 3, 2, DM])
        Ah = sb("Ah", [P, 3, 2, KT, S], F16)
        Al = sb("Al", [P, 3, 2, KT, S], F16)
        rt = sb("rt", [P, 2, DM])
        qr = sb("qr", [P, 2, DM])
        KQ = sb("KQ", [P, 3, 2, P])
        KD = sb("KD", [P, 2, XT_H, S])
        xm = sb("xm", [P, 4, REP])
        XP = sb("XP", [P, 4, REP, S])
        XPT = sb("XPT", [P, 2, REP, S])
        rz = sb("rz", [P, XT_H])
        O2 = sb("O2", [P, 2, DM])
        O2T = sb("O2T", [P, 2, KT, S])
        lg = sb("lg", [P, E])
        ex = sb("ex", [P, E])
        mx = sb("mx", [P, 1])
        gt = sb("gt", [P, E, E])
        eq = sb("eq", [P, E, E])
        rank = sb("rank", [P, E])
        low = sb("low", [P, 2, E * R])
        lowT = sb("lowT", [P, 2, S])
        assert top[0] <= end1 - 4 * KT * TOK * 2

        PS = es.enter_context(nc.psum_tensor("PS", [P, 8, 512], F32))

        YD = nc.dram_tensor("q_content_parts", [H, CR, TOK], F16, kind="Internal").ap()
        XD = nc.dram_tensor("k_content_parts", [H, CR, TOK], F16, kind="Internal").ap()
        OD = nc.dram_tensor("head_outputs", [NG, GH * VC, GH, B, S], F32, kind="Internal").ap()

        s_x, s_wd, s_up, s_wo = sem("x_in"), sem("wd_in"), sem("up_in"), sem("wo_in")
        s_zero, s_fill, s_id = sem("zeroed"), sem("filled"), sem("ident_ready")
        s_con = sem("constants")
        s_dch, s_pch = sem("dve_chain"), sem("pool_chain")
        s_wds = sem("wd_split")
        s_c, s_ce, s_kl, s_kc = sem("c_ready"), sem("c_out"), sem("k_low"), sem("k_copied")
        s_u, s_uh, s_ul, s_uv = sem("up_ready"), sem("up_high"), sem("up_low"), sem("v_out")
        s_yx = sem("content_stored")
        s_w = [sem("w_in0"), sem("w_in1")]
        s_ws = sem("w_split")
        s_vg = sem("vg_ready")
        s_q, s_qh, s_ql = sem("q_ready"), sem("q_high"), sem("q_low")
        s_y = [sem("y_in0"), sem("y_in1")]
        s_a, s_m, s_mt, s_me = sem("a_ready"), sem("max_ready"), sem("mT_ready"), sem("mT_out")
        s_md = [sem("m_in0"), sem("m_in1")]
        s_qd = [sem("qs_in0"), sem("qs_in1")]
        s_b, s_e, s_pv, s_oe = sem("b_ready"), sem("exp_ready"), sem("pv_ready"), sem("o_out")
        s_od = [sem("o_stored0"), sem("o_stored1")]
        s_ud = [sem(f"u_in{T}") for T in range(KT)]
        s_un, s_o1, s_x1 = sem("u_norm"), sem("o1_ready"), sem("x1_ready")
        s_out = sem("stored")
        s_wx, s_ctx, s_pos, s_ffn = sem("xw_in"), [sem(f"ctx_in{k}") for k in range(KT)], sem("pos_in"), sem("ffn_in")
        s_red, s_sc = sem("angles_ready"), sem("sincos_ready")
        s_kw, s_kvh, s_kvl = sem("kvw_in"), sem("ctx_high"), sem("ctx_low")
        s_kv, s_kvo, s_kvr, s_kx = sem("kv_ready"), sem("kv_out"), sem("k_roped"), sem("k_spread")
        s_xh, s_xl = sem("weights_high"), sem("weights_low")
        n_var = [sem(f"var_ready{n}") for n in range(3)]
        n_sd = [sem(f"rstd_ready{n}") for n in range(3)]
        n_xn = [sem(f"normed{n}") for n in range(3)]
        n_tp = [sem(f"normed_turned{n}") for n in range(3)]
        n_th = [sem(f"normed_high{n}") for n in range(3)]
        n_tl = [sem(f"normed_low{n}") for n in range(3)]
        s_xq, s_xqp, s_xqr = sem("xq_ready"), sem("xq_read"), sem("xq_roped")
        s_xt, s_kq, s_kd = sem("kq_turned"), sem("kq_out"), sem("kd_ready")
        s_s, s_xm, s_ex, s_pt, s_pe = sem("xs_ready"), sem("xmax_ready"), sem("xexp_ready"), sem("pT_ready"), sem("pT_out")
        s_xo, s_xon = sem("xo_ready"), sem("xo_out")
        s_ot, s_oT, s_o2, s_x2 = sem("oT_ready"), sem("oT_out"), sem("o2_ready"), sem("x2_ready")
        s_xb, s_lg, s_lge, s_ge = sem("bias_added"), sem("low_ready"), sem("logits_out"), sem("low_out")
        s_gx, s_gy = sem("gate_ready"), sem("gate_exp")
        s_lw, s_lt, s_lT, s_f, s_x3 = sem("low_weighted"), sem("lowT_ready"), sem("lowT_out"), sem("ffn_ready"), sem("x3_ready")

        bF = (6, 7)
        FIRST, LAST = -2 * KT, (B + 2) * KT
        bQ, bA, bB, bM, bO = (0, 1), (2, 3), (4, 5), 6, 7
        block = es.enter_context(nc.Block())

        def steps(eng, step, first, last, before, after):
            for g in before:
                step(g, g % 2)
            with eng.Fori(0, (last - first + 1) // 2) as i:
                step(2 * i + first, 1)
                step(2 * i + first + 1, 0)
            for g in after:
                step(g, g % 2)

        @block.sync
        def _(sp):
            sp.dma_start(posi[:], pos).then_inc(s_pos, 16)
            sp.dma_start(kvw_raw[:], xwkv).then_inc(s_kw, 16)
            for k in range(KT):
                sp.dma_start(ctx_raw[:, k], ctxT[:, k]).then_inc(s_ctx[k], 16)
            for b in range(B):
                sp.dma_start(xs[:, b, :], x[b]).then_inc(s_x, 16)
            sp.dma_start(wd_raw[:], wdkr).then_inc(s_wd, 16)
            sp.dma_start(up[:], wup).then_inc(s_up, 16)
            sp.dma_start(vup[P - LAT:P, :], wvup).then_inc(s_up, 16)
            for g in range(2):
                sp.dma_start(Wraw[:, g], wqr[g]).then_inc(s_w[g], 16)
            sp.dma_start(wo_sb[:], wo).then_inc(s_wo, 16)
            sp.dma_start(wx_raw[:], xwq).then_inc(s_wx, 16)
            for t, d in ((xwo_sb, xwo), (bw_raw, bw), (ag_raw, ag)):
                sp.dma_start(t[:], d).then_inc(s_ffn, 16)
            sp.wait_ge(s_uh, 16)
            sp.wait_ge(s_ul, 16)
            for p, (q, k) in enumerate([(0, 2), (0, 3), (1, 2)]):
                for D, w in ((YD, q), (XD, k)):
                    for T in range(KT):
                        sp.dma_start(D[HT * T:HT * (T + 1), HD * p:HD * (p + 1), :],
                                     stg[:, w, T, :]).then_inc(s_yx, 16)
            sp.wait_ge(s_yx, 16 * 6 * KT)
            sp.wait_ge(s_zero, 4)
            sp.wait_ge(s_kc, 2)

            def contents(g, par):
                for j in range(GH):
                    r = CROW + CR * j
                    sp.dma_start(QC[r:r + CR, par, :, j, :], YD[bass.ds(g * GH + j, 1)].rearrange("h r k -> (h r) k")
                                 ).then_inc(s_y[par], 16)
                sp.dma_start(KC[CROW:MROW, par, :], XD[bass.ds(g * GH, GH)].rearrange("h r k -> (h r) k")
                             ).then_inc(s_y[par], 16)

            def q_again(g, par, t):
                sp.wait_ge(s_qh, 8 * g + 4 * (t + 1))
                sp.dma_start(QS[RD:P, par, t], QC[0:RD, par, t]).then_inc(s_qd[t], 16)

            def maxima(g, par, t):
                sp.wait_ge(s_me, 2 * g + t + 1)
                sp.dma_start(QC[MROW:MROW + 1, par, t], mT[:, t, :]).then_inc(s_md[t], 16)

            def outputs(g, t):
                sp.wait_ge(s_oe, 2 * g + t + 1)
                for b in range(4):
                    sp.dma_start(OD[bass.ds(g, 1), :, :, 4 * t + b, :].rearrange("a r j q -> (a r) j q"),
                                 OS[32 * b:32 * b + GH * VC, t, :]).then_inc(s_od[t], 16)

            def step(g, par):
                cur, nxt = not isinstance(g, int) or g >= 0, not isinstance(g, int) or g + 1 < NG
                if cur:
                    q_again(g, par, 1)
                if nxt:
                    if not isinstance(g, int) or g >= 1:
                        sp.wait_ge(s_b, 8 * g)
                    contents(g + 1, 1 - par)
                if not isinstance(g, int) or g >= 1:
                    outputs(g - 1, 1)
                if not isinstance(g, int) or g + 3 < NG:
                    sp.wait_ge(s_ws, g + 2)
                    sp.dma_start(Wraw[:, 1 - par], wqr[bass.ds(g + 3, 1)].rearrange("a p k n -> (a p) k n")
                                 ).then_inc(s_w[1 - par], 16)
                if cur:
                    maxima(g, par, 1)
                if nxt:
                    q_again(g + 1, 1 - par, 0)
                if cur:
                    outputs(g, 0)
                if nxt:
                    maxima(g + 1, 1 - par, 0)

            def gather(T):
                for t in range(2):
                    sp.wait_ge(s_od[t], 64 * (T + 1) * NG // KT)
                src = OD[T * NG // KT:(T + 1) * NG // KT].rearrange("g r j b q -> g r j (b q)")
                for j in range(GH):
                    rows = slice(j * P // GH, (j + 1) * P // GH)
                    sums = src[:, VC * j + HD:VC * (j + 1), j, :].to_broadcast([NG // KT, HD, TOK])
                    sp.dma_start(U[rows, T, :], src[:, VC * j:VC * j + HD, j, :]).then_inc(s_ud[T], 16)
                    sp.dma_start(SU[rows, T, :], sums).then_inc(s_ud[T], 16)

            steps(sp, step, 1, 24, [-1, 0], [])
            for g in range(25, NG):
                step(g, g % 2)
                if g - 25 < KT - 1:
                    gather(g - 25)
            outputs(NG - 1, 1)
            gather(KT - 1)
            sp.wait_ge(s_q, 4 * NG)
            sp.dma_start(lb_sb[:], lb).then_inc(s_ffn, 16)
            sp.dma_start(bias[:], bb.to_broadcast([P, DM])).then_inc(s_ffn, 16)
            for b in range(B):
                sp.wait_ge(s_x3, b + 1)
                sp.dma_start(out[b], xs[:, b, :]).then_inc(s_out, 16)
            sp.wait_ge(s_out, 16 * B)

        @block.gpsimd
        def _(pool):
            nc.gpsimd.memset(ident[:], 0.0).then_inc(s_pch, 1)
            pool.wait_ge(s_pch, 1)
            nc.gpsimd.affine_select(out=ident[:], in_=ident[:], compare_op=ALU.not_equal, fill=1.0,
                                    base=0, pattern=[[-1, P]], channel_multiplier=1).then_inc(s_id, 1)
            pool.wait_ge(s_id, 1)
            nc.gpsimd.memset(QC[RD:P], 0.0).then_inc(s_zero, 1)
            pool.wait_ge(s_zero, 1)
            nc.gpsimd.memset(KC[96:P], MS).then_inc(s_zero, 1)
            pool.wait_ge(s_zero, 2)
            nc.gpsimd.memset(Vg[:], 0.0).then_inc(s_zero, 1)
            nc.gpsimd.memset(power[:], -0.5)
            nc.gpsimd.memset(xv[:, :, :, XD_], 1.0)
            nc.gpsimd.memset(wscale[:], WS).then_inc(s_zero, 1)
            for i in range(HF):
                nc.gpsimd.memset(invf[:, i:i + 1], 1.0 / THETA ** (2 * i / XD_))
            nc.gpsimd.memset(before[:], 1.0)
            nc.gpsimd.memset(mask[:], 1.0).then_inc(s_con, 1)
            pool.wait_ge(s_con, 1)
            nc.gpsimd.affine_select(out=mask[:], in_=mask[:], compare_op=ALU.is_ge, fill=0.0, base=0,
                                    pattern=[[-XD_, XT_H]], channel_multiplier=1).then_inc(s_con, 1)
            nc.gpsimd.affine_select(out=before[:], in_=before[:], compare_op=ALU.is_gt, fill=0.0, base=0,
                                    pattern=[[1, E], [-1, E]], channel_multiplier=0).then_inc(s_con, 1)
            pool.wait_ge(s_con, 2)
            nc.gpsimd.affine_select(out=mask[:], in_=mask[:], compare_op=ALU.is_ge, fill=0.0, base=XD_ - 1,
                                    pattern=[[XD_, XT_H]], channel_multiplier=-1).then_inc(s_con, 1)
            pool.wait_ge(n_var[0], 1)
            nc.gpsimd.tensor_tensor(rstd[:, 0], rstd[:, 0], power[:].to_broadcast([P, B]), ALU.pow).then_inc(n_sd[0], 1)
            pool.wait_ge(s_kv, B)
            pool.wait_ge(s_kvr, B)
            nc.gpsimd.memset(V[:, :, :, HD], 1.0).then_inc(s_zero, 1)

            def split(g, par):
                if not isinstance(g, int) or g >= 2:
                    pool.wait_ge(s_q, 4 * (g - 1))
                pool.wait_ge(s_w[par], 8 * (g - par) + 16)
                scale = wscale[:].to_broadcast([P, KT, GW])
                nc.gpsimd.tensor_tensor(Wh[:, par], Wraw[:, par], scale, ALU.mult).then_inc(s_pch, 1)
                pool.wait_ge(s_pch, 2 * g + 2)
                nc.gpsimd.tensor_tensor(Wraw[:, par], Wraw[:, par], scale, ALU.mult).then_inc(s_pch, 1)
                pool.wait_ge(s_pch, 2 * g + 3)
                nc.gpsimd.tensor_tensor(Wl[:, par], Wraw[:, par], Wh[:, par], ALU.subtract).then_inc(s_ws, 1)

            def values(g, par):
                if not isinstance(g, int) or g >= 2:
                    pool.wait_ge(s_pv, 2 * (g - 1))
                nc.gpsimd.tensor_copy(
                    Vg[:, par, :, 0:GH * VC],
                    V[:].rearrange("p b h c -> p b (h c)")[:, :, bass.ds(g * (GH * VC), GH * VC)]).then_inc(s_vg, 1)

            pool.wait_ge(s_zero, 5)
            split(0, 0)
            split(1, 1)
            pool.wait_ge(s_ce, 4)
            for i in range(2):
                nc.gpsimd.tensor_copy(KC[0:RD, i, :], KS[0:RD, :]).then_inc(s_kc, 1)
            pool.wait_ge(s_uv, B)
            values(0, 0)

            def step(g, par):
                if not isinstance(g, int) or g + 2 < NG:
                    split(g + 2, par)
                if not isinstance(g, int) or g + 1 < NG:
                    values(g + 1, 1 - par)

            steps(pool, step, 1, 28, [0], [29, 30])

            pool.wait_ge(s_pv, 2 * NG)
            nc.gpsimd.tensor_copy(kr[:].rearrange("p b h r d -> p (b h) r d"),
                                  krc[:].rearrange("p b h d -> p (b h) d")[:, :, None, :].to_broadcast([P, B * NKV, REP, XD_])
                                  ).then_inc(s_kx, 1)

            def inverse(n, b):
                if 0 <= b < B:
                    pool.wait_ge(n_var[n], b + 1)
                    nc.gpsimd.tensor_tensor(rstd[:, n, b:b + 1], rstd[:, n, b:b + 1], power[:], ALU.pow).then_inc(n_sd[n], 1)

            inverse(1, 0)
            pool.wait_ge(s_ffn, 80)
            for u in range(FIRST, LAST):
                b, r = u // KT, u % KT
                if 0 <= u + 2 < NU:
                    v = u + 2
                    pool.wait_ge(s_kq, v + 1)
                    if v >= 2:
                        pool.wait_ge(s_s, 2 * (v - 1))
                    nc.gpsimd.tensor_tensor(KD[:, v % 2], KQ[:, v % 3, 0, None, :].to_broadcast([P, XT_H, S]),
                                            mask[:, :, None].to_broadcast([P, XT_H, S]), ALU.mult).then_inc(s_kd, 1)
                if r == 0 and 0 <= b + 1 < B:
                    v = b + 1
                    pool.wait_ge(s_xqp, v + 1)
                    if v >= 2:
                        pool.wait_ge(s_xt, KT * (v - 1))
                    nc.gpsimd.tensor_tensor(qr[:, v % 2], rt[:, 0], rt[:, 1], ALU.add).then_inc(s_xqr, 1)
                if r == 0 and 0 <= b - 2 < B:
                    v = b - 2
                    pool.wait_ge(n_xn[2], v + 1)
                    nc.gpsimd.tensor_tensor(xs[:, v, :], xs[:, v, :], bias[:], ALU.add).then_inc(s_xb, 1)
                if r == 3:
                    inverse(2, b - 1)
                    inverse(1, b + 3)

        @block.scalar
        def _(act):
            act.wait_ge(s_kw, 16)
            nc.scalar.activation(kvw_h[:], kvw_raw[:], ACT.Copy, scale=WS).then_inc(s_kvh, 1)
            for k in range(KT):
                act.wait_ge(s_ctx[k], 16)
                nc.scalar.activation(CTh[:, k], ctx_raw[:, k], ACT.Copy).then_inc(s_kvh, 1)
            act.wait_ge(s_red, 1)
            nc.scalar.activation(sincos[:].rearrange("p a b f -> p (a b f)"), red[:].rearrange("p a b f -> p (a b f)"),
                                 ACT.Sin).then_inc(s_sc, 1)
            act.wait_ge(s_zero, 4)
            for b in range(B):
                act.wait_ge(s_kv, b + 1)
                kv = PS[:, 4 + b % 2, :].rearrange("p (a h d) -> p a h d", h=NKV, d=XD_)
                nc.scalar.activation(krc[:, b], kv[:, 0], ACT.Copy, scale=1 / WS)
                nc.scalar.activation(xv[:, b, :, 0:XD_], kv[:, 1], ACT.Copy, scale=1 / WS).then_inc(s_kvo, 1)
            for b in range(B):
                act.wait_ge(n_tp[0], b + 1)
                nc.scalar.activation(XTh[:, :, b * S:(b + 1) * S],
                                     PS[:, b % 2, :].rearrange("p (k s) -> p k s", k=KT), ACT.Copy).then_inc(n_th[0], 1)
            act.wait_ge(s_c, 4)
            for t in range(2):
                sl = slice(t * HALF, (t + 1) * HALF)
                nc.scalar.activation(cT[:, sl], PS[:, 2 + t, :], ACT.Copy, scale=1 / WS).then_inc(s_ce, 1)
                nc.scalar.activation(KS[0:RD, sl], PS[0:RD, 4 + t, :], ACT.Copy, scale=1 / WS).then_inc(s_ce, 1)
            for u in range(16):
                act.wait_ge(s_u, u + 1)
                w, T, t = u // 8, u // 2 % 4, u % 2
                nc.scalar.activation(stg[:, 2 * w, T, t * HALF:(t + 1) * HALF], PS[:, (6, 7, 0, 1)[u % 4], :],
                                     ACT.Copy).then_inc(s_uh, 1)
            act.wait_ge(s_zero, 5)
            for b in range(B):
                act.wait_ge(s_u, 17 + b)
                nc.scalar.activation(V[:, b, :, 0:HD], PS[:, (6, 7, 0, 1)[b % 4], :].rearrange("p (h d) -> p h d", d=HD),
                                     ACT.Copy).then_inc(s_uv, 1)

            def q_high(g, par, c):
                t, p = c // 2, c % 2
                act.wait_ge(s_q, 4 * g + c + 1)
                for h in range(2):
                    nc.scalar.activation(QC[0:RD, par, t, 2 * p + h, :],
                                         PS[RD * h:RD * (h + 1), bQ[c % 2], :], ACT.Copy, scale=1 / WS).then_inc(s_qh, 1)

            def exps(g, b):
                act.wait_ge(s_b, 8 * g + b + 1)
                if not isinstance(g, int) or g >= 1:
                    act.wait_ge(s_pv, 2 * g - 1 + b // 4)
                nc.scalar.activation(PR[:, b, :], PS[:, bB[b % 2], :], ACT.Exp, scale=ATT_SCALE).then_inc(s_e, 1)

            def o_out(g, t):
                act.wait_ge(s_pv, 2 * g + t + 1)
                if not isinstance(g, int) or g >= 1:
                    act.wait_ge(s_od[t], 64 * g)
                nc.scalar.activation(OS[:, t, :], PS[:, bO, :], ACT.Copy).then_inc(s_oe, 1)

            def step(g, par):
                cur, nxt = not isinstance(g, int) or g >= 0, not isinstance(g, int) or g + 1 < NG
                if not isinstance(g, int) or g >= 1:
                    o_out(g - 1, 1)
                if nxt:
                    if not isinstance(g, int) or g >= 1:
                        act.wait_ge(s_b, 8 * g)
                    q_high(g + 1, 1 - par, 0)
                if cur:
                    for b in range(4):
                        exps(g, b)
                if nxt:
                    q_high(g + 1, 1 - par, 1)
                if cur:
                    o_out(g, 0)
                    exps(g, 4)
                    exps(g, 5)
                if nxt:
                    q_high(g + 1, 1 - par, 2)
                if cur:
                    exps(g, 6)
                    exps(g, 7)
                if nxt:
                    q_high(g + 1, 1 - par, 3)

            steps(act, step, 1, 30, [-1, 0], [31])
            o_out(NG - 1, 1)

            act.wait_ge(s_wx, 16)
            act.wait_ge(s_ffn, 48)
            act.wait_ge(s_b, 8 * NG)
            for h, w in ((Wxh, wx_raw), (bwh, bw_raw), (agh, ag_raw)):
                nc.scalar.activation(h[:], w[:], ACT.Copy, scale=WS).then_inc(s_xh, 1)

            def norm_high(n, b, bank, used):
                if 0 <= b < B:
                    act.wait_ge(n_tp[n], b + 1)
                    if b >= 2:
                        act.wait_ge(used, b - 1)
                    nc.scalar.activation(Ah[:, n, b % 2], PS[:, bank, :].rearrange("p (k s) -> p k s", k=KT),
                                         ACT.Copy).then_inc(n_th[n], 1)

            def exp_half(n):
                act.wait_ge(s_xm, n + 1)
                if n >= 4:
                    act.wait_ge(s_pt, n - 3)
                for j in range(REP):
                    last = nc.scalar.activation(XP[:, n % 4, j], PS[:, 2 + n % 3, j * S:(j + 1) * S], ACT.Exp,
                                                bias=xm[:, n % 4, j:j + 1])
                last.then_inc(s_ex, 1)

            for u in range(FIRST, LAST):
                b, r = u // KT, u % KT
                if 0 <= u + 2 < NU:
                    v = u + 2
                    act.wait_ge(s_xt, v + 1)
                    if v >= 3:
                        act.wait_ge(s_kd, v - 2)
                        act.wait_ge(s_s, 2 * (v - 2))
                    nc.scalar.activation(KQ[:, v % 3].rearrange("p a s -> p (a s)"), PS[:, 0, 0:2 * S], ACT.Copy).then_inc(s_kq, 1)
                if r == 1 and 0 <= b - 1 < B:
                    v = b - 1
                    act.wait_ge(s_ot, v + 1)
                    if v >= 2:
                        act.wait_ge(s_o2, v - 1)
                    nc.scalar.activation(O2T[:, v % 2], PS[:, bF[0], :].rearrange("p (k s) -> p k s", k=KT), ACT.Copy
                                         ).then_inc(s_oT, 1)
                if r == 2 and 0 <= b - 2 < B:
                    act.wait_ge(s_gx, b - 1)
                    nc.scalar.activation(ex[:], ex[:], ACT.Exp).then_inc(s_gy, 1)
                if r == 3 and 0 <= b - 2 < B:
                    v = b - 2
                    act.wait_ge(s_lt, v + 1)
                    if v >= 2:
                        act.wait_ge(s_f, v - 1)
                    nc.scalar.activation(lowT[:, v % 2], PS[:, bF[0], 0:S], ACT.Copy, scale=WS).then_inc(s_lT, 1)
                if 0 <= u + 1 < NU:
                    exp_half(2 * u + 2)
                    exp_half(2 * u + 3)
                if r == 0:
                    norm_high(2, b - 2, bF[1], s_f)
                if r == 1:
                    if 0 <= b - 2 < B:
                        v = b - 2
                        act.wait_ge(s_lge, v + 1)
                        if v >= 2:
                            act.wait_ge(s_lt, v - 1)
                        nc.scalar.activation(low[:, v % 2, :], PS[:, bF[1], 0:E * R], ACT.Copy, scale=1 / WS).then_inc(s_ge, 1)
                    norm_high(1, b + 2, bF[0], s_xq)

        @block.vector
        def _(dve):
            chain = [0]

            def link(ins):
                chain[0] += 1
                ins.then_inc(s_dch, 1)
                dve.wait_ge(s_dch, chain[0])

            dve.wait_ge(s_pos, 16)
            dve.wait_ge(s_con, 4)
            link(nc.vector.tensor_copy(posf[:], posi[:]))
            link(nc.vector.tensor_tensor(ang[:], posf[:, :, None].to_broadcast([P, B, HF]),
                                         invf[:, None, :].to_broadcast([P, B, HF]), ALU.mult))
            for i, quarter in enumerate((0.0, 0.25)):
                r = red[:, i]
                link(nc.vector.tensor_scalar(turns[:], ang[:], 1 / (2 * math.pi), quarter, ALU.mult, ALU.add))
                link(nc.vector.tensor_scalar(turns[:], turns[:], MAGIC, None, ALU.add))
                link(nc.vector.tensor_scalar(turns[:], turns[:], MAGIC, None, ALU.subtract))
                src = ang[:]
                for part in TWO_PI:
                    link(nc.vector.scalar_tensor_tensor(r, turns[:], -part, src, ALU.mult, ALU.add))
                    src = r
                link(nc.vector.tensor_scalar(r, r, quarter * 2 * math.pi, math.pi, ALU.add, ALU.min))
                last = nc.vector.tensor_scalar(r, r, -math.pi, None, ALU.max)
                if i == 0:
                    link(last)
            last.then_inc(s_red, 1)
            dve.wait_ge(s_kvh, 1)
            nc.vector.scalar_tensor_tensor(kvw_l[:], kvw_raw[:], WS, kvw_h[:], ALU.mult, ALU.subtract).then_inc(s_kvl, 1)
            for k in range(KT):
                dve.wait_ge(s_kvh, k + 2)
                nc.vector.tensor_tensor(CTl[:, k], ctx_raw[:, k], CTh[:, k], ALU.subtract).then_inc(s_kvl, 1)

            dve.wait_ge(s_x, 16 * B)
            for b in range(B):
                last = nc.vector.bn_stats(stats[:, b, :], xs[:, b, :])
            link(last)
            for b in range(B):
                last = nc.vector.bn_aggr(mv[:, 0, b, :], stats[:, b, :])
            link(last)
            nc.vector.tensor_scalar(rstd[:, 0], mv[:, 0, :, 1], EPS, None, ALU.add).then_inc(n_var[0], 1)
            dve.wait_ge(n_sd[0], 1)
            for b in range(B):
                nc.vector.tensor_scalar(xn[:, b, :], xs[:, b, :], mv[:, 0, b, 0:1], rstd[:, 0, b:b + 1],
                                        ALU.subtract, ALU.mult).then_inc(n_xn[0], 1)
            dve.wait_ge(s_sc, 1)
            for co, si, f in ((cosq, sinq, XS / WS), (cosk, sink, 1.0)):
                nc.vector.tensor_scalar(co[:], sincos[:, 1], f, None, ALU.mult)
                nc.vector.tensor_scalar(si[:, :, 0, :], sincos[:, 0], -f, None, ALU.mult)
                last = nc.vector.tensor_scalar(si[:, :, 1, :], sincos[:, 0], f, None, ALU.mult)
            link(last)
            dve.wait_ge(s_wd, 16)
            link(nc.vector.tensor_scalar(wd_raw[:], wd_raw[:], WS, None, ALU.mult))
            link(nc.vector.tensor_copy(wd_h[:], wd_raw[:]))
            nc.vector.tensor_tensor(wd_l[:], wd_raw[:], wd_h[:], ALU.subtract).then_inc(s_wds, 1)
            for b in range(B):
                dve.wait_ge(n_th[0], b + 1)
                sl = slice(b * S, (b + 1) * S)
                nc.vector.tensor_tensor(XTl[:, :, sl], PS[:, b % 2, :].rearrange("p (k s) -> p k s", k=KT),
                                        XTh[:, :, sl], ALU.subtract).then_inc(n_tl[0], 1)

            def rope(q, t, nh, b, co, si):
                q = q.rearrange("p (h a f) -> p h a f", a=2, f=HF)
                t = [t[:, i, :].rearrange("p (h a f) -> p h a f", a=2, f=HF) for i in range(2)]
                nc.vector.tensor_tensor(t[0], q, co[:, b, None, None, :].to_broadcast([P, nh, 2, HF]), ALU.mult)
                nc.vector.tensor_tensor(t[1][:, :, 0, :], q[:, :, 1, :], si[:, b, 0, None, :].to_broadcast([P, nh, HF]), ALU.mult)
                return nc.vector.tensor_tensor(t[1][:, :, 1, :], q[:, :, 0, :], si[:, b, 1, None, :].to_broadcast([P, nh, HF]), ALU.mult)

            for t in range(2):
                sl = slice(t * HALF, (t + 1) * HALF)
                dve.wait_ge(s_ce, 2 * t + 2)
                nc.vector.scalar_tensor_tensor(KS[RD:P, sl], PS[0:RD, 4 + t, :], 1 / WS, KS[0:RD, sl],
                                               ALU.mult, ALU.subtract).then_inc(s_kl, 1)
            for u in range(16):
                dve.wait_ge(s_uh, u + 1)
                w, T, t = u // 8, u // 2 % 4, u % 2
                sl = slice(t * HALF, (t + 1) * HALF)
                nc.vector.tensor_tensor(stg[:, 2 * w + 1, T, sl], PS[:, (6, 7, 0, 1)[u % 4], :],
                                        stg[:, 2 * w, T, sl], ALU.subtract).then_inc(s_ul, 1)
                if u % 2:
                    b = u // 2
                    dve.wait_ge(s_kvo, b + 1)
                    k = krc[:, b].rearrange("p h d -> p (h d)")
                    link(rope(k, krt, NKV, b, cosk, sink))
                    nc.vector.tensor_tensor(k, krt[:, 0], krt[:, 1], ALU.add).then_inc(s_kvr, 1)
                    dve.wait_ge(s_kvr, b + 1)

            def q_low(g, par, c):
                t, p = c // 2, c % 2
                for h in range(2):
                    dve.wait_ge(s_qh, 8 * g + 2 * c + h + 1)
                    j = 2 * p + h
                    nc.vector.scalar_tensor_tensor(QS[0:RD, par, t, j, :], PS[RD * h:RD * (h + 1), bQ[c % 2], :], 1 / WS,
                                                   QC[0:RD, par, t, j, :], ALU.mult, ALU.subtract).then_inc(s_ql, 1)

            def row_max(g, par, b):
                dve.wait_ge(s_a, 8 * g + b + 1)
                nc.vector.tensor_reduce(mneg[:, par, b // 4, :, b % 4],
                                        PS[:, bA[b % 2], :].rearrange("p (j k) -> p j k", j=GH),
                                        AX.X, ALU.max, negate=True).then_inc(s_m, 1)

            def max_out(g, t):
                dve.wait_ge(s_mt, 2 * g + t + 1)
                if not isinstance(g, int) or g >= 1:
                    dve.wait_ge(s_md[t], 16 * g)
                nc.vector.tensor_scalar(mT[:, t, :], PS[0:16, bM, 0:S], 1 / MS, None, ALU.mult).then_inc(s_me, 1)

            def step(g, par):
                cur, nxt = not isinstance(g, int) or g >= 0, not isinstance(g, int) or g + 1 < NG
                if cur:
                    for b in (4, 5, 6):
                        row_max(g, par, b)
                if nxt:
                    q_low(g + 1, 1 - par, 0)
                if cur:
                    row_max(g, par, 7)
                    max_out(g, 1)
                if nxt:
                    q_low(g + 1, 1 - par, 1)
                    row_max(g + 1, 1 - par, 0)
                    row_max(g + 1, 1 - par, 1)
                    q_low(g + 1, 1 - par, 2)
                    row_max(g + 1, 1 - par, 2)
                    row_max(g + 1, 1 - par, 3)
                    max_out(g + 1, 0)
                    q_low(g + 1, 1 - par, 3)

            def normalise(T, t):
                sl = slice(t * HALF, (t + 1) * HALF)
                dve.wait_ge(s_ud[T], 32 * GH)
                link(nc.vector.reciprocal(SU[:, T, sl], SU[:, T, sl]))
                nc.vector.tensor_tensor(U[:, T, sl], U[:, T, sl], SU[:, T, sl], ALU.mult).then_inc(s_un, 1)

            steps(dve, step, 1, 24, [-1, 0], [])
            for g in range(25, NG):
                step(g, g % 2)
                if g >= 26:
                    normalise((g - 26) // 2, g % 2)
            for i, (l, w, h) in enumerate(((Wxl, wx_raw, Wxh), (bwl, bw_raw, bwh), (agl, ag_raw, agh))):
                dve.wait_ge(s_xh, i + 1)
                nc.vector.scalar_tensor_tensor(l[:], w[:], WS, h[:], ALU.mult, ALU.subtract).then_inc(s_xl, 1)
            for t in range(2):
                normalise(KT - 1, t)

            def norm_stats(n, b):
                if 0 <= b < B:
                    link(nc.vector.bn_stats(stats[:, n, :], xs[:, b, :]))
                    link(nc.vector.bn_aggr(mv[:, n, b, :], stats[:, n, :]))
                    nc.vector.tensor_scalar(rstd[:, n, b:b + 1], mv[:, n, b, 1:2], EPS, None, ALU.add).then_inc(n_var[n], 1)

            def norm_rows(n, b):
                if 0 <= b < B:
                    dve.wait_ge(n_sd[n], b + 1)
                    if b >= 2:
                        dve.wait_ge(n_tp[n], b - 1)
                    nc.vector.tensor_scalar(pn[:, n, b % 2], xs[:, b, :], mv[:, n, b, 0:1], rstd[:, n, b:b + 1],
                                            ALU.subtract, ALU.mult).then_inc(n_xn[n], 1)

            def norm_low(n, b, bank):
                if 0 <= b < B:
                    dve.wait_ge(n_th[n], b + 1)
                    nc.vector.tensor_tensor(Al[:, n, b % 2], PS[:, bank, :].rearrange("p (k s) -> p k s", k=KT),
                                            Ah[:, n, b % 2], ALU.subtract).then_inc(n_tl[n], 1)

            def x_max(n):
                dve.wait_ge(s_s, n + 1)
                if n >= 4:
                    dve.wait_ge(s_ex, n - 3)
                nc.vector.tensor_reduce(xm[:, n % 4], PS[:, 2 + n % 3, :].rearrange("p (j k) -> p j k", j=REP),
                                        AX.X, ALU.max, negate=True).then_inc(s_xm, 1)

            def p_turned(n):
                dve.wait_ge(s_pt, n + 1)
                if n >= 2:
                    dve.wait_ge(s_xo, n - 1)
                nc.vector.tensor_copy(XPT[:, n % 2].rearrange("p j q -> p (j q)"), PS[:, 5, :]).then_inc(s_pe, 1)

            def x_outputs(u):
                b, t = u // KT, u % KT
                dve.wait_ge(s_xo, 2 * u + 2)
                if t == 0 and b >= 2:
                    dve.wait_ge(s_ot, b - 1)
                o = PS[:, 1, 0:XT_H * XVC].rearrange("p (h c) -> p h c", c=XVC)
                link(nc.vector.reciprocal(rz[:], o[:, :, XD_]))
                nc.vector.tensor_tensor(O2[:, b % 2, t * P:(t + 1) * P].rearrange("p (h d) -> p h d", d=XD_), o[:, :, 0:XD_],
                                        rz[:, :, None].to_broadcast([P, XT_H, XD_]), ALU.mult).then_inc(s_xon, 1)
                dve.wait_ge(s_xon, u + 1)

            def gate_first(b):
                dve.wait_ge(s_lg, b + 1)
                nc.vector.tensor_scalar(lg[:], PS[:, bF[1], E * R:AG], 1 / WS, None, ALU.mult).then_inc(s_lge, 1)
                dve.wait_ge(s_lge, b + 1)
                link(nc.vector.tensor_reduce(mx[:], lg[:], AX.X, ALU.max))
                nc.vector.tensor_scalar(ex[:], lg[:], mx[:], None, ALU.subtract).then_inc(s_gx, 1)
                one, other = lg[:, :, None].to_broadcast([P, E, E]), lg[:, None, :].to_broadcast([P, E, E])
                nc.vector.tensor_tensor(gt[:], other, one, ALU.is_gt)
                link(nc.vector.tensor_tensor(eq[:], other, one, ALU.is_equal))
                link(nc.vector.tensor_tensor(eq[:], eq[:], before[:], ALU.mult))
                link(nc.vector.tensor_tensor(gt[:], gt[:], eq[:], ALU.add))
                link(nc.vector.tensor_reduce(rank[:], gt[:], AX.X, ALU.add))

            def gate_last(b):
                dve.wait_ge(s_gy, b + 1)
                link(nc.vector.scalar_tensor_tensor(ex[:], rank[:], 1.5, ex[:], ALU.is_lt, ALU.mult))
                link(nc.vector.tensor_reduce(mx[:], ex[:], AX.X, ALU.add))
                link(nc.vector.reciprocal(mx[:], mx[:]))
                link(nc.vector.tensor_scalar(ex[:], ex[:], mx[:], SCALING, ALU.mult, ALU.mult))
                dve.wait_ge(s_ge, b + 1)
                l = low[:, b % 2, :].rearrange("p (e r) -> p e r", r=R)
                nc.vector.tensor_tensor(l, l, ex[:, :, None].to_broadcast([P, E, R]), ALU.mult).then_inc(s_lw, 1)
                dve.wait_ge(s_lw, b + 1)

            for b in range(B):
                dve.wait_ge(s_o1, b + 1)
                nc.vector.tensor_tensor(xs[:, b, :], xs[:, b, :], PS[:, (b + 6) % 8, :], ALU.add).then_inc(s_x1, 1)
                if b == 0:
                    dve.wait_ge(s_x1, 1)
                    norm_stats(1, 0)
            dve.wait_ge(s_x1, B)
            for u in range(FIRST, LAST):
                b, r = u // KT, u % KT
                if 0 <= u - 1 < NU:
                    x_outputs(u - 1)
                if r == 0:
                    if 0 <= b - 3 < B:
                        v = b - 3
                        dve.wait_ge(s_f, v + 1)
                        dve.wait_ge(s_xb, v + 1)
                        nc.vector.scalar_tensor_tensor(xs[:, v, :], PS[:, bF[1], :], 1 / WS, xs[:, v, :],
                                                       ALU.mult, ALU.add).then_inc(s_x3, 1)
                    norm_rows(2, b - 2)
                    norm_rows(1, b + 2)
                    if 0 <= b + 1 < B:
                        v = b + 1
                        dve.wait_ge(s_xq, v + 1)
                        if v >= 1:
                            dve.wait_ge(s_xqr, v)
                        rope(PS[:, bF[0], :], rt, XH, v, cosq, sinq).then_inc(s_xqp, 1)
                for h in range(2):
                    if 0 <= u < NU:
                        p_turned(2 * u + h)
                    if 0 <= u + 1 < NU:
                        x_max(2 * u + 2 + h)
                if r == 0:
                    norm_low(2, b - 2, bF[1])
                if r == 1:
                    if 0 <= b - 2 < B:
                        gate_first(b - 2)
                    norm_low(1, b + 2, bF[0])
                if r == 2:
                    if 0 <= b - 2 < B:
                        gate_last(b - 2)
                    if 0 <= b - 1 < B:
                        v = b - 1
                        dve.wait_ge(s_o2, v + 1)
                        nc.vector.tensor_tensor(xs[:, v, :], xs[:, v, :], PS[:, bF[1], :], ALU.add).then_inc(s_x2, 1)
                        dve.wait_ge(s_x2, v + 1)
                if r == 3:
                    norm_stats(2, b - 1)
                    norm_stats(1, b + 3)
            v = B - 1
            dve.wait_ge(s_f, v + 1)
            dve.wait_ge(s_xb, v + 1)
            nc.vector.scalar_tensor_tensor(xs[:, v, :], PS[:, bF[1], :], 1 / WS, xs[:, v, :],
                                           ALU.mult, ALU.add).then_inc(s_x3, 1)

        @block.tensor
        def _(pe):
            mm = nc.tensor.matmul
            def parts(bank, xh, xl, wh, wl, c0, c1, start=True, stop=True):
                for k in range(KT):
                    for n, (xt, wt) in enumerate([(xh, wh), (xh, wl), (xl, wh)]):
                        last = mm(PS[:, bank, 0:c1 - c0], xt[:, k], wt[:, k, c0:c1],
                                  start=(start and k == 0 and n == 0), stop=(stop and k == KT - 1 and n == 2))
                return last

            pe.wait_ge(s_kvl, 1 + KT)
            for b in range(B):
                if b >= 2:
                    pe.wait_ge(s_kvo, b - 1)
                sl = slice(b * S, (b + 1) * S)
                parts(4 + b % 2, CTh[:, :, sl], CTl[:, :, sl], kvw_h, kvw_l, 0, 2 * KW).then_inc(s_kv, 1)

            pe.wait_ge(s_id, 1)
            for b in range(B):
                pe.wait_ge(n_xn[0], b + 1)
                if b >= 2:
                    pe.wait_ge(n_tl[0], b - 1)
                for k in range(KT):
                    last = nc.tensor.transpose(PS[:, b % 2, k * S:(k + 1) * S], xn[:, b, k * P:(k + 1) * P], ident[:])
                last.then_inc(n_tp[0], 1)
            pe.wait_ge(s_kvo, B)

            pe.wait_ge(s_wds, 1)
            pe.wait_ge(n_tl[0], B)
            for m, (c0, w) in enumerate([(0, 2 * LAT), (2 * LAT, RD)]):
                for t in range(2):
                    sl = slice(t * HALF, (t + 1) * HALF)
                    for k in range(KT):
                        for n, (wt, xt) in enumerate([(wd_h, XTh), (wd_h, XTl), (wd_l, XTh)]):
                            last = mm(PS[0:w, 2 + 2 * m + t, :], wt[:, k, c0:c0 + w], xt[:, k, sl],
                                      start=(k == 0 and n == 0), stop=(k == KT - 1 and n == 2))
                    last.then_inc(s_c, 1)
            pe.wait_ge(s_up, 32)
            pe.wait_ge(s_ce, 4)
            for u in range(24):
                bank = (6, 7, 0, 1)[u % 4]
                if 4 <= u < 20:
                    pe.wait_ge(s_ul, u - 3)
                if u >= 20:
                    pe.wait_ge(s_uv, u - 19)
                if u < 16:
                    w, T, t = u // 8, u // 2 % 4, u % 2
                    r = LAT * w
                    mm(PS[:, bank, :], up[r:r + LAT, T * P:(T + 1) * P], cT[r:r + LAT, t * HALF:(t + 1) * HALF],
                       start=True, stop=True).then_inc(s_u, 1)
                else:
                    b = u - 16
                    mm(PS[:, bank, :], cT[LAT:P, b * S:(b + 1) * S], vup[LAT:P, :],
                       start=True, stop=True).then_inc(s_u, 1)
            pe.wait_ge(s_kl, 2)
            pe.wait_ge(s_ul, 16)
            pe.wait_ge(s_uv, B)

            def project(g, par, c, k):
                t, p = c // 2, c % 2
                sl = slice(t * HALF, (t + 1) * HALF)
                if k == 0:
                    if c == 0:
                        pe.wait_ge(s_ws, g + 1)
                    if not isinstance(g, int) or g >= 1 or c >= 2:
                        pe.wait_ge(s_ql, 8 * g + 2 * (c - 1))
                for n, (wt, xt) in enumerate([(Wh, XTh), (Wh, XTl), (Wl, XTh)]):
                    last = mm(PS[:, bQ[c % 2], :], wt[:, par, k, p * P:(p + 1) * P], xt[:, k, sl],
                              start=(k == 0 and n == 0), stop=(k == KT - 1 and n == 2))
                if k == KT - 1:
                    last.then_inc(s_q, 1)

            def rough_scores(g, par, b):
                if b == 0:
                    pe.wait_ge(s_y[par], (g - par) * 40 + 80)
                if b % 4 == 0:
                    pe.wait_ge(s_qh, 8 * g + b + 4)
                if not isinstance(g, int) or g >= 1 or b >= 2:
                    pe.wait_ge(s_m, 8 * g + b - 1)
                for j in range(GH):
                    last = mm(PS[:, bA[b % 2], j * S:(j + 1) * S], QC[0:MROW, par, b // 4, j, b % 4 * S:(b % 4 + 1) * S],
                              KC[0:MROW, par, b * S:(b + 1) * S], start=True, stop=True)
                last.then_inc(s_a, 1)

            def max_turn(g, par, t):
                pe.wait_ge(s_m, 8 * g + 4 * t + 4)
                if not isinstance(g, int) or g >= 1 or t >= 1:
                    pe.wait_ge(s_me, 2 * g + t)
                nc.tensor.transpose(PS[0:16, bM, 0:S], mneg[:, par, t].rearrange("p j b -> p (j b)"), ident[:]).then_inc(s_mt, 1)

            def scores(g, par, b):
                t = b // 4
                if b % 4 == 0:
                    pe.wait_ge(s_md[t], 16 * (g + 1))
                    pe.wait_ge(s_qd[t], 16 * (g + 1))
                    pe.wait_ge(s_ql, 8 * g + 4 * t + 4)
                if not isinstance(g, int) or g >= 1 or b >= 2:
                    pe.wait_ge(s_e, 8 * g + b - 1)
                mm(PS[:, bB[b % 2], :].rearrange("p (j q) -> p j q", j=GH), KC[0:MROW + 1, par, b * S:(b + 1) * S],
                   QC[0:MROW + 1, par, t, :, b % 4 * S:(b % 4 + 1) * S], start=True, stop=False)
                mm(PS[:, bB[b % 2], :].rearrange("p (j q) -> p j q", j=GH), KS[:, b * S:(b + 1) * S],
                   QS[:, par, t, :, b % 4 * S:(b % 4 + 1) * S], start=False, stop=True).then_inc(s_b, 1)

            def weigh(g, par, t):
                pe.wait_ge(s_e, 8 * g + 4 * t + 4)
                if t == 0:
                    pe.wait_ge(s_vg, g + 1)
                if not isinstance(g, int) or g >= 1 or t >= 1:
                    pe.wait_ge(s_oe, 2 * g + t)
                for b in range(4):
                    last = mm(PS[32 * b:32 * (b + 1), bO, :], Vg[:, par, 4 * t + b, :], PR[:, 4 * t + b, :],
                              start=True, stop=True)
                last.then_inc(s_pv, 1)

            def step(g, par):
                cur, nxt = not isinstance(g, int) or g >= 0, not isinstance(g, int) or g + 1 < NG
                prev = not isinstance(g, int) or g >= 1
                o = 1 - par
                for c in range(4):
                    for k in range(KT):
                        if nxt:
                            project(g + 1, o, c, k)
                        at = (c, k)
                        if cur and at in ((0, 1), (0, 2), (0, 3), (1, 0)):
                            rough_scores(g, par, 4 * c + k + 3)
                        if prev and at == (0, 2):
                            weigh(g - 1, o, 1)
                        if cur and at == (1, 2):
                            max_turn(g, par, 1)
                        if cur and c == 1:
                            scores(g, par, k)
                        if cur and at == (2, 1):
                            weigh(g, par, 0)
                        if nxt and at in ((2, 2), (2, 3), (3, 0), (3, 1)):
                            rough_scores(g + 1, o, 4 * c + k - 10)
                        if cur and at in ((2, 2), (2, 3), (3, 0), (3, 1)):
                            scores(g, par, 4 * c + k - 6)
                        if nxt and at == (3, 3):
                            max_turn(g + 1, o, 0)

            steps(pe, step, 1, 30, [-1, 0], [31])
            weigh(NG - 1, (NG - 1) % 2, 1)

            pe.wait_ge(s_wo, 16)
            pe.wait_ge(s_un, 2 * (KT - 1))
            pe.wait_ge(s_e, 8 * NG)
            pe.wait_ge(s_oe, 2 * NG)
            for b in range(B):
                for T in range(KT - 1):
                    mm(PS[:, (b + 6) % 8, :], U[:, T, b * S:(b + 1) * S], wo_sb[:, T, :], start=(T == 0), stop=False)
            for b in range(B):
                if b % 4 == 0:
                    pe.wait_ge(s_un, 2 * (KT - 1) + b // 4 + 1)
                mm(PS[:, (b + 6) % 8, :], U[:, KT - 1, b * S:(b + 1) * S], wo_sb[:, KT - 1, :],
                   start=False, stop=True).then_inc(s_o1, 1)

            pe.wait_ge(s_x1, B)
            pe.wait_ge(s_kx, 1)
            pe.wait_ge(s_xl, 3)
            pe.wait_ge(s_ffn, 80)
            last_read = {}

            def take(bank, sem, value):
                if bank in last_read:
                    pe.wait_ge(*last_read[bank])
                last_read[bank] = (sem, value)

            def turn(u):
                b, t = u // KT, u % KT
                if u >= 1:
                    pe.wait_ge(s_kq, u)
                if t == 0:
                    pe.wait_ge(s_xqr, b + 1)
                keys = kr[:, b, 2 * t:2 * t + 2].rearrange("p h r d -> p (h r d)")
                nc.tensor.transpose(PS[:, 0, 0:P], keys, ident[:])
                nc.tensor.transpose(PS[:, 0, P:2 * P], qr[:, b % 2, t * P:(t + 1) * P], ident[:]).then_inc(s_xt, 1)

            def x_scores(n):
                u = n // 2
                pe.wait_ge(s_kd, u + 1)
                if n >= 3:
                    pe.wait_ge(s_ex, n - 2)
                mm(PS[:, 2 + n % 3, :], KQ[:, u % 3, 1], KD[:, u % 2, REP * (n % 2):REP * (n % 2 + 1), :],
                   start=True, stop=True).then_inc(s_s, 1)

            def turn_probs(n):
                pe.wait_ge(s_ex, n + 1)
                if n >= 1:
                    pe.wait_ge(s_pe, n)
                for j in range(REP):
                    last = nc.tensor.transpose(PS[:, 5, j * S:(j + 1) * S], XP[:, n % 4, j], ident[:])
                last.then_inc(s_pt, 1)

            def x_weigh(u):
                b, t = u // KT, u % KT
                if u >= 1:
                    pe.wait_ge(s_xon, u)
                for h in range(2):
                    pe.wait_ge(s_pe, 2 * u + h + 1)
                    for j in range(REP):
                        c = (h * REP + j) * XVC
                        last = mm(PS[:, 1, c:c + XVC], XPT[:, h, j], xv[:, b, 2 * t + h, :], start=True, stop=True)
                    last.then_inc(s_xo, 1)

            def norm_turn(n, b, bank):
                if 0 <= b < B:
                    pe.wait_ge(n_xn[n], b + 1)
                    take(bank, n_tl[n], b + 1)
                    for k in range(KT):
                        last = nc.tensor.transpose(PS[:, bank, k * S:(k + 1) * S], pn[:, n, b % 2, k * P:(k + 1) * P], ident[:])
                    last.then_inc(n_tp[n], 1)

            for u in range(FIRST, LAST):
                b, r = u // KT, u % KT
                if 0 <= u + 2 < NU:
                    turn(u + 2)
                if 0 <= u - 1 < NU:
                    x_weigh(u - 1)
                if r == 0 and 0 <= b + 1 < B:
                    v = b + 1
                    pe.wait_ge(n_tl[1], v + 1)
                    take(bF[0], s_xqp, v + 1)
                    parts(bF[0], Ah[:, 1, v % 2], Al[:, 1, v % 2], Wxh, Wxl, 0, DM).then_inc(s_xq, 1)
                if r == 1 and 0 <= b - 1 < B:
                    v = b - 1
                    pe.wait_ge(s_xon, KT * (v + 1))
                    take(bF[0], s_oT, v + 1)
                    for k in range(KT):
                        last = nc.tensor.transpose(PS[:, bF[0], k * S:(k + 1) * S], O2[:, v % 2, k * P:(k + 1) * P], ident[:])
                    last.then_inc(s_ot, 1)
                if r == 2 and 0 <= b - 1 < B:
                    v = b - 1
                    pe.wait_ge(s_oT, v + 1)
                    take(bF[1], s_x2, v + 1)
                    for k in range(KT):
                        last = mm(PS[:, bF[1], :], O2T[:, v % 2, k], xwo_sb[:, k, :], start=(k == 0), stop=(k == KT - 1))
                    last.then_inc(s_o2, 1)
                if r == 3 and 0 <= b - 2 < B:
                    v = b - 2
                    pe.wait_ge(s_lw, v + 1)
                    take(bF[0], s_lT, v + 1)
                    nc.tensor.transpose(PS[:, bF[0], 0:S], low[:, v % 2, :], ident[:]).then_inc(s_lt, 1)
                    take(bF[1], s_x3, v + 1)
                    parts(bF[1], Ah[:, 2, v % 2], Al[:, 2, v % 2], bwh, bwl, 0, DM, stop=False)
                for h in range(2):
                    if 0 <= u < NU:
                        turn_probs(2 * u + h)
                    if 0 <= u + 1 < NU:
                        x_scores(2 * u + 2 + h)
                if r == 0:
                    norm_turn(2, b - 2, bF[1])
                if r == 1:
                    if 0 <= b - 2 < B:
                        v = b - 2
                        pe.wait_ge(n_tl[2], v + 1)
                        take(bF[1], s_ge, v + 1)
                        parts(bF[1], Ah[:, 2, v % 2], Al[:, 2, v % 2], agh, agl, 0, AG).then_inc(s_lg, 1)
                    norm_turn(1, b + 2, bF[0])
                if r == 3 and 0 <= b - 2 < B:
                    v = b - 2
                    pe.wait_ge(s_lT, v + 1)
                    mm(PS[:, bF[1], :], lowT[:, v % 2], lb_sb[:], start=False, stop=True).then_inc(s_f, 1)


def kernel(**inputs):
    import numpy as np
    import concourse.bacc as bacc
    from concourse.bass_utils import run_bass_kernel_spmd

    a = {k: np.asarray(v) for k, v in inputs.items()}
    rows = lambda w: np.ascontiguousarray(w.reshape(KT, P, -1).transpose(1, 0, 2))
    arrays = {
        "x": a["x"],
        "ctxT": rows(a["ctx_4096"].reshape(TOK, DM).T),
        "pos": np.ascontiguousarray(a["itok_BxS2_0_2047"].T),
        "wdkr": rows(np.concatenate([a["L0_attn_Wq_down"], a["L0_attn_Wkv_down"], a["L0_attn_Wk_rope"]], 1)),
        "wup": np.concatenate([a["L0_attn_Wq_up"], a["L0_attn_Wk_up"]], 0),
        "wvup": a["L0_attn_Wv_up"],
        "wqr": np.ascontiguousarray(a["L0_attn_Wq_rope"].reshape(KT, P, NG, GW).transpose(2, 1, 0, 3)),
        "wo": rows(a["L0_attn_Wo"].reshape(KT, NG // KT, GH, HD, DM).transpose(0, 2, 1, 3, 4).reshape(DM, DM)),
        "xwq": rows(a["L0_xattn_Wq"]),
        "xwkv": rows(np.concatenate([a["L0_xattn_Wk"], a["L0_xattn_Wv"]], 1)),
        "xwo": rows(a["L0_xattn_Wo"]),
        "bw": rows(a["L0_ffn_base_w"].T),
        "ag": rows(np.concatenate([a["L0_ffn_lora_A"].reshape(P, DM).T, a["L0_ffn_gate_w"].T], 1)),
        "lb": np.ascontiguousarray(a["L0_ffn_lora_B"].transpose(0, 2, 1).reshape(P, DM)),
        "bb": a["L0_ffn_base_b"].reshape(1, DM),
    }
    nc = bacc.Bacc("TRN2", target_bir_lowering=False, num_devices=1)
    args = [nc.dram_tensor("in_" + k, v.shape, mybir.dt.from_np(v.dtype), kind="ExternalInput").ap() for k, v in arrays.items()]
    out = nc.dram_tensor("y", (B, S, DM), F32, kind="ExternalOutput").ap()
    build(nc, *args, out)
    r = run_bass_kernel_spmd(nc, [{"in_" + k: np.ascontiguousarray(v) for k, v in arrays.items()}], core_ids=[0])
    return r.results[0]["y"]
```

```python
import math
from contextlib import ExitStack

import concourse.bass as bass
from concourse import mybir

F32 = mybir.dt.float32
F16 = mybir.dt.float16
I32 = mybir.dt.int32
ALU = mybir.AluOpType
ACT = mybir.ActivationFunctionType
AX = mybir.AxisListType

P = 128
B, S, DM = 8, 128, 512
TOK = B * S
KT = DM // P
HALF = TOK // 2
EPS = 1e-5
WS = 256.0

H, HD, RD, LAT = 128, 4, 64, 64
GH = 4
NG = H // GH
HT = H // KT
GW = GH * RD
CR = 3 * HD
CROW = RD
MROW = RD + GH * CR
MS = 16.0
ATT_SCALE = float(HD + RD) ** -0.5
VC = HD + 1

XH, NKV, XD_, THETA = 32, 8, 16, 10000.0
REP = XH // NKV
HF = XD_ // 2
XT_H = P // XD_
XS = float(XD_) ** -0.5
XVC = XD_ + 1
KW = NKV * XD_
XROW = P // 2
X3 = 3 * XD_
UQ, UC = XT_H // 2, XT_H // 2 + XT_H // REP
NU = B * KT
TWO_PI = (6.28125, 0.0019340515136718750, 1.2556659146e-06)
MAGIC = 1.5 * 2 ** 23

E, R, SCALING = 8, 16, 2.0
AG = E * R + E


def build(nc, x, ctxT, pos, wdkr, wup, wqr, wo, xwq, xwkv, xwo, bw, ag, lb, bb, out):
    es = ExitStack()
    with es:
        def sem(name):
            return es.enter_context(nc.semaphore(name))

        top = [(nc.sbuf_base + 63) // 64 * 64]
        size = {F32: 4, F16: 2, I32: 4}

        def sb(name, shape, dt=F32):
            n = size[dt]
            for s in shape[1:]:
                n *= s
            at = top[0]
            top[0] = at + (n + 63) // 64 * 64
            return nc.alloc_sbuf_tensor_at(name, shape, dt, offset=at)

        xs = sb("xs", [P, B, DM])
        ident = sb("ident", [P, P])
        stats = sb("stats", [P, B, 6])
        mv = sb("mv", [P, 3, B, 2])
        rstd = sb("rstd", [P, 3, B])
        power = sb("power", [P, 1])
        wscale = sb("wscale", [P, 1, 1])
        wo_sb = sb("wo_sb", [P, KT, DM])
        wx_raw = sb("wx_raw", [P, KT, DM])
        krc = sb("krc", [P, B, NKV, XD_])
        xv = sb("xv", [P, B, NKV, XVC])
        xwo_sb = sb("xwo_sb", [P, KT, DM])
        bw_raw = sb("bw_raw", [P, KT, DM])
        ag_raw = sb("ag_raw", [P, KT, AG])
        posi = sb("posi", [P, B], I32)
        posf = sb("posf", [P, B])
        invf = sb("invf", [P, HF])
        ang = sb("ang", [P, B, HF])
        turns = sb("turns", [P, B, HF])
        red = sb("red", [P, 2, B, HF])
        sincos = sb("sincos", [P, 2, B, HF])
        cosq = sb("cosq", [P, B, HF])
        sinq = sb("sinq", [P, B, 2, HF])
        cosk = sb("cosk", [P, B, HF])
        sink = sb("sink", [P, B, 2, HF])
        before = sb("before", [P, E, E])
        phase = top[0]

        XTh = sb("XTh", [P, KT, TOK], F16)
        XTl = sb("XTl", [P, KT, TOK], F16)
        Wraw = sb("Wraw", [P, 2, KT, GW])
        Wh = sb("Wh", [P, 2, KT, GW], F16)
        Wl = sb("Wl", [P, 2, KT, GW], F16)
        QC = sb("QC", [P, 2, 2, GH, HALF], F16)
        t2_at = top[0]
        QS = sb("QS", [P, 2, 2, GH, HALF], F16)
        KC = sb("KC", [P, 2, TOK], F16)
        KS = sb("KS", [P, TOK], F16)
        pr_at = top[0]
        PR = sb("PR", [P, B, GH * S])
        v_at = top[0]
        V = sb("V", [P, B, H, VC])
        Vg = sb("Vg", [P, 2, B, 32])
        os_at = top[0]
        OS = sb("OS", [P, 2, GH * S])
        mneg = sb("mneg", [P, 2, 2, GH, B // 2])
        mT = sb("mT", [16, 2, S], F16)
        stg = sb("stg", [P, 4, KT, TOK], F16)
        end1 = top[0]
        top[0] = pr_at
        xn = sb("xn", [P, B, DM])
        top[0] = t2_at
        wd_raw = sb("wd_raw", [P, KT, 3 * LAT])
        wd_h = sb("wd_h", [P, KT, 3 * LAT], F16)
        wd_l = sb("wd_l", [P, KT, 3 * LAT], F16)
        up = sb("up", [P, 3, DM])
        up_h = sb("up_h", [P, 3, DM], F16)
        assert top[0] <= t2_at + 2 * 2 * GH * HALF * 2
        top[0] = pr_at
        up_l = sb("up_l", [P, 3, DM], F16)
        krt = sb("krt", [P, 2, KW])
        top[0] = os_at
        CS = sb("CS", [P, 2, TOK], F16)
        assert top[0] <= os_at + 2 * GH * S * 4
        top[0] = end1 - 4 * KT * TOK * 2
        U = sb("U", [P, KT, TOK])
        SU = sb("SU", [P, KT, TOK])
        assert end1 <= nc.sbuf_usable_end
        top[0] = v_at
        kvw_raw = sb("kvw_raw", [P, KT, 2 * KW])
        kvw_h = sb("kvw_h", [P, KT, 2 * KW], F16)
        kvw_l = sb("kvw_l", [P, KT, 2 * KW], F16)
        assert top[0] <= v_at + B * H * VC * 4
        top[0] = end1 - 4 * KT * TOK * 2
        ctx_raw = sb("ctx_raw", [P, KT, TOK])
        CTh = sb("CTh", [P, KT, TOK], F16)
        CTl = sb("CTl", [P, KT, TOK], F16)
        top[0] = phase
        lb_sb = sb("lb_sb", [P, DM])
        bias = sb("bias", [P, DM])
        Wxh = sb("Wxh", [P, KT, DM], F16)
        Wxl = sb("Wxl", [P, KT, DM], F16)
        woh = sb("woh", [P, KT, DM], F16)
        wol = sb("wol", [P, KT, DM], F16)
        bwh = sb("bwh", [P, KT, DM], F16)
        bwl = sb("bwl", [P, KT, DM], F16)
        agh = sb("agh", [P, KT, AG], F16)
        agl = sb("agl", [P, KT, AG], F16)
        id16 = sb("id16", [P, P], F16)
        kst = sb("kst", [P, 2, NKV, 2, XROW], F16)
        qst = sb("qst", [P, 2, XH, XROW], F16)
        pn = sb("pn", [P, 3, 2, DM])
        Ah = sb("Ah", [P, 3, 2, KT, S], F16)
        Al = sb("Al", [P, 3, 2, KT, S], F16)
        rt = sb("rt", [P, 2, DM])
        qr = sb("qr", [P, DM])
        KQ = sb("KQ", [P, 2, UC, S], F16)
        xvz = sb("xvz", [P, B, NKV, 32])
        xm = sb("xm", [P, 4, REP])
        XP = sb("XP", [P, 4, REP, S])
        XPT = sb("XPT", [P, 4, REP, S])
        OW = sb("OW", [P, 2 * S])
        rz = sb("rz", [P, XT_H])
        O2 = sb("O2", [P, 2, DM])
        O2h = sb("O2h", [P, 2, KT, S], F16)
        O2l = sb("O2l", [P, 2, KT, S], F16)
        ex = sb("ex", [P, E])
        mx = sb("mx", [P, 1])
        gt = sb("gt", [P, E, E])
        eq = sb("eq", [P, E, E])
        rank = sb("rank", [P, E])
        low = sb("low", [P, 2, AG])
        lowT = sb("lowT", [P, 2, S])
        assert top[0] <= end1 - 4 * KT * TOK * 2

        PS = es.enter_context(nc.psum_tensor("PS", [P, 8, 512], F32))

        PT16 = PS[:, 0, :].bitcast(F16)

        YD = nc.dram_tensor("q_content_parts", [H, CR, TOK], F16, kind="Internal").ap()
        XD = nc.dram_tensor("k_content_parts", [H, CR, TOK], F16, kind="Internal").ap()
        OD = nc.dram_tensor("head_outputs", [NG, GH * VC, GH, B, S], F32, kind="Internal").ap()

        s_x = [sem(f"x_in{b}") for b in range(B)]
        s_wd, s_up, s_wo = sem("wd_in"), sem("up_in"), sem("wo_in")
        s_zero, s_id = sem("zeroed"), sem("ident_ready")
        s_con = sem("constants")
        s_dch, s_pch = sem("dve_chain"), sem("pool_chain")
        s_wdh, s_wds = sem("wd_high"), sem("wd_split")
        s_c, s_ce, s_cl, s_kc = sem("c_ready"), sem("c_high"), sem("c_low"), sem("k_copied")
        s_u, s_uh, s_ul, s_uv = sem("up_ready"), sem("up_high"), sem("up_low"), sem("v_out")
        s_yx = [sem("content_stored0"), sem("content_stored1")]
        s_w = [sem("w_in0"), sem("w_in1")]
        s_ws = sem("w_split")
        s_vg = sem("vg_ready")
        s_q, s_qh, s_ql = sem("q_ready"), sem("q_high"), sem("q_low")
        s_y = [sem("y_in0"), sem("y_in1")]
        s_a, s_m, s_mt, s_me = sem("a_ready"), sem("max_ready"), sem("mT_ready"), sem("mT_out")
        s_md = [sem("m_in0"), sem("m_in1")]
        s_qd = [sem("qs_in0"), sem("qs_in1")]
        s_b, s_e, s_pv, s_oe = sem("b_ready"), sem("exp_ready"), sem("pv_ready"), sem("o_out")
        s_od = [sem("o_stored0"), sem("o_stored1")]
        s_ud = [sem(f"u_in{T}") for T in range(KT)]
        s_un, s_o1, s_x1 = sem("u_norm"), sem("o1_ready"), sem("x1_ready")
        s_out = sem("stored")
        s_wx, s_ctx, s_pos, s_ffn = sem("xw_in"), [sem(f"ctx_in{k}") for k in range(KT)], sem("pos_in"), sem("ffn_in")
        s_red, s_sc = sem("angles_ready"), sem("sincos_ready")
        s_kw, s_kvh, s_kvl = sem("kvw_in"), sem("ctx_high"), sem("ctx_low")
        s_kv, s_kvo, s_kvr, s_kx = sem("kv_ready"), sem("kv_out"), sem("k_roped"), sem("k_spread")
        s_xh, s_xl = sem("weights_high"), sem("weights_low")
        n_var = [sem(f"var_ready{n}") for n in range(3)]
        n_sd = [sem(f"rstd_ready{n}") for n in range(3)]
        n_xn = [sem(f"normed{n}") for n in range(3)]
        n_tp = [sem(f"normed_turned{n}") for n in range(3)]
        n_th = [sem(f"normed_high{n}") for n in range(3)]
        n_tl = [sem(f"normed_low{n}") for n in range(3)]
        s_xq, s_xqp, s_xqr = sem("xq_ready"), sem("xq_read"), sem("xq_roped")
        s_xvz, s_ow, s_bk = sem("xv_zeros"), sem("xo_copied"), sem("xo_turned")
        s_xqa, s_qst, s_kst = sem("xq_added"), sem("xq_high"), sem("xk_parts")
        s_xt, s_kq = sem("kq_turned"), sem("kq_out")
        s_s, s_xm, s_ex, s_pt = sem("xs_ready"), sem("xmax_ready"), sem("xexp_ready"), sem("pT_ready")
        s_pe = [sem("pT_out0"), sem("pT_out1")]
        s_xo, s_xon = sem("xo_ready"), sem("xo_out")
        s_ot, s_oT, s_oTl, s_o2, s_x2 = sem("oT_ready"), sem("oT_high"), sem("oT_low"), sem("o2_ready"), sem("x2_ready")
        s_xb, s_lg, s_ge = sem("bias_added"), sem("low_ready"), sem("low_out")
        s_gx, s_gy = sem("gate_ready"), sem("gate_exp")
        s_lw, s_lt, s_lT, s_f, s_x3 = sem("low_weighted"), sem("lowT_ready"), sem("lowT_out"), sem("ffn_ready"), sem("x3_ready")

        bF = (6, 7)
        EARLY = 6
        FIRST, LAST = -2 * KT, (B + 3) * KT - 3
        bQ, bA, bB, bM, bO = (0, 1), (2, 3), (4, 5), 6, 7
        def base_bank(v):
            return bF[1] if v < B - 2 else 2 + v % 2

        bT = (0, 1, 6, 7)
        block = es.enter_context(nc.Block())

        def latents(CS, KS):
            return [(CS[:, w], 2 + t, RD * w, t) for w in range(2) for t in range(2)] + \
                [(KS, 4 + t, RD * t, t) for t in range(2)]

        def steps(eng, step, first, last, before, after):
            for g in before:
                step(g, g % 2)
            with eng.Fori(0, (last - first + 1) // 2) as i:
                step(2 * i + first, 1)
                step(2 * i + first + 1, 0)
            for g in after:
                step(g, g % 2)

        @block.sync
        def _(sp):
            for b in range(B):
                sp.dma_start(xs[:, b, :], x[b]).then_inc(s_x[b], 16)
            sp.dma_start(wd_raw[:], wdkr).then_inc(s_wd, 16)
            sp.dma_start(posi[:], pos).then_inc(s_pos, 16)
            sp.dma_start(kvw_raw[:], xwkv).then_inc(s_kw, 16)
            for k in range(KT):
                sp.dma_start(ctx_raw[:, k], ctxT[:, k]).then_inc(s_ctx[k], 16)
            sp.dma_start(up[:], wup).then_inc(s_up, 16)
            for g in range(2):
                sp.dma_start(Wraw[:, g], wqr[g]).then_inc(s_w[g], 16)
            sp.dma_start(wo_sb[:], wo).then_inc(s_wo, 16)
            sp.dma_start(wx_raw[:], xwq).then_inc(s_wx, 16)
            for t, d in ((xwo_sb, xwo), (bw_raw, bw), (ag_raw, ag)):
                sp.dma_start(t[:], d).then_inc(s_ffn, 16)
            def store(T):
                sp.wait_ge(s_uh, 4 * (T + 1))
                sp.wait_ge(s_ul, 4 * (T + 1))
                for p, (q, k) in enumerate([(0, 2), (0, 3), (1, 2)]):
                    for D, w in ((YD, q), (XD, k)):
                        sp.dma_start(D[HT * T:HT * (T + 1), HD * p:HD * (p + 1), :],
                                     stg[:, w, T, :]).then_inc(s_yx[T > 0], 16)

            def contents(g, par):
                for j in range(GH):
                    r = CROW + CR * j
                    sp.dma_start(QC[r:r + CR, par, :, j, :], YD[bass.ds(g * GH + j, 1)].rearrange("h r k -> (h r) k")
                                 ).then_inc(s_y[par], 16)
                sp.dma_start(KC[CROW:MROW, par, :], XD[bass.ds(g * GH, GH)].rearrange("h r k -> (h r) k")
                             ).then_inc(s_y[par], 16)

            def q_again(g, par, t):
                sp.wait_ge(s_qh, 8 * g + 4 * (t + 1))
                sp.dma_start(QS[RD:P, par, t], QC[0:RD, par, t]).then_inc(s_qd[t], 16)

            def maxima(g, par, t):
                sp.wait_ge(s_me, 2 * g + t + 1)
                sp.dma_start(QC[MROW:MROW + 1, par, t], mT[:, t, :]).then_inc(s_md[t], 16)

            def outputs(g, t):
                sp.wait_ge(s_oe, 2 * g + t + 1)
                for b in range(4):
                    sp.dma_start(OD[bass.ds(g, 1), :, :, 4 * t + b, :].rearrange("a r j q -> (a r) j q"),
                                 OS[32 * b:32 * b + GH * VC, t, :]).then_inc(s_od[t], 16)

            def step(g, par):
                cur, nxt = not isinstance(g, int) or g >= 0, not isinstance(g, int) or g + 1 < NG
                if cur:
                    q_again(g, par, 1)
                if nxt:
                    if not isinstance(g, int) or g >= 1:
                        sp.wait_ge(s_b, 8 * g)
                    contents(g + 1, 1 - par)
                if not isinstance(g, int) or g >= 1:
                    outputs(g - 1, 1)
                if not isinstance(g, int) or g + 3 < NG:
                    sp.wait_ge(s_ws, g + 2)
                    sp.dma_start(Wraw[:, 1 - par], wqr[bass.ds(g + 3, 1)].rearrange("a p k n -> (a p) k n")
                                 ).then_inc(s_w[1 - par], 16)
                if cur:
                    maxima(g, par, 1)
                if nxt:
                    q_again(g + 1, 1 - par, 0)
                if cur:
                    outputs(g, 0)
                if nxt:
                    maxima(g + 1, 1 - par, 0)

            def gather(T):
                for t in range(2):
                    sp.wait_ge(s_od[t], 64 * (T + 1) * NG // KT)
                src = OD[T * NG // KT:(T + 1) * NG // KT].rearrange("g r j b q -> g r j (b q)")
                for j in range(GH):
                    rows = slice(j * P // GH, (j + 1) * P // GH)
                    sums = src[:, VC * j + HD:VC * (j + 1), j, :].to_broadcast([NG // KT, HD, TOK])
                    sp.dma_start(U[rows, T, :], src[:, VC * j:VC * j + HD, j, :]).then_inc(s_ud[T], 16)
                    sp.dma_start(SU[rows, T, :], sums).then_inc(s_ud[T], 16)

            store(0)
            store(1)
            sp.wait_ge(s_yx[0], 16 * 6)
            sp.wait_ge(s_zero, 3)
            contents(0, 0)
            sp.wait_ge(s_ws, 1)
            sp.dma_start(Wraw[:, 0], wqr[2]).then_inc(s_w[0], 16)
            store(2)
            store(3)
            sp.wait_ge(s_kc, 2)
            q_again(0, 0, 0)
            maxima(0, 0, 0)
            sp.wait_ge(s_yx[1], 16 * 6 * (KT - 1))
            steps(sp, step, 1, 24, [0], [])
            for g in range(25, NG):
                step(g, g % 2)
                if g - 25 < KT - 1:
                    gather(g - 25)
            outputs(NG - 1, 1)
            gather(KT - 1)
            sp.wait_ge(s_q, 4 * NG)
            sp.dma_start(lb_sb[:], lb).then_inc(s_ffn, 16)
            sp.dma_start(bias[:], bb.to_broadcast([P, DM])).then_inc(s_ffn, 16)
            for b in range(B):
                sp.wait_ge(s_x3, b + 1)
                sp.dma_start(out[b], xs[:, b, :]).then_inc(s_out, 16)
            sp.wait_ge(s_out, 16 * B)

        @block.gpsimd
        def _(pool):
            nc.gpsimd.memset(ident[:], 0.0).then_inc(s_pch, 1)
            pool.wait_ge(s_pch, 1)
            nc.gpsimd.affine_select(out=ident[:], in_=ident[:], compare_op=ALU.not_equal, fill=1.0,
                                    base=0, pattern=[[-1, P]], channel_multiplier=1).then_inc(s_id, 1)
            nc.gpsimd.memset(power[:], -0.5)
            nc.gpsimd.memset(xv[:, :, :, XD_], 1.0)
            nc.gpsimd.memset(wscale[:], WS)
            for i in range(HF):
                nc.gpsimd.memset(invf[:, i:i + 1], 1.0 / THETA ** (2 * i / XD_))
            nc.gpsimd.memset(before[:], 1.0).then_inc(s_con, 1)
            pool.wait_ge(s_con, 1)
            nc.gpsimd.affine_select(out=before[:], in_=before[:], compare_op=ALU.is_gt, fill=0.0, base=0,
                                    pattern=[[1, E], [-1, E]], channel_multiplier=0).then_inc(s_con, 1)
            pool.wait_ge(n_var[0], 1)
            nc.gpsimd.tensor_tensor(rstd[:, 0], rstd[:, 0], power[:].to_broadcast([P, B]), ALU.pow).then_inc(n_sd[0], 1)

            pool.wait_ge(n_sd[0], 1)
            nc.gpsimd.memset(QC[RD:P], 0.0).then_inc(s_zero, 1)
            pool.wait_ge(s_zero, 1)
            nc.gpsimd.memset(KC[96:P], MS).then_inc(s_zero, 1)
            pool.wait_ge(s_zero, 2)
            nc.gpsimd.memset(Vg[:], 0.0).then_inc(s_zero, 1)
            pool.wait_ge(s_zero, 3)

            def split(g, par):
                if not isinstance(g, int) or g >= 2:
                    pool.wait_ge(s_q, 4 * (g - 1))
                pool.wait_ge(s_w[par], 8 * (g - par) + 16)
                scale = wscale[:].to_broadcast([P, KT, GW])
                nc.gpsimd.tensor_tensor(Wh[:, par], Wraw[:, par], scale, ALU.mult).then_inc(s_pch, 1)
                pool.wait_ge(s_pch, 2 * g + 2)
                nc.gpsimd.tensor_tensor(Wraw[:, par], Wraw[:, par], scale, ALU.mult).then_inc(s_pch, 1)
                pool.wait_ge(s_pch, 2 * g + 3)
                nc.gpsimd.tensor_tensor(Wl[:, par], Wraw[:, par], Wh[:, par], ALU.subtract).then_inc(s_ws, 1)

            def values(g, par):
                if not isinstance(g, int) or g >= 2:
                    pool.wait_ge(s_pv, 2 * (g - 1))
                nc.gpsimd.tensor_copy(
                    Vg[:, par, :, 0:GH * VC],
                    V[:].rearrange("p b h c -> p b (h c)")[:, :, bass.ds(g * (GH * VC), GH * VC)]).then_inc(s_vg, 1)

            split(0, 0)
            split(1, 1)
            pool.wait_ge(s_ce, 6)
            for i in range(2):
                nc.gpsimd.tensor_copy(KC[0:RD, i, :], KS[0:RD, :]).then_inc(s_kc, 1)
            pool.wait_ge(s_kv, B)
            nc.gpsimd.memset(V[:, :, :, HD], 1.0).then_inc(s_zero, 1)
            pool.wait_ge(s_uv, B)
            pool.wait_ge(s_zero, 4)
            values(0, 0)

            def step(g, par):
                if not isinstance(g, int) or g + 2 < NG:
                    split(g + 2, par)
                if not isinstance(g, int) or g + 1 < NG:
                    values(g + 1, 1 - par)

            steps(pool, step, 1, 28, [0], [29, 30])

            pool.wait_ge(s_pv, 2 * NG)
            nc.gpsimd.tensor_copy(id16[:], ident[:])
            nc.gpsimd.memset(kst[:], 0.0)
            nc.gpsimd.memset(xvz[:], 0.0).then_inc(s_xvz, 1)
            nc.gpsimd.memset(qst[:], 0.0).then_inc(s_kx, 1)
            pool.wait_ge(s_xvz, 1)
            nc.gpsimd.tensor_copy(xvz[:, :, :, 0:XVC], xv[:]).then_inc(s_xvz, 1)
            pool.wait_ge(s_kx, 1)

            def inverse(n, b):
                if 0 <= b < B:
                    pool.wait_ge(n_var[n], b + 1)
                    nc.gpsimd.tensor_tensor(rstd[:, n, b:b + 1], rstd[:, n, b:b + 1], power[:], ALU.pow).then_inc(n_sd[n], 1)

            pool.wait_ge(s_ffn, 80)
            for u in range(FIRST, LAST):
                b, r = (u + 1) // KT, (u + 1) % KT
                if r == 0 and 0 <= b - 2 < B:
                    v = b - 2
                    pool.wait_ge(n_xn[2], v + 1)
                    nc.gpsimd.tensor_tensor(xs[:, v, :], xs[:, v, :], bias[:], ALU.add).then_inc(s_xb, 1)
                if r == 1 and 0 <= b + 1 < B:
                    v = b + 1
                    pool.wait_ge(s_xqp, v + 1)
                    if v >= 2:
                        pool.wait_ge(s_xt, KT * (v - 1))
                    q, t = (w.rearrange("p (h d) -> p h d", d=XD_) for w in (qr[:], rt[:, 0]))
                    part = [qst[:, v % 2, :, XD_ * i:XD_ * (i + 1)] for i in range(3)]
                    t1 = rt[:, 1].rearrange("p (h d) -> p h d", d=XD_)
                    nc.gpsimd.tensor_tensor(part[0], t, t1, ALU.add).then_inc(s_qst, 1)
                    nc.gpsimd.tensor_tensor(part[1], t, t1, ALU.add)
                    pool.wait_ge(s_qst, v + 1)
                    pool.wait_ge(s_xqa, v + 1)
                    nc.gpsimd.tensor_tensor(part[2], q, part[0], ALU.subtract).then_inc(s_xqr, 1)
                if r == 2:
                    inverse(1, b + 2)
                if r == 2 and 0 <= b + 2 < B:
                    v = b + 2
                    if v >= 2:
                        pool.wait_ge(s_xt, KT * (v - 1))
                    k = krc[:, v, :, None, :].to_broadcast([P, NKV, 2, XD_])
                    part = [kst[:, v % 2, :, :, XD_ * i:XD_ * (i + 1)] for i in range(3)]
                    nc.gpsimd.tensor_copy(part[0], k).then_inc(s_kst, 1)
                    nc.gpsimd.tensor_copy(part[2], k)
                    pool.wait_ge(s_kst, 2 * v + 1)
                    nc.gpsimd.tensor_tensor(part[1], k, part[0], ALU.subtract).then_inc(s_kst, 1)
                if r == 3:
                    inverse(2, b - 1)

        @block.scalar
        def _(act):
            act.wait_ge(s_wd, 16)
            nc.scalar.activation(wd_h[:], wd_raw[:], ACT.Copy, scale=WS).then_inc(s_wdh, 1)
            act.wait_ge(s_kw, 16)
            nc.scalar.activation(kvw_h[:], kvw_raw[:], ACT.Copy, scale=WS).then_inc(s_kvh, 1)
            for b in range(B):
                act.wait_ge(n_tp[0], b + 1)
                nc.scalar.activation(XTh[:, :, b * S:(b + 1) * S],
                                     PS[:, bT[b % 4], :].rearrange("p (k s) -> p k s", k=KT), ACT.Copy).then_inc(n_th[0], 1)
            for k in range(KT):
                act.wait_ge(s_ctx[k], 16)
                nc.scalar.activation(CTh[:, k], ctx_raw[:, k], ACT.Copy).then_inc(s_kvh, 1)
            act.wait_ge(s_up, 16)
            nc.scalar.activation(up_h[:], up[:], ACT.Copy, scale=WS).then_inc(s_wdh, 1)
            for n, (to, bank, r, t) in enumerate(latents(CS, KS)):
                act.wait_ge(s_c, (1, 2, 2, 2, 3, 4)[n])
                nc.scalar.activation(to[0:RD, t * HALF:(t + 1) * HALF], PS[r:r + RD, bank, :], ACT.Copy,
                                     scale=1 / WS).then_inc(s_ce, 1)
            act.wait_ge(s_con, 2)
            for b in range(B):
                if b == B // 2:
                    act.wait_ge(s_red, 1)
                    nc.scalar.activation(sincos[:].rearrange("p a b f -> p (a b f)"), red[:].rearrange("p a b f -> p (a b f)"),
                                         ACT.Sin).then_inc(s_sc, 1)
                act.wait_ge(s_kv, b + 1)
                kv = PS[:, bT[b % 4], :].rearrange("p (a h d) -> p a h d", h=NKV, d=XD_)
                nc.scalar.activation(krc[:, b], kv[:, 0], ACT.Copy, scale=1 / WS)
                nc.scalar.activation(xv[:, b, :, 0:XD_], kv[:, 1], ACT.Copy, scale=1 / WS).then_inc(s_kvo, 1)
            for u in range(16):
                act.wait_ge(s_u, u + 1)
                T, w, t = u // 4, u // 2 % 2, u % 2
                nc.scalar.activation(stg[:, 2 * w, T, t * HALF:(t + 1) * HALF], PS[:, bT[u % 4], :],
                                     ACT.Copy, scale=1 / WS).then_inc(s_uh, 1)
            act.wait_ge(s_zero, 4)
            for b in range(B):
                act.wait_ge(s_u, 17 + b)
                nc.scalar.activation(V[:, b, :, 0:HD], PS[:, bT[b % 4], :].rearrange("p (h d) -> p h d", d=HD),
                                     ACT.Copy, scale=1 / WS).then_inc(s_uv, 1)
            act.wait_ge(s_kvr, B)

            def q_high(g, par, c):
                t, p = c // 2, c % 2
                act.wait_ge(s_q, 4 * g + c + 1)
                for h in range(2):
                    nc.scalar.activation(QC[0:RD, par, t, 2 * p + h, :],
                                         PS[RD * h:RD * (h + 1), bQ[c % 2], :], ACT.Copy, scale=1 / WS).then_inc(s_qh, 1)

            def exps(g, b):
                act.wait_ge(s_b, 8 * g + b + 1)
                if not isinstance(g, int) or g >= 1:
                    act.wait_ge(s_pv, 2 * g - 1 + b // 4)
                nc.scalar.activation(PR[:, b, :], PS[:, bB[b % 2], :], ACT.Exp, scale=ATT_SCALE).then_inc(s_e, 1)

            def o_out(g, t):
                act.wait_ge(s_pv, 2 * g + t + 1)
                if not isinstance(g, int) or g >= 1:
                    act.wait_ge(s_od[t], 64 * g)
                nc.scalar.activation(OS[:, t, :], PS[:, bO, :], ACT.Copy).then_inc(s_oe, 1)

            def step(g, par):
                cur, nxt = not isinstance(g, int) or g >= 0, not isinstance(g, int) or g + 1 < NG
                if not isinstance(g, int) or g >= 1:
                    o_out(g - 1, 1)
                if nxt:
                    if not isinstance(g, int) or g >= 1:
                        act.wait_ge(s_b, 8 * g)
                    q_high(g + 1, 1 - par, 0)
                if cur:
                    for b in range(4):
                        exps(g, b)
                if nxt:
                    q_high(g + 1, 1 - par, 1)
                if cur:
                    o_out(g, 0)
                    exps(g, 4)
                    exps(g, 5)
                if nxt:
                    q_high(g + 1, 1 - par, 2)
                if cur:
                    exps(g, 6)
                    exps(g, 7)
                if nxt:
                    q_high(g + 1, 1 - par, 3)

            steps(act, step, 1, 30, [-1, 0], [31])
            o_out(NG - 1, 1)

            act.wait_ge(s_wx, 16)
            act.wait_ge(s_ffn, 48)
            act.wait_ge(s_b, 8 * NG)
            for h, w in ((Wxh, wx_raw), (woh, xwo_sb), (bwh, bw_raw), (agh, ag_raw)):
                nc.scalar.activation(h[:], w[:], ACT.Copy, scale=WS).then_inc(s_xh, 1)

            def norm_high(n, b, bank, used):
                if 0 <= b < B:
                    act.wait_ge(n_tp[n], b + 1)
                    if b >= 2:
                        act.wait_ge(used, b - 1)
                    nc.scalar.activation(Ah[:, n, b % 2], PS[:, bank, :].rearrange("p (k s) -> p k s", k=KT),
                                         ACT.Copy).then_inc(n_th[n], 1)

            def probs_out(u, h):
                act.wait_ge(s_pt, 2 * u + h + 1)
                if u >= 2:
                    act.wait_ge(s_xo, u - 1)
                nc.scalar.activation(XPT[:, (2 * u + h) % 4].rearrange("p j q -> p (j q)"), PS[:, 4 + h, :],
                                     ACT.Copy).then_inc(s_pe[h], 1)

            def exp_half(n):
                act.wait_ge(s_xm, n + 1)
                if n >= 4:
                    act.wait_ge(s_pt, n - 3)
                for j in range(REP):
                    last = nc.scalar.activation(XP[:, n % 4, j], PS[:, 2 + n % 2, j * S:(j + 1) * S], ACT.Exp,
                                                bias=xm[:, n % 4, j:j + 1])
                last.then_inc(s_ex, 1)

            def turned_out(u):
                if 0 <= u + 2 < NU:
                    v = u + 2
                    act.wait_ge(s_xt, v + 1)
                    if v >= 2:
                        act.wait_ge(s_s, 2 * (v - 1))
                    nc.scalar.activation(KQ[:, v % 2].rearrange("p c s -> p (c s)"), PT16[:, 0:UC * S], ACT.Copy).then_inc(s_kq, 1)

            for u in range(FIRST, LAST):
                b, r = (u + 1) // KT, (u + 1) % KT
                turned_out(u)
                if r == 1 and 0 <= b - 3 < B:
                    v = b - 3
                    act.wait_ge(s_lt, v + 1)
                    if v >= 2:
                        act.wait_ge(s_f, v - 1)
                    nc.scalar.activation(lowT[:, v % 2], PS[:, 0, 3 * S:], ACT.Copy, scale=WS).then_inc(s_lT, 1)
                if r == 3 and 0 <= b - 2 < B:
                    act.wait_ge(s_gx, b - 1)
                    nc.scalar.activation(ex[:], ex[:], ACT.Exp).then_inc(s_gy, 1)
                if r == 1:
                    norm_high(2, b - 2, bF[0], s_f)
                if r == 2 and 0 <= b - 2 < B:
                    v = b - 2
                    act.wait_ge(s_lg, v + 1)
                    if v >= 2:
                        act.wait_ge(s_lt, v - 1)
                    nc.scalar.activation(low[:, v % 2, :], PS[:, bF[1], 0:AG], ACT.Copy, scale=1 / WS).then_inc(s_ge, 1)
                if r == 2 and 0 <= b - 1 < B:
                    v = b - 1
                    act.wait_ge(s_ot, v + 1)
                    if v >= 2:
                        act.wait_ge(s_o2, v - 1)
                    nc.scalar.activation(O2h[:, v % 2], PS[:, bF[0], :].rearrange("p (k s) -> p k s", k=KT), ACT.Copy
                                         ).then_inc(s_oT, 1)
                if r == 3:
                    norm_high(1, b + 2, bF[0], s_xq)
                if 0 <= u < NU and r % 2 == 1:
                    probs_out(u, 0)
                if 0 <= u - 1 < NU:
                    act.wait_ge(s_xo, u)
                    if u >= 2:
                        act.wait_ge(s_bk, u - 1)
                    nc.scalar.activation(OW[:], PS[:, 1, 0:2 * S], ACT.Copy).then_inc(s_ow, 1)
                if 0 <= u + 1 < NU:
                    exp_half(2 * u + 2)
                if 0 <= u < NU:
                    probs_out(u, 1)
                if 0 <= u + 1 < NU:
                    exp_half(2 * u + 3)

        @block.vector
        def _(dve):
            chain = [0]

            def link(ins):
                chain[0] += 1
                ins.then_inc(s_dch, 1)
                dve.wait_ge(s_dch, chain[0])

            for b in range(B):
                dve.wait_ge(s_x[b], 16)
                last = nc.vector.bn_stats(stats[:, b, :], xs[:, b, :])
            link(last)
            for b in range(B):
                last = nc.vector.bn_aggr(mv[:, 0, b, :], stats[:, b, :])
            link(last)
            nc.vector.tensor_scalar(rstd[:, 0], mv[:, 0, :, 1], EPS, None, ALU.add).then_inc(n_var[0], 1)
            dve.wait_ge(n_sd[0], 1)
            for b in range(B):
                nc.vector.tensor_scalar(xn[:, b, :], xs[:, b, :], mv[:, 0, b, 0:1], rstd[:, 0, b:b + 1],
                                        ALU.subtract, ALU.mult).then_inc(n_xn[0], 1)
            dve.wait_ge(s_wdh, 1)
            nc.vector.scalar_tensor_tensor(wd_l[:], wd_raw[:], WS, wd_h[:], ALU.mult, ALU.subtract).then_inc(s_wds, 1)
            for b in range(B):
                dve.wait_ge(n_th[0], b + 1)
                sl = slice(b * S, (b + 1) * S)
                nc.vector.tensor_tensor(XTl[:, :, sl], PS[:, bT[b % 4], :].rearrange("p (k s) -> p k s", k=KT),
                                        XTh[:, :, sl], ALU.subtract).then_inc(n_tl[0], 1)
            dve.wait_ge(s_kvh, 1)
            nc.vector.scalar_tensor_tensor(kvw_l[:], kvw_raw[:], WS, kvw_h[:], ALU.mult, ALU.subtract).then_inc(s_kvl, 1)
            for k in range(KT):
                dve.wait_ge(s_kvh, k + 2)
                nc.vector.tensor_tensor(CTl[:, k], ctx_raw[:, k], CTh[:, k], ALU.subtract).then_inc(s_kvl, 1)

            dve.wait_ge(s_wdh, 2)
            nc.vector.scalar_tensor_tensor(up_l[:], up[:], WS, up_h[:], ALU.mult, ALU.subtract).then_inc(s_wds, 1)
            dve.wait_ge(s_pos, 16)
            dve.wait_ge(s_con, 2)
            link(nc.vector.tensor_copy(posf[:], posi[:]))
            link(nc.vector.tensor_tensor(ang[:], posf[:, :, None].to_broadcast([P, B, HF]),
                                         invf[:, None, :].to_broadcast([P, B, HF]), ALU.mult))
            for i, quarter in enumerate((0.0, 0.25)):
                r = red[:, i]
                link(nc.vector.tensor_scalar(turns[:], ang[:], 1 / (2 * math.pi), quarter, ALU.mult, ALU.add))
                link(nc.vector.tensor_scalar(turns[:], turns[:], MAGIC, None, ALU.add))
                link(nc.vector.tensor_scalar(turns[:], turns[:], MAGIC, None, ALU.subtract))
                src = ang[:]
                for part in TWO_PI:
                    link(nc.vector.scalar_tensor_tensor(r, turns[:], -part, src, ALU.mult, ALU.add))
                    src = r
                link(nc.vector.tensor_scalar(r, r, quarter * 2 * math.pi, math.pi, ALU.add, ALU.min))
                last = nc.vector.tensor_scalar(r, r, -math.pi, None, ALU.max)
                if i == 0:
                    link(last)
            last.then_inc(s_red, 1)
            def rope(q, t, nh, b, co, si):
                q = q.rearrange("p (h a f) -> p h a f", a=2, f=HF)
                t = [t[:, i, :].rearrange("p (h a f) -> p h a f", a=2, f=HF) for i in range(2)]
                nc.vector.tensor_tensor(t[0], q, co[:, b, None, None, :].to_broadcast([P, nh, 2, HF]), ALU.mult)
                nc.vector.tensor_tensor(t[1][:, :, 0, :], q[:, :, 1, :], si[:, b, 0, None, :].to_broadcast([P, nh, HF]), ALU.mult)
                return nc.vector.tensor_tensor(t[1][:, :, 1, :], q[:, :, 0, :], si[:, b, 1, None, :].to_broadcast([P, nh, HF]), ALU.mult)

            for n, (to, bank, r, t) in enumerate(latents(CS, KS)):
                dve.wait_ge(s_ce, n + 1)
                sl = slice(t * HALF, (t + 1) * HALF)
                nc.vector.scalar_tensor_tensor(to[RD:P, sl], PS[r:r + RD, bank, :], 1 / WS, to[0:RD, sl],
                                               ALU.mult, ALU.subtract).then_inc(s_cl, 1)
            dve.wait_ge(s_sc, 1)
            for co, si, f in ((cosq, sinq, XS / WS), (cosk, sink, 1.0)):
                nc.vector.tensor_scalar(co[:], sincos[:, 1], f, None, ALU.mult)
                nc.vector.tensor_scalar(si[:, :, 0, :], sincos[:, 0], -f, None, ALU.mult)
                last = nc.vector.tensor_scalar(si[:, :, 1, :], sincos[:, 0], f, None, ALU.mult)
            link(last)

            for u in range(16):
                dve.wait_ge(s_uh, u + 1)
                T, w, t = u // 4, u // 2 % 2, u % 2
                sl = slice(t * HALF, (t + 1) * HALF)
                nc.vector.scalar_tensor_tensor(stg[:, 2 * w + 1, T, sl], PS[:, bT[u % 4], :], 1 / WS,
                                               stg[:, 2 * w, T, sl], ALU.mult, ALU.subtract).then_inc(s_ul, 1)
            for b in range(B):
                dve.wait_ge(s_kvo, b + 1)
                k = krc[:, b].rearrange("p h d -> p (h d)")
                link(rope(k, krt, NKV, b, cosk, sink))
                nc.vector.tensor_tensor(k, krt[:, 0], krt[:, 1], ALU.add).then_inc(s_kvr, 1)
                dve.wait_ge(s_kvr, b + 1)

            def q_low(g, par, c):
                t, p = c // 2, c % 2
                for h in range(2):
                    dve.wait_ge(s_qh, 8 * g + 2 * c + h + 1)
                    j = 2 * p + h
                    nc.vector.scalar_tensor_tensor(QS[0:RD, par, t, j, :], PS[RD * h:RD * (h + 1), bQ[c % 2], :], 1 / WS,
                                                   QC[0:RD, par, t, j, :], ALU.mult, ALU.subtract).then_inc(s_ql, 1)

            def row_max(g, par, b):
                dve.wait_ge(s_a, 8 * g + b + 1)
                nc.vector.tensor_reduce(mneg[:, par, b // 4, :, b % 4],
                                        PS[:, bA[b % 2], :].rearrange("p (j k) -> p j k", j=GH),
                                        AX.X, ALU.max, negate=True).then_inc(s_m, 1)

            def max_out(g, t):
                dve.wait_ge(s_mt, 2 * g + t + 1)
                if not isinstance(g, int) or g >= 1:
                    dve.wait_ge(s_md[t], 16 * g)
                nc.vector.tensor_scalar(mT[:, t, :], PS[0:16, bM, 0:S], 1 / MS, None, ALU.mult).then_inc(s_me, 1)

            def step(g, par):
                cur, nxt = not isinstance(g, int) or g >= 0, not isinstance(g, int) or g + 1 < NG
                if cur:
                    row_max(g, par, 4)
                    row_max(g, par, 5)
                    piece(g, 0)
                    row_max(g, par, 6)
                if nxt:
                    q_low(g + 1, 1 - par, 0)
                if cur:
                    row_max(g, par, 7)
                    max_out(g, 1)
                    piece(g, 1)
                if nxt:
                    q_low(g + 1, 1 - par, 1)
                    row_max(g + 1, 1 - par, 0)
                    row_max(g + 1, 1 - par, 1)
                piece(g, 2)
                if nxt:
                    q_low(g + 1, 1 - par, 2)
                    row_max(g + 1, 1 - par, 2)
                    row_max(g + 1, 1 - par, 3)
                    max_out(g + 1, 0)
                piece(g, 3)
                if nxt:
                    q_low(g + 1, 1 - par, 3)

            def piece(g, n):
                if isinstance(g, int) and g >= 26:
                    m = 4 * (g - 26) + n
                    normalise(m // B, m % B)

            def normalise(T, b):
                sl = slice(b * S, (b + 1) * S)
                dve.wait_ge(s_ud[T], 32 * GH)
                link(nc.vector.reciprocal(SU[:, T, sl], SU[:, T, sl]))
                nc.vector.tensor_tensor(U[:, T, sl], U[:, T, sl], SU[:, T, sl], ALU.mult).then_inc(s_un, 1)

            steps(dve, step, 1, 24, [-1, 0], [])
            for g in range(25, NG):
                step(g, g % 2)
            for i, (l, w, h) in enumerate(((Wxl, wx_raw, Wxh), (wol, xwo_sb, woh), (bwl, bw_raw, bwh), (agl, ag_raw, agh))):
                dve.wait_ge(s_xh, i + 1)
                nc.vector.scalar_tensor_tensor(l[:], w[:], WS, h[:], ALU.mult, ALU.subtract).then_inc(s_xl, 1)
            normalise(KT - 1, 0)
            normalise(KT - 1, 1)

            def norm_stats(n, b):
                if 0 <= b < B:
                    link(nc.vector.bn_stats(stats[:, n, :], xs[:, b, :]))
                    link(nc.vector.bn_aggr(mv[:, n, b, :], stats[:, n, :]))
                    nc.vector.tensor_scalar(rstd[:, n, b:b + 1], mv[:, n, b, 1:2], EPS, None, ALU.add).then_inc(n_var[n], 1)

            def norm_rows(n, b):
                if 0 <= b < B:
                    dve.wait_ge(n_sd[n], b + 1)
                    if b >= 2:
                        dve.wait_ge(n_tp[n], b - 1)
                    nc.vector.tensor_scalar(pn[:, n, b % 2], xs[:, b, :], mv[:, n, b, 0:1], rstd[:, n, b:b + 1],
                                            ALU.subtract, ALU.mult).then_inc(n_xn[n], 1)

            def norm_low(n, b, bank):
                if 0 <= b < B:
                    dve.wait_ge(n_th[n], b + 1)
                    nc.vector.tensor_tensor(Al[:, n, b % 2], PS[:, bank, :].rearrange("p (k s) -> p k s", k=KT),
                                            Ah[:, n, b % 2], ALU.subtract).then_inc(n_tl[n], 1)

            def x_max(n):
                dve.wait_ge(s_s, n + 1)
                if n >= 4:
                    dve.wait_ge(s_ex, n - 3)
                nc.vector.tensor_reduce(xm[:, n % 4], PS[:, 2 + n % 2, :].rearrange("p (j k) -> p j k", j=REP),
                                        AX.X, ALU.max, negate=True).then_inc(s_xm, 1)

            def p_turned(n):
                dve.wait_ge(s_pt, n + 1)
                if n >= 4:
                    dve.wait_ge(s_xo, n // 2 - 1)
                nc.vector.tensor_copy(XPT[:, n % 4].rearrange("p j q -> p (j q)"), PS[:, 4, :]).then_inc(s_pe[0], 1)

            def x_outputs(u):
                b, t = u // KT, u % KT
                dve.wait_ge(s_bk, u + 1)
                if t == 0 and b >= 2:
                    dve.wait_ge(s_ot, b - 1)
                o = PS[:, 1, 2 * S:4 * S].rearrange("p (i g h c) -> p i g h c", i=2, g=2, h=2)
                link(nc.vector.reciprocal(rz[:].rearrange("p (g i h) -> p i g h", g=2, h=2), o[:, :, :, :, XD_]))
                to = O2[:, b % 2, t * P:(t + 1) * P].rearrange("p (g i h d) -> p g i h d", g=2, i=2, h=2)
                by = rz[:].rearrange("p (g i h) -> p g i h", g=2, i=2)
                for i in range(2):
                    last = nc.vector.tensor_tensor(to[:, :, i], o[:, i, :, :, 0:XD_],
                                                   by[:, :, i, :, None].to_broadcast([P, 2, 2, XD_]), ALU.mult)
                last.then_inc(s_xon, 1)
                dve.wait_ge(s_xon, u + 1)

            def gate_first(b):
                dve.wait_ge(s_ge, b + 1)
                lg = low[:, b % 2, E * R:AG]
                link(nc.vector.tensor_reduce(mx[:], lg, AX.X, ALU.max))
                nc.vector.tensor_scalar(ex[:], lg, mx[:], None, ALU.subtract).then_inc(s_gx, 1)
                one, other = lg[:, :, None].to_broadcast([P, E, E]), lg[:, None, :].to_broadcast([P, E, E])
                nc.vector.tensor_tensor(gt[:], other, one, ALU.is_gt)
                link(nc.vector.tensor_tensor(eq[:], other, one, ALU.is_equal))
                link(nc.vector.tensor_tensor(eq[:], eq[:], before[:], ALU.mult))
                link(nc.vector.tensor_tensor(gt[:], gt[:], eq[:], ALU.add))
                link(nc.vector.tensor_reduce(rank[:], gt[:], AX.X, ALU.add))

            def gate_last(b):
                dve.wait_ge(s_gy, b + 1)
                link(nc.vector.scalar_tensor_tensor(ex[:], rank[:], 1.5, ex[:], ALU.is_lt, ALU.mult))
                link(nc.vector.tensor_reduce(mx[:], ex[:], AX.X, ALU.add))
                link(nc.vector.reciprocal(mx[:], mx[:]))
                link(nc.vector.tensor_scalar(ex[:], ex[:], mx[:], SCALING, ALU.mult, ALU.mult))
                l = low[:, b % 2, 0:E * R].rearrange("p (e r) -> p e r", r=R)
                nc.vector.tensor_tensor(l, l, ex[:, :, None].to_broadcast([P, E, R]), ALU.mult).then_inc(s_lw, 1)
                dve.wait_ge(s_lw, b + 1)

            def x1(v):
                dve.wait_ge(s_o1, v + 1)
                nc.vector.tensor_tensor(xs[:, v, :], xs[:, v, :], PS[:, v % EARLY, :], ALU.add).then_inc(s_x1, 1)

            x1(0)
            dve.wait_ge(s_x1, 1)
            for u in range(FIRST, LAST):
                b, r = (u + 1) // KT, (u + 1) % KT
                if 0 <= u + 1 < NU:
                    x_max(2 * u + 2)
                if r == 1:
                    norm_low(2, b - 2, bF[0])
                    if 0 <= b - 3 < B:
                        v = b - 3
                        dve.wait_ge(s_f, v + 1)
                        dve.wait_ge(s_xb, v + 1)
                        nc.vector.scalar_tensor_tensor(xs[:, v, :], PS[:, base_bank(v), :], 1 / WS, xs[:, v, :],
                                                       ALU.mult, ALU.add).then_inc(s_x3, 1)
                if r == 2 and 0 <= b - 1 < B:
                    v = b - 1
                    dve.wait_ge(s_oT, v + 1)
                    nc.vector.tensor_tensor(O2l[:, v % 2], PS[:, bF[0], :].rearrange("p (k s) -> p k s", k=KT),
                                            O2h[:, v % 2], ALU.subtract).then_inc(s_oTl, 1)
                if r == 3:
                    norm_low(1, b + 2, bF[0])
                if 0 <= u + 1 < NU:
                    x_max(2 * u + 3)
                if r == 3:
                    if 0 <= b - 1 < B:
                        v = b - 1
                        dve.wait_ge(s_o2, v + 1)
                        nc.vector.scalar_tensor_tensor(xs[:, v, :], PS[:, bF[1], :], 1 / WS, xs[:, v, :],
                                                       ALU.mult, ALU.add).then_inc(s_x2, 1)
                        dve.wait_ge(s_x2, v + 1)
                if 0 <= u < NU and r % 2 == 0:
                    p_turned(2 * u)
                if 0 <= u - 1 < NU:
                    x_outputs(u - 1)
                if r == 0:
                    norm_rows(2, b - 2)
                    if 0 <= b + 1 < B:
                        v = b + 1
                        dve.wait_ge(s_xq, v + 1)
                        if v >= 1:
                            dve.wait_ge(s_xqr, v)
                        rope(PS[:, bF[0], :], rt, XH, v, cosq, sinq).then_inc(s_xqp, 1)
                        dve.wait_ge(s_xqp, v + 1)
                        nc.vector.tensor_tensor(qr[:], rt[:, 0], rt[:, 1], ALU.add).then_inc(s_xqa, 1)
                if r == 1:
                    norm_stats(1, b + 2)
                if r == 2:
                    norm_rows(1, b + 2)
                    if 0 <= b - 2 < B:
                        gate_first(b - 2)
                if r == 3:
                    if b - 1 == B - 1:
                        norm_stats(2, b - 1)
                    if 0 <= b - 2 < B:
                        gate_last(b - 2)
                    if b - 1 < B - 1:
                        norm_stats(2, b - 1)
                if u == FIRST:
                    normalise(KT - 1, 2)
                    x1(1)
                    normalise(KT - 1, 3)
                if u == FIRST + 1:
                    normalise(KT - 1, 4)
                    x1(2)
                if u == FIRST + 2:
                    for v in range(3, EARLY):
                        normalise(KT - 1, v + 2)
                        x1(v)
                if u == FIRST + 5:
                    for v in range(EARLY, B):
                        x1(v)
                    dve.wait_ge(s_x1, B)

        @block.tensor
        def _(pe):
            mm = nc.tensor.matmul
            def parts(bank, xh, xl, wh, wl, c0, c1, start=True, stop=True):
                for k in range(KT):
                    for n, (xt, wt) in enumerate([(xh, wh), (xh, wl), (xl, wh)]):
                        last = mm(PS[:, bank, 0:c1 - c0], xt[:, k], wt[:, k, c0:c1],
                                  start=(start and k == 0 and n == 0), stop=(stop and k == KT - 1 and n == 2))
                return last

            pe.wait_ge(s_id, 1)
            for b in range(B):
                pe.wait_ge(n_xn[0], b + 1)
                if b >= 4:
                    pe.wait_ge(n_tl[0], b - 3)
                for k in range(KT):
                    last = nc.tensor.transpose(PS[:, bT[b % 4], k * S:(k + 1) * S], xn[:, b, k * P:(k + 1) * P], ident[:])
                last.then_inc(n_tp[0], 1)

            pe.wait_ge(s_wds, 1)
            pe.wait_ge(n_tl[0], B)
            down = [(wd_h, XTh), (wd_h, XTl), (wd_l, XTh)]
            for t in range(2):
                for k in range(KT):
                    for n, (wt, xt) in enumerate(down):
                        last = mm(PS[:, 2 + t, :], wt[:, k, 0:2 * LAT], xt[:, k, t * HALF:(t + 1) * HALF],
                                  start=(k == 0 and n == 0), stop=(k == KT - 1 and n == 2))
                last.then_inc(s_c, 1)
            for k in range(KT):
                for n, (wt, xt) in enumerate(down):
                    for t in range(2):
                        last = mm(PS[RD * t:RD * (t + 1), 4 + t, :], wt[:, k, 2 * LAT:], xt[:, k, t * HALF:(t + 1) * HALF],
                                  start=(k == 0 and n == 0), stop=(k == KT - 1 and n == 2))
                        if k == KT - 1 and n == 2:
                            last.then_inc(s_c, 1)
            pe.wait_ge(s_kvl, 1 + KT)
            for b in range(B):
                if b >= 4:
                    pe.wait_ge(s_kvo, b - 3)
                sl = slice(b * S, (b + 1) * S)
                parts(bT[b % 4], CTh[:, :, sl], CTl[:, :, sl], kvw_h, kvw_l, 0, 2 * KW).then_inc(s_kv, 1)

            pe.wait_ge(s_wds, 2)
            for u in range(24):
                bank = PS[:, bT[u % 4], :]
                if u < 4:
                    pe.wait_ge(s_kvo, u + 5)
                if 4 <= u < 20:
                    pe.wait_ge(s_ul, u - 3)
                if u >= 20:
                    pe.wait_ge(s_uv, u - 19)
                if u < 16:
                    T, w, t = u // 4, u // 2 % 2, u % 2
                    if u < 4:
                        pe.wait_ge(s_cl, u + 1)
                    for n, wt in enumerate((up_h, up_l)):
                        last = mm(bank, wt[:, w, T * P:(T + 1) * P], CS[:, w, t * HALF:(t + 1) * HALF],
                                  start=(n == 0), stop=(n == 1))
                else:
                    b = u - 16
                    for n, wt in enumerate((up_h, up_l)):
                        last = mm(bank, CS[:, 1, b * S:(b + 1) * S], wt[:, 2, :], start=(n == 0), stop=(n == 1))
                last.then_inc(s_u, 1)
            pe.wait_ge(s_cl, 6)
            pe.wait_ge(s_ul, 16)
            pe.wait_ge(s_uv, B)

            def project(g, par, c, k):
                t, p = c // 2, c % 2
                sl = slice(t * HALF, (t + 1) * HALF)
                if k == 0:
                    if c == 0:
                        pe.wait_ge(s_ws, g + 1)
                    if not isinstance(g, int) or g >= 1 or c >= 2:
                        pe.wait_ge(s_ql, 8 * g + 2 * (c - 1))
                for n, (wt, xt) in enumerate([(Wh, XTh), (Wh, XTl), (Wl, XTh)]):
                    last = mm(PS[:, bQ[c % 2], :], wt[:, par, k, p * P:(p + 1) * P], xt[:, k, sl],
                              start=(k == 0 and n == 0), stop=(k == KT - 1 and n == 2))
                if k == KT - 1:
                    last.then_inc(s_q, 1)

            def rough_scores(g, par, b):
                if b == 0:
                    if isinstance(g, int) and g == 0:
                        pe.wait_ge(s_kc, 2)
                    pe.wait_ge(s_y[par], (g - par) * 40 + 80)
                if b % 4 == 0:
                    pe.wait_ge(s_qh, 8 * g + b + 4)
                if not isinstance(g, int) or g >= 1 or b >= 2:
                    pe.wait_ge(s_m, 8 * g + b - 1)
                for j in range(GH):
                    last = mm(PS[:, bA[b % 2], j * S:(j + 1) * S], QC[0:MROW, par, b // 4, j, b % 4 * S:(b % 4 + 1) * S],
                              KC[0:MROW, par, b * S:(b + 1) * S], start=True, stop=True)
                last.then_inc(s_a, 1)

            def max_turn(g, par, t):
                pe.wait_ge(s_m, 8 * g + 4 * t + 4)
                if not isinstance(g, int) or g >= 1 or t >= 1:
                    pe.wait_ge(s_me, 2 * g + t)
                nc.tensor.transpose(PS[0:16, bM, 0:S], mneg[:, par, t].rearrange("p j b -> p (j b)"), ident[:]).then_inc(s_mt, 1)

            def scores(g, par, b):
                t = b // 4
                if b % 4 == 0:
                    pe.wait_ge(s_md[t], 16 * (g + 1))
                    pe.wait_ge(s_qd[t], 16 * (g + 1))
                    pe.wait_ge(s_ql, 8 * g + 4 * t + 4)
                if not isinstance(g, int) or g >= 1 or b >= 2:
                    pe.wait_ge(s_e, 8 * g + b - 1)
                mm(PS[:, bB[b % 2], :].rearrange("p (j q) -> p j q", j=GH), KC[0:MROW + 1, par, b * S:(b + 1) * S],
                   QC[0:MROW + 1, par, t, :, b % 4 * S:(b % 4 + 1) * S], start=True, stop=False)
                mm(PS[:, bB[b % 2], :].rearrange("p (j q) -> p j q", j=GH), KS[:, b * S:(b + 1) * S],
                   QS[:, par, t, :, b % 4 * S:(b % 4 + 1) * S], start=False, stop=True).then_inc(s_b, 1)

            def weigh(g, par, t):
                pe.wait_ge(s_e, 8 * g + 4 * t + 4)
                if t == 0:
                    pe.wait_ge(s_vg, g + 1)
                if not isinstance(g, int) or g >= 1 or t >= 1:
                    pe.wait_ge(s_oe, 2 * g + t)
                for b in range(4):
                    last = mm(PS[32 * b:32 * (b + 1), bO, :], Vg[:, par, 4 * t + b, :], PR[:, 4 * t + b, :],
                              start=True, stop=True)
                last.then_inc(s_pv, 1)

            def step(g, par):
                cur, nxt = not isinstance(g, int) or g >= 0, not isinstance(g, int) or g + 1 < NG
                prev = not isinstance(g, int) or g >= 1
                o = 1 - par
                for c in range(4):
                    for k in range(KT):
                        if nxt:
                            project(g + 1, o, c, k)
                        at = (c, k)
                        if cur and at in ((0, 1), (0, 2), (0, 3), (1, 0)):
                            rough_scores(g, par, 4 * c + k + 3)
                        if prev and at == (0, 2):
                            weigh(g - 1, o, 1)
                        if cur and at == (1, 2):
                            max_turn(g, par, 1)
                        if cur and c == 1:
                            scores(g, par, k)
                        if cur and at == (2, 1):
                            weigh(g, par, 0)
                        if nxt and at in ((2, 2), (2, 3), (3, 0), (3, 1)):
                            rough_scores(g + 1, o, 4 * c + k - 10)
                        if cur and at in ((2, 2), (2, 3), (3, 0), (3, 1)):
                            scores(g, par, 4 * c + k - 6)
                        if nxt and at == (3, 3):
                            max_turn(g + 1, o, 0)
                        if not nxt and at in spare:
                            v, T = spare[at]
                            if v == 2 and T == 0:
                                pe.wait_ge(s_m, 8 * NG)
                            output(v, T)

            def output(v, T):
                if v == 0 or T == KT - 1:
                    pe.wait_ge(s_un, B * (T + 1) if T < KT - 1 else B * T + v + 1)
                last = mm(PS[:, v % EARLY, :], U[:, T, v * S:(v + 1) * S], wo_sb[:, T, :], start=(T == 0), stop=(T == KT - 1))
                if T == KT - 1:
                    last.then_inc(s_o1, 1)

            pe.wait_ge(s_wo, 16)
            spare = {(0, 1): (0, 0), (0, 3): (1, 0), (1, 0): (0, 1), (1, 1): (1, 1),
                     (1, 3): (2, 0), (2, 0): (3, 0), (2, 1): (2, 1), (3, 1): (3, 1)}
            steps(pe, step, 1, 30, [-1, 0], [31])
            weigh(NG - 1, (NG - 1) % 2, 1)

            pe.wait_ge(s_e, 8 * NG)
            for v in range(EARLY):
                for T in range(KT - 1):
                    if (v, T) not in spare.values():
                        output(v, T)
            for v in range(3):
                output(v, KT - 1)

            pe.wait_ge(s_kx, 1)
            pe.wait_ge(s_xvz, 2)
            pe.wait_ge(s_xl, 4)
            pe.wait_ge(s_ffn, 80)
            def base(v):
                parts(base_bank(v), Ah[:, 2, v % 2], Al[:, 2, v % 2], bwh, bwl, 0, DM, stop=False)

            last_read = {}

            def take(bank, sem, value):
                if bank in last_read:
                    pe.wait_ge(*last_read[bank])
                last_read[bank] = (sem, value)

            def turn(u):
                b, t = u // KT, u % KT
                if u >= 1:
                    pe.wait_ge(s_kq, u)
                if t == 0:
                    pe.wait_ge(s_xqr, b + 1)
                q = qst[:, b % 2].rearrange("p h r -> p (h r)")
                k = kst[:, b % 2].rearrange("p h a r -> p (h a r)")
                for c in range(UC):
                    src = q[:, (t * UQ + c) * P:(t * UQ + c + 1) * P] if c < UQ else \
                        k[:, (t * (UC - UQ) + c - UQ) * P:(t * (UC - UQ) + c - UQ + 1) * P]
                    last = nc.tensor.transpose(PT16[:, c * S:(c + 1) * S], src, id16[:])
                last.then_inc(s_xt, 1)

            def x_scores(n):
                u = n // 2
                pe.wait_ge(s_kq, u + 1)
                if n >= 2:
                    pe.wait_ge(s_ex, n - 1)
                r = XROW * (n % 2)
                for j in range(REP):
                    last = mm(PS[:, 2 + n % 2, j * S:(j + 1) * S], KQ[r:r + X3, u % 2, j], KQ[r:r + X3, u % 2, UQ + 2 * j // REP],
                              start=True, stop=True)
                last.then_inc(s_s, 1)

            def turn_probs(n):
                pe.wait_ge(s_ex, n + 1)
                if n >= 2:
                    pe.wait_ge(s_pe[n % 2], n // 2)
                for j in range(REP):
                    last = nc.tensor.transpose(PS[:, 4 + n % 2, j * S:(j + 1) * S], XP[:, n % 4, j], ident[:])
                last.then_inc(s_pt, 1)

            def x_weigh(u):
                b, t = u // KT, u % KT
                if u >= 1:
                    pe.wait_ge(s_xon, u)
                for h in range(2):
                    pe.wait_ge(s_pe[h], u + 1)
                for g in range(2):
                    for h in range(2):
                        r = 32 * (2 * g + h)
                        last = mm(PS[r:r + 32, 1, 0:2 * S], xvz[:, b, 2 * t + g, :], XPT[:, (2 * u + h) % 4, 2 * g:2 * g + 2],
                                  start=True, stop=True)
                last.then_inc(s_xo, 1)

            def x_back(u):
                pe.wait_ge(s_ow, u + 1)
                for i in range(2):
                    last = nc.tensor.transpose(PS[:, 1, (2 + i) * S:(3 + i) * S], OW[:, i * S:(i + 1) * S], ident[:])
                last.then_inc(s_bk, 1)

            def norm_turn(n, b, bank):
                if 0 <= b < B:
                    pe.wait_ge(n_xn[n], b + 1)
                    take(bank, n_tl[n], b + 1)
                    for k in range(KT):
                        last = nc.tensor.transpose(PS[:, bank, k * S:(k + 1) * S], pn[:, n, b % 2, k * P:(k + 1) * P], ident[:])
                    last.then_inc(n_tp[n], 1)

            for u in range(FIRST, LAST):
                b, r = (u + 1) // KT, (u + 1) % KT
                if u == -2:
                    pe.wait_ge(s_x1, B)
                if 0 <= u - 2 < NU:
                    x_back(u - 2)
                if r == 1 and 0 <= b - 3 < B:
                    v = b - 3
                    pe.wait_ge(s_lw, v + 1)
                    pe.wait_ge(s_kq, min(u + 2, NU))
                    nc.tensor.transpose(PS[:, 0, 3 * S:], low[:, v % 2, 0:E * R], ident[:]).then_inc(s_lt, 1)
                if 0 <= u + 2 < NU:
                    turn(u + 2)
                if r == 0:
                    if 0 <= b + 1 < B:
                        v = b + 1
                        pe.wait_ge(n_tl[1], v + 1)
                        take(bF[0], s_xqp, v + 1)
                        parts(bF[0], Ah[:, 1, v % 2], Al[:, 1, v % 2], Wxh, Wxl, 0, DM).then_inc(s_xq, 1)
                if r == 1:
                    if 0 <= b - 3 < B:
                        v = b - 3
                        if v < B - 2:
                            take(bF[1], s_x3, v + 1)
                            base(v)
                        pe.wait_ge(s_lT, v + 1)
                        mm(PS[:, base_bank(v), :], lowT[:, v % 2], lb_sb[:], start=False, stop=True).then_inc(s_f, 1)
                    norm_turn(2, b - 2, bF[0])
                if r == 2:
                    if 0 <= b - 2 < B:
                        v = b - 2
                        pe.wait_ge(n_tl[2], v + 1)
                        take(bF[1], s_ge, v + 1)
                        parts(bF[1], Ah[:, 2, v % 2], Al[:, 2, v % 2], agh, agl, 0, AG).then_inc(s_lg, 1)
                        if v == B - 1:
                            base(v)
                    if 0 <= b - 1 < B:
                        v = b - 1
                        pe.wait_ge(s_xon, KT * (v + 1))
                        take(bF[0], s_oTl, v + 1)
                        for k in range(KT):
                            last = nc.tensor.transpose(PS[:, bF[0], k * S:(k + 1) * S], O2[:, v % 2, k * P:(k + 1) * P], ident[:])
                        last.then_inc(s_ot, 1)
                if r == 3:
                    if 0 <= b - 1 < B:
                        v = b - 1
                        pe.wait_ge(s_oTl, v + 1)
                        take(bF[1], s_x2, v + 1)
                        parts(bF[1], O2h[:, v % 2], O2l[:, v % 2], woh, wol, 0, DM).then_inc(s_o2, 1)
                    if b - 2 == B - 2:
                        base(B - 2)
                    norm_turn(1, b + 2, bF[0])
                if u == FIRST + 2:
                    for v in range(3, EARLY):
                        output(v, KT - 1)
                if u == FIRST + 3:
                    for v in range(EARLY, B):
                        pe.wait_ge(s_x1, v - EARLY + 1)
                        for T in range(KT):
                            output(v, T)
                for h in range(2):
                    if 0 <= u < NU:
                        turn_probs(2 * u + h)
                    if 0 <= u + 1 < NU:
                        x_scores(2 * u + 2 + h)
                    if h == 0 and 0 <= u - 1 < NU:
                        x_weigh(u - 1)


def kernel(**inputs):
    import numpy as np
    import concourse.bacc as bacc
    from concourse.bass_utils import run_bass_kernel_spmd

    a = {k: np.asarray(v) for k, v in inputs.items()}
    rows = lambda w: np.ascontiguousarray(w.reshape(KT, P, -1).transpose(1, 0, 2))
    arrays = {
        "x": a["x"],
        "ctxT": rows(a["ctx_4096"].reshape(TOK, DM).T),
        "pos": np.ascontiguousarray(a["itok_BxS2_0_2047"].T),
        "wdkr": rows(np.concatenate([a["L0_attn_Wq_down"], a["L0_attn_Wkv_down"], a["L0_attn_Wk_rope"]], 1)),
        "wup": np.ascontiguousarray(np.stack([np.concatenate([a[f"L0_attn_W{w}_up"]] * 2, 0) for w in "qkv"], 1)),
        "wqr": np.ascontiguousarray(a["L0_attn_Wq_rope"].reshape(KT, P, NG, GW).transpose(2, 1, 0, 3)),
        "wo": rows(a["L0_attn_Wo"].reshape(KT, NG // KT, GH, HD, DM).transpose(0, 2, 1, 3, 4).reshape(DM, DM)),
        "xwq": rows(a["L0_xattn_Wq"]),
        "xwkv": rows(np.concatenate([a["L0_xattn_Wk"], a["L0_xattn_Wv"]], 1)),
        "xwo": rows(a["L0_xattn_Wo"]),
        "bw": rows(a["L0_ffn_base_w"].T),
        "ag": rows(np.concatenate([a["L0_ffn_lora_A"].reshape(P, DM).T, a["L0_ffn_gate_w"].T], 1)),
        "lb": np.ascontiguousarray(a["L0_ffn_lora_B"].transpose(0, 2, 1).reshape(P, DM)),
        "bb": a["L0_ffn_base_b"].reshape(1, DM),
    }
    nc = bacc.Bacc("TRN2", target_bir_lowering=False, num_devices=1)
    args = [nc.dram_tensor("in_" + k, v.shape, mybir.dt.from_np(v.dtype), kind="ExternalInput").ap() for k, v in arrays.items()]
    out = nc.dram_tensor("y", (B, S, DM), F32, kind="ExternalOutput").ap()
    build(nc, *args, out)
    r = run_bass_kernel_spmd(nc, [{"in_" + k: np.ascontiguousarray(v) for k, v in arrays.items()}], core_ids=[0])
    return r.results[0]["y"]
```
